# Optimizing a Trainium2 kernel written in Bass

```python
import numpy as np
import jax
import jax.numpy as jnp

def _softmax(x, axis=-1):
    return jax.nn.softmax(x, axis=axis)

def _gelu(x):
    return jax.nn.gelu(x, approximate=True)

def _silu(x):
    return jax.nn.silu(x)

def _sigmoid(x):
    return jax.nn.sigmoid(x)

def _layernorm(x, axis=-1, eps=1e-05):
    m = jnp.mean(x, axis=axis, keepdims=True)
    v = jnp.var(x, axis=axis, keepdims=True)
    return (x - m) / jnp.sqrt(v + eps)

def _scatter_add(tgt, idx, src, axis=0):
    return tgt.at[idx].add(src)

def _segment_sum(src, seg, n):
    return jax.ops.segment_sum(src, seg, n)
kernel_name = 'mk_vit_tower_cls_d1_tok_img1024_r4_669928'

def setup_inputs(seed: int=0):
    np.random.seed(seed)
    _w = jnp.asarray

    def _rec_inputs():
        import jax
        import jax.numpy as jnp
        _rk = jax.random.key(seed)
        x = -0.000392918 + 0.999932 * jax.random.normal(jax.random.fold_in(_rk, 1), (32, 256, 256, 1), jnp.float32)
        cls_tok = 0.02 * jax.random.normal(jax.random.fold_in(_rk, 5), (1, 1, 256), jnp.float32)
        return (x, cls_tok)
    x, cls_tok = _rec_inputs()

    def _L0_tok_setup():
        import jax, jax.numpy as jnp
        import numpy as np
        INV_SQRT2 = 0.7071067811865476
        LEVEL = 3

        def _split(x, axis):
            ax = axis % x.ndim
            sl0 = [slice(None)] * x.ndim
            sl0[ax] = slice(0, None, 2)
            sl1 = [slice(None)] * x.ndim
            sl1[ax] = slice(1, None, 2)
            x0, x1 = (x[tuple(sl0)], x[tuple(sl1)])
            return ((x0 + x1) * INV_SQRT2, (x0 - x1) * INV_SQRT2)

        def _merge(lo, hi, axis):
            ax = axis % lo.ndim
            e = (lo + hi) * INV_SQRT2
            o = (lo - hi) * INV_SQRT2
            s = jnp.stack([e, o], axis=ax + 1)
            shape = list(lo.shape)
            shape[ax] *= 2
            return s.reshape(shape)

        def _dwt2(x):
            lo, hi = _split(x, -1)
            a, h = _split(lo, -2)
            v, d = _split(hi, -2)
            return (a, h, v, d)

        def _idwt2(a, h, v, d):
            lo = _merge(a, h, -2)
            hi = _merge(v, d, -2)
            return _merge(lo, hi, -1)
        key = jax.random.key(seed)
        ks = jax.random.split(key, 8)
        B, H, W = (16, 256, 256)
        x = jax.random.normal(ks[0], (B, H, W, 1), dtype=jnp.float32)
        na = H // 8 * (W // 8)
        n2 = H // 4 * (W // 4)
        n1 = H // 2 * (W // 2)
        scale = 0.02
        Wa = jax.random.normal(ks[1], (na, 1), dtype=jnp.float32) * scale
        ba = jnp.zeros((1,), jnp.float32)
        Wd1 = jax.random.normal(ks[2], (3 * na, 3), dtype=jnp.float32) * scale
        bd1 = jnp.zeros((3,), jnp.float32)
        Wd2 = jax.random.normal(ks[3], (3 * n2, 3), dtype=jnp.float32) * scale
        bd2 = jnp.zeros((3,), jnp.float32)
        Wd3 = jax.random.normal(ks[4], (3 * n1, 3), dtype=jnp.float32) * scale
        bd3 = jnp.zeros((3,), jnp.float32)
        return {'x': x, 'Wa': Wa, 'ba': ba, 'Wd1': Wd1, 'bd1': bd1, 'Wd2': Wd2, 'bd2': bd2, 'Wd3': Wd3, 'bd3': bd3}
    _L0_tok_all = _L0_tok_setup()
    _L0_tok_in = {k: v for k, v in _L0_tok_all.items() if k in ('Wa', 'ba', 'Wd1', 'bd1', 'Wd2', 'bd2', 'Wd3', 'bd3')}
    del _L0_tok_all

    def _L0_attn_setup():
        import jax, jax.numpy as jnp
        import numpy as np
        INF = 1000000000.0
        D = 256
        key = jax.random.key(seed)
        k_enc, k_r = jax.random.split(key)
        encoding = jax.random.normal(k_enc, (8, 512, D), dtype=jnp.float32)
        R = jax.random.normal(k_r, (D, D), dtype=jnp.float32) / D
        return {'encoding': encoding, 'R': R}
    _L0_attn_all = _L0_attn_setup()
    _L0_attn_in = {k: v for k, v in _L0_attn_all.items() if k in ('R',)}
    del _L0_attn_all

    def _L0_ffn_setup():
        import jax, jax.numpy as jnp
        import numpy as np
        EMBED_DIM = 256
        MLP_RATIO = 4
        NUM_EXPERTS = 8
        CAPACITY = 1.0
        LN_EPS = 1e-05

        def _layernorm(y, gamma, beta):
            mu = jnp.mean(y, axis=-1, keepdims=True)
            var = jnp.mean(jnp.square(y - mu), axis=-1, keepdims=True)
            return (y - mu) * jax.lax.rsqrt(var + LN_EPS) * gamma + beta
        key = jax.random.key(seed)
        k0, k1, k2, k3, k4, k5 = jax.random.split(key, 6)
        d = EMBED_DIM
        dd = EMBED_DIM * MLP_RATIO
        n = NUM_EXPERTS
        x = jax.random.normal(k0, (4, 512, d), dtype=jnp.float32)
        gate_w = jax.random.normal(k1, (n, d), dtype=jnp.float32) * 0.02
        ln_gamma = jnp.ones((d,), dtype=jnp.float32)
        ln_beta = jnp.zeros((d,), dtype=jnp.float32)
        fc1s = jax.random.normal(k2, (n, dd, d), dtype=jnp.float32) * (1.0 / np.sqrt(d))
        b1s = jax.random.normal(k3, (n, dd), dtype=jnp.float32) * 0.02
        fc2s = jax.random.normal(k4, (n, d, dd), dtype=jnp.float32) * (1.0 / np.sqrt(dd))
        b2s = jax.random.normal(k5, (n, d), dtype=jnp.float32) * 0.02
        return {'x': x, 'gate_w': gate_w, 'ln_gamma': ln_gamma, 'ln_beta': ln_beta, 'fc1s': fc1s, 'b1s': b1s, 'fc2s': fc2s, 'b2s': b2s}
    _L0_ffn_all = _L0_ffn_setup()
    _L0_ffn_in = {k: v for k, v in _L0_ffn_all.items() if k in ('gate_w', 'ln_gamma', 'ln_beta', 'fc1s', 'b1s', 'fc2s', 'b2s')}
    del _L0_ffn_all
    return {'x': x, 'cls_tok': cls_tok, 'L0_tok_Wa': _L0_tok_in['Wa'], 'L0_tok_ba': _L0_tok_in['ba'], 'L0_tok_Wd1': _L0_tok_in['Wd1'], 'L0_tok_bd1': _L0_tok_in['bd1'], 'L0_tok_Wd2': _L0_tok_in['Wd2'], 'L0_tok_bd2': _L0_tok_in['bd2'], 'L0_tok_Wd3': _L0_tok_in['Wd3'], 'L0_tok_bd3': _L0_tok_in['bd3'], 'L0_attn_R': _L0_attn_in['R'], 'L0_ffn_gate_w': _L0_ffn_in['gate_w'], 'L0_ffn_ln_gamma': _L0_ffn_in['ln_gamma'], 'L0_ffn_ln_beta': _L0_ffn_in['ln_beta'], 'L0_ffn_fc1s': _L0_ffn_in['fc1s'], 'L0_ffn_b1s': _L0_ffn_in['b1s'], 'L0_ffn_fc2s': _L0_ffn_in['fc2s'], 'L0_ffn_b2s': _L0_ffn_in['b2s']}

def reference(x, cls_tok, L0_tok_Wa, L0_tok_ba, L0_tok_Wd1, L0_tok_bd1, L0_tok_Wd2, L0_tok_bd2, L0_tok_Wd3, L0_tok_bd3, L0_attn_R, L0_ffn_gate_w, L0_ffn_ln_gamma, L0_ffn_ln_beta, L0_ffn_fc1s, L0_ffn_b1s, L0_ffn_fc2s, L0_ffn_b2s):
    import jax
    import jax.numpy as jnp

    def _L0_tok_ref(x, Wa, ba, Wd1, bd1, Wd2, bd2, Wd3, bd3):
        import jax, jax.numpy as jnp
        import numpy as np
        INV_SQRT2 = 0.7071067811865476
        LEVEL = 3

        def _split(x, axis):
            ax = axis % x.ndim
            sl0 = [slice(None)] * x.ndim
            sl0[ax] = slice(0, None, 2)
            sl1 = [slice(None)] * x.ndim
            sl1[ax] = slice(1, None, 2)
            x0, x1 = (x[tuple(sl0)], x[tuple(sl1)])
            return ((x0 + x1) * INV_SQRT2, (x0 - x1) * INV_SQRT2)

        def _merge(lo, hi, axis):
            ax = axis % lo.ndim
            e = (lo + hi) * INV_SQRT2
            o = (lo - hi) * INV_SQRT2
            s = jnp.stack([e, o], axis=ax + 1)
            shape = list(lo.shape)
            shape[ax] *= 2
            return s.reshape(shape)

        def _dwt2(x):
            lo, hi = _split(x, -1)
            a, h = _split(lo, -2)
            v, d = _split(hi, -2)
            return (a, h, v, d)

        def _idwt2(a, h, v, d):
            lo = _merge(a, h, -2)
            hi = _merge(v, d, -2)
            return _merge(lo, hi, -1)
        img = x[..., 0]
        B = img.shape[0]
        details = []
        cur = img
        for _ in range(LEVEL):
            cur, h, v, d = _dwt2(cur)
            details.append((h, v, d))
        aw = jax.nn.sigmoid(cur.reshape(B, -1) @ Wa + ba)
        rec = cur * aw[:, :, None]
        det_params = [(Wd1, bd1), (Wd2, bd2), (Wd3, bd3)]
        for (h, v, d), (Wd, bd) in zip(reversed(details), det_params):
            flat = jnp.stack([h, v, d], axis=1).reshape(B, -1)
            w = jax.nn.softmax(flat @ Wd + bd, axis=-1)
            rec = _idwt2(rec, h * w[:, 0, None, None], v * w[:, 1, None, None], d * w[:, 2, None, None])
        return rec

    def _L0_attn_ref(encoding, R):
        import jax, jax.numpy as jnp
        import numpy as np
        INF = 1000000000.0
        D = 256
        b, n, d = encoding.shape
        encR = jnp.einsum('bnd,de->bne', encoding, R)
        scores = jnp.einsum('bnd,bmd->bnm', encR, encoding)
        mask = jnp.where(jnp.tril(jnp.ones((n, n), dtype=bool)), 0.0, -INF).astype(scores.dtype)
        A = jax.nn.softmax(scores + mask, axis=2)
        return jnp.einsum('bnm,bmd->bnd', A, encoding)

    def _L0_ffn_ref(x, gate_w, ln_gamma, ln_beta, fc1s, b1s, fc2s, b2s):
        import jax, jax.numpy as jnp
        import numpy as np
        EMBED_DIM = 256
        MLP_RATIO = 4
        NUM_EXPERTS = 8
        CAPACITY = 1.0
        LN_EPS = 1e-05

        def _layernorm(y, gamma, beta):
            mu = jnp.mean(y, axis=-1, keepdims=True)
            var = jnp.mean(jnp.square(y - mu), axis=-1, keepdims=True)
            return (y - mu) * jax.lax.rsqrt(var + LN_EPS) * gamma + beta
        og_shape = x.shape
        d = og_shape[-1]
        xf = x.reshape(-1, d)
        bs = xf.shape[0]
        n = gate_w.shape[0]
        k = int(bs * CAPACITY) // n
        scores = xf @ gate_w.T
        scores = (jnp.tanh(scores) + 1.0) * 0.5
        vals, idx = jax.lax.top_k(scores.T, k)
        kept_w = vals.T
        flat_idx = idx.T.reshape(-1)
        y = xf[flat_idx].reshape(k, n, d)
        y = _layernorm(y, ln_gamma, ln_beta)
        h = jnp.einsum('knd,nfd->knf', y, fc1s) + b1s
        h = jax.nn.gelu(h, approximate=True)
        o = jnp.einsum('knf,ndf->knd', h, fc2s) + b2s
        o = o * kept_w[:, :, None]
        out = xf.at[flat_idx].add(o.reshape(k * n, d))
        return out.reshape(og_shape)
    h = _L0_tok_ref(x, L0_tok_Wa, L0_tok_ba, L0_tok_Wd1, L0_tok_bd1, L0_tok_Wd2, L0_tok_bd2, L0_tok_Wd3, L0_tok_bd3)
    h = jnp.concatenate([jnp.broadcast_to(cls_tok, (h.shape[0], 1, h.shape[2])), h], axis=1)
    h = h + _L0_attn_ref(_layernorm(h, axis=-1), L0_attn_R)
    h = h + _L0_ffn_ref(_layernorm(h, axis=-1), L0_ffn_gate_w, L0_ffn_ln_gamma, L0_ffn_ln_beta, L0_ffn_fc1s, L0_ffn_b1s, L0_ffn_fc2s, L0_ffn_b2s)
    return h

_drawn_inputs = setup_inputs


def setup_inputs(seed=0):
    import zlib

    import numpy as np

    out = dict(_drawn_inputs(seed))
    spreads = {'L0_tok_bd1': (0.0, 0.1),
     'L0_tok_bd2': (0.0, 0.1),
     'L0_tok_bd3': (0.0, 0.1),
     'L0_ffn_ln_gamma': (1.0, 0.2),
     'L0_ffn_ln_beta': (0.0, 0.1)}
    factors = {'L0_ffn_b1s': 8.0, 'L0_ffn_b2s': 6.067}
    for name, (base, spread) in spreads.items():
        noise = np.random.default_rng([zlib.crc32(name.encode()), seed]).standard_normal(out[name].shape)
        drawn = base * np.exp(spread * noise) if base else spread * noise
        out[name] = jnp.asarray(drawn.astype(out[name].dtype))
    for name, factor in factors.items():
        out[name] = (out[name] * factor).astype(out[name].dtype)
    return out
```

```python
from contextlib import ExitStack

import concourse.bass as bass
from concourse import mybir

ALU = mybir.AluOpType
ACT = mybir.ActivationFunctionType
AX_X = mybir.AxisListType.X
F32 = mybir.dt.float32
BF16 = mybir.dt.bfloat16
I32 = mybir.dt.int32

P = 128
NB = 32
NH = 2
D = 256
NT = 257
NE = 8
NF = 1024
KTOK = NB * NT // NE
NJ = 10
CG = 8
DG = D + NE
LEAF = 4
SLOTS = [P] * 8 + [KTOK - 8 * P]
CHUNKS = [(0, 3), (3, 6), (6, 9)]
EPS = 1e-5
MASKED = -1.0e9
BITS = 26

CONST = {}
_at = 0
for _name, _n in [("ident", P), ("fwd", P), ("inv", P), ("same", P), ("before", P), ("causal", P),
                  ("sign", 3), ("slot", 9), ("batch", 1), ("diag", CG), ("pick", NJ), ("spread", 4 * P),
                  ("owner", 5)]:
    CONST[_name] = (_at, _at + _n)
    _at += _n
NCONST = _at


def build_program(nc, x, cls_tok, Wa, ba, Wd1, bd1, Wd2, bd2, Wd3, bd3, R, gate_w, gate_wT, gamma, beta,
                  fc1T, b1, fc2T, b2, const, out, debug=None):
    ctx = ExitStack()
    with ctx:
        def sb(name, shape, dt=F32):
            return ctx.enter_context(nc.sbuf_tensor(name, shape, dt))

        def sem(name):
            return ctx.enter_context(nc.semaphore(name))

        ypre = nc.dram_tensor("ypre", [NB * NT, D], F32).ap()
        vtab = nc.dram_tensor("vtab", [NB * NT, NE], F32).ap()
        out_rows = out.rearrange("b t d -> (b t) d")

        bank = [ctx.enter_context(nc.psum_tensor(f"bank{i}", [P, 512], F32)) for i in range(8)]
        Zb, Hb, Tb, Rb, Sb, Pb, Ab0, Ab1 = bank
        Ab = [Ab0, Ab1]

        C = sb("C", [P, NCONST])

        def cst(name):
            return C[:, CONST[name][0]:CONST[name][1]]
        ident = cst("ident")
        identb = sb("identb", [P, P], BF16)
        causalb = sb("causalb", [P, P], BF16)
        Rw = sb("Rw", [P, 2, D])
        gwT = sb("gwT", [P, 2, NE])
        gam = sb("gam", [P, 2])
        bet = sb("bet", [P, 2])
        b1s = sb("b1s", [P, NE, 8])
        bandb = sb("bandb", [NB, NJ])
        mhalf = sb("mhalf", [P, 4])
        BIG = sb("BIG", [P, NB * NH * D])
        XS = BIG[:, :].rearrange("p (b h c) -> p b h c", b=NB, h=NH)
        o = [0]

        def part(n):
            o[0] += n
            return BIG[:, o[0] - n:o[0]]
        w1s = [part(2 * NF).rearrange("p (c f) -> p c f", c=2) for _ in range(2)]
        w2s = [part(8 * D).rearrange("p (c d) -> p c d", c=8) for _ in range(2)]
        yg = [part(9 * D).rearrange("p (t d) -> p t d", t=9) for _ in range(2)]
        assert o[0] <= NB * NH * D
        ARENA = sb("ARENA", [P, 10816])
        a = [0]

        def cut(n):
            a[0] += n
            assert a[0] <= 10816, a[0]
            return ARENA[:, a[0] - n:a[0]]
        WP = cut(NH * D * NJ).rearrange("p (h c j) -> p h c j", h=NH, c=D)
        bands = {lv: cut(NH * 3 * (D >> lv) * 3).rearrange("p (h k m) -> p h k m", h=NH, k=3) for lv in (1, 2, 3)}
        bsum = {lv: cut(NH * (D >> lv) * 3).rearrange("p (h m) -> p h m", h=NH) for lv in (1, 2, 3)}
        bandA = cut(NH * 32).rearrange("p (h m) -> p h m", h=NH)
        a[0] = 0
        Xc = [cut(NH * D).rearrange("p (h c) -> p h c", h=NH) for _ in range(2)]
        L1 = cut(NH * 128).rearrange("p (h c) -> p h c", h=NH)
        L2 = cut(NH * 64).rearrange("p (h c) -> p h c", h=NH)
        Zw = [cut(NH * D).rearrange("p (h c) -> p h c", h=NH) for _ in range(2)]
        I2 = cut(NH * 64).rearrange("p (h c) -> p h c", h=NH)
        I1 = cut(NH * 128).rearrange("p (h c) -> p h c", h=NH)
        Q = [cut(NH * D).rearrange("p (h c) -> p h c", h=NH) for _ in range(2)]
        hc = [cut(NH * D).rearrange("p (h c) -> p h c", h=NH) for _ in range(2)]
        Ex = [cut(NH * DG).rearrange("p (h c) -> p h c", h=NH) for _ in range(2)]
        ERT = [cut(2 * D).rearrange("p (c t) -> p c t", c=2) for _ in range(2)]
        Pr = [cut(388) for _ in range(2)]
        PTS = [cut(384) for _ in range(2)]
        U = [cut(NH * DG).rearrange("p (h c) -> p h c", h=NH) for _ in range(2)]
        ET = [sb(f"ET{i}", [P, 2, NT]) for i in range(2)]
        H1 = [sb(f"H1{i}", [P, NH, D]) for i in range(2)]
        Bs = [sb(f"Bs{i}", [P, NH, D]) for i in range(2)]
        Yp = [sb(f"Yp{i}", [P, NH, D]) for i in range(2)]
        bn0 = sb("bn0", [P, NH, 6])
        bn1 = sb("bn1", [P, NH, 6])
        ST = [sb(f"ST{i}", [P, 14]) for i in range(2)]
        A0 = sb("A0", [P, 2])
        N0 = [sb(f"N0{i}", [P, 2]) for i in range(2)]
        A1 = sb("A1", [P, 4])
        R4 = [sb(f"R4{i}", [P, 4]) for i in range(2)]
        N4 = [sb(f"N4{i}", [P, 4]) for i in range(2)]
        O1 = [sb(f"O1{i}", [P, 2]) for i in range(2)]
        nmx = [sb(f"nmx{i}", [P, 2]) for i in range(2)]
        rsm = [sb(f"rsm{i}", [P, 2]) for i in range(2)]
        W8 = sb("W8", [P, NB, 8])
        TUG = sb("TUG", [P, NB, NH, NE])
        TEG = sb("TEG", [P, NB, NH, NE])
        TST = sb("TST", [P, NB, 14])
        LM = sb("LM", [CG * NJ, NB, CG])
        lgr = sb("lgr", [CG * NJ, NB])
        zz = sb("zz", [NB, NJ])
        z2 = sb("z2", [NB, NJ])
        bw = sb("bw", [NB, NJ])
        mx3 = sb("mx3", [NB, 3])
        bwT = sb("bwT", [NJ, NB])
        gwb = sb("gwb", [P, NE, D])
        clsb = sb("clsb", [P, D])
        CX = sb("CX", [P, DG])
        ch = sb("ch", [P, DG])
        cbs = sb("cbs", [P, D])
        cyp = sb("cyp", [P, D])
        junk = sb("junk", [P, D])
        cst8 = sb("cst8", [P, 24])
        cbn = sb("cbn", [P, 6])
        cpw = sb("cpw", [P, 4])
        sg = sb("sg", [P, NE])
        cgl = sb("cgl", [P, NE])
        vcls = sb("vcls", [P, NE])
        GL = sb("GL", [P, NB, NH, NE])
        GM = sb("GM", [P, NB, NH, NE])
        sd0 = sb("sd0", [P, NB, NH])
        dm = sb("dm", [P, NB, NH])
        GV = sb("GV", [P, NH, 2, 4, NB])
        V = sb("V", [P, 2, NT])
        ge = sb("ge", [P, 2, NT])
        eq = sb("eq", [P, 2, NT])
        sc = sb("sc", [P, 2, NT])
        one = sb("one", [P, NT])
        Tv = sb("Tv", [P, 2])
        Tc = sb("Tc", [P, 2])
        bit = sb("bit", [P, 2])
        cnt = sb("cnt", [P, 2])
        mm2 = sb("mm2", [P, 2])
        cgt = sb("cgt", [P, 2])
        need = sb("need", [P, 2])
        tot = sb("tot", [P, 2])
        beg = sb("beg", [P, 2])
        fin = sb("fin", [P, 2])
        begM = sb("begM", [P, 5, 2])
        finM = sb("finM", [P, 5, 2])
        TB = sb("TB", [P, 2, NT + 3], BF16)
        iot = sb("iot", [P, KTOK])
        ohu = sb("ohu", [P, KTOK], BF16)
        oh = sb("oh", [P, KTOK], BF16)
        SM = sb("SM", [P, 9, 3])
        rk = sb("rk", [P, 9])
        pos = sb("pos", [P, 9])
        jk = sb("jk", [P, NT], BF16)
        rowf = sb("rowf", [P, 9])
        idx = [sb(f"idx{i}", [P, 9], I32) for i in range(2)]
        kv = [sb(f"kv{i}", [P, 9, NE]) for i in range(2)]
        yT = sb("yT", [P, 2, 384])
        hT = [ARENA[:, i * 3072:(i + 1) * 3072].rearrange("p (f t) -> p f t", f=8) for i in range(2)]
        ob = [ARENA[:, 6144 + i * D:6144 + (i + 1) * D] for i in range(3)]
        b2b = [sb(f"b2b{i}", [P, D]) for i in range(2)]
        ot = [sb(f"ot{i}", [P, D]) for i in range(2)]

        names = """ld_const ld_x0 ld_x1 ld_par ld_band ld_band2 ld_band3 cvt wp wp_part lg_mm lg_m lg_r z_mm z_c z_e bw_t bw_c w8_mm w8
            cls_d cls_p cls_a cls_t et0 cls_st cls_g zero
            xc xc_l z_done zw inv q h0 st0_b st0 pw0_c pw0 hcE et et_ev er er_ev eg eg_ev sm nmax pexp pt pt_ev av u h1 rv
            st1_b st1 pw1_c pw1 base yp tab base_st0 base_st1 yp_st0 yp_st1
            gt_c gt_t gt_v vt_st vsp_t vsp thr tc cn tk_c tk_mm
            ohd smm smc ixc ixd wld0 wld1 gat0 gat1 kvg0 kvg1 wfree yt_t yt hmm hact om oadd omul scat0 scat1 scat2 idxfree gfree""".split()
        s = {n: sem(n) for n in names}

        def after(eng, name, count):
            if not isinstance(count, int) or count > 0:
                eng.wait_ge(s[name], count)

        def apart(eng):
            eng.nop(nofuse=True)

        class Img:
            def __init__(self, i, k):
                self.n, self.h, self.p = i * 2 + k, i + k // 2, k % 2

        STEPS = range(NB + 2)
        HEAD, TAIL = 4, 30

        def steps(eng, emit):
            for k in range(HEAD):
                emit(0, k, lambda m: 0 <= m < NB, k)
            with eng.Fori(HEAD // 2, TAIL // 2) as i:
                for k in range(2):
                    emit(i, k, lambda m: True, 8)
            for k in range(TAIL, NB + 2):
                emit(0, k, lambda m: 0 <= m < NB, k)

        block = ctx.enter_context(nc.Block())

        @block.sync
        def _(sp):
            sp.dma_start(C[:, :], const).then_inc(s["ld_const"], 16)
            sp.dma_start(BIG[:, 0:16 * 512], x[:, 0:16 * 512]).then_inc(s["ld_x0"], 16)
            sp.dma_start(BIG[:, 16 * 512:], x[:, 16 * 512:]).then_inc(s["ld_x1"], 16)
            sp.dma_start(Rw[:, :, :], R.rearrange("(c p) e -> p c e", p=P)).then_inc(s["ld_par"], 16)
            sp.dma_start(gwT[:, :, :], gate_wT).then_inc(s["ld_par"], 16)
            sp.dma_start(gam[:, :], gamma).then_inc(s["ld_par"], 16)
            sp.dma_start(bet[:, :], beta).then_inc(s["ld_par"], 16)
            sp.dma_start(b1s[:, :, :], b1).then_inc(s["ld_par"], 16)
            after(sp, "cls_g", 1)
            cls_out = out.rearrange("b t d -> b (t d)")[:, 0:D]
            cls_yp = ypre.rearrange("(b t) d -> b (t d)", b=NB)[:, 0:D]
            cls_v = vtab.rearrange("(b t) d -> b (t d)", b=NB)[:, 0:NE]
            sp.dma_start(cls_out, cbs[0:NB, :]).then_inc(s["cls_st"], 16)
            sp.dma_start(cls_yp, cyp[0:NB, :]).then_inc(s["cls_st"], 16)
            sp.dma_start(cls_v, vcls[0:NB, :]).then_inc(s["cls_st"], 16)

            out_img = out.rearrange("b t d -> b (t d)")
            yp_img = ypre.rearrange("(b t) d -> b (t d)", b=NB)

            def emit(i, k, have, _):
                m = Img(i, k - 2)
                if have(k - 2):
                    dst = out_img[bass.ds(m.n, 1), D:].rearrange("b (h p d) -> p (b h) d", h=NH, p=P)
                    sp.wait_ge(s["base"], m.n + 1)
                    sp.dma_start(dst, Bs[m.p][:, :, :]).then_inc(s[f"base_st{m.p}"], 16)
                    dst = yp_img[bass.ds(m.n, 1), D:].rearrange("b (h p d) -> p (b h) d", h=NH, p=P)
                    sp.wait_ge(s["yp"], m.n + 1)
                    sp.dma_start(dst, Yp[m.p][:, :, :]).then_inc(s[f"yp_st{m.p}"], 16)
            steps(sp, emit)
            vt = vtab.rearrange("(b t) e -> b (t e)", b=NB)[:, NE:].rearrange("b (h p e) -> p b h e", h=NH, p=P)
            sp.wait_ge(s["gt_v"], 2)
            for h in range(NH):
                sp.dma_start(vt[:, :, h, :], GL[:, :, h, :]).then_inc(s["vt_st"], 16)

            def weights(el, eh, used):
                after(sp, "wfree", used)
                e = el + 4 * eh
                sp.dma_start(w1s[eh][:, :, :], fc1T[bass.ds(e, 1), :, :].rearrange("e p (c f) -> p (e c) f", c=2))\
                    .then_inc(s[f"wld{eh}"], 16)
                sp.dma_start(w2s[eh][:, :, :], fc2T[bass.ds(e, 1), :, :].rearrange("e p (c d) -> p (e c) d", c=8))\
                    .then_inc(s[f"wld{eh}"], 16)
                sp.dma_start(b2b[eh][:, :], b2[bass.ds(e, 1), :].partition_broadcast(P).rearrange("p e d -> p (e d)"))\
                    .then_inc(s[f"wld{eh}"], 16)
            sp.wait_ge(s["xc"], NB)
            weights(0, 0, 0)
            weights(0, 1, 0)
            with sp.Fori(1, 4) as el:
                weights(el, 0, el * 2 - 1)
                weights(el, 1, el * 2)
            for r in range(3):
                sp.wait_ge(s[f"scat{r}"], 16 * 3 * NE)

        @block.gpsimd
        def _(po):
            g = nc.gpsimd
            g.memset(mhalf[:, :], -0.5).then_inc(s["zero"], 1)
            g.iota(iot[:, :], [[1, KTOK]], base=0, channel_multiplier=0, allow_small_or_imprecise_dtypes=True)\
                .then_inc(s["zero"], 1)
            po.wait_ge(s["cls_d"], 1)
            po.wait_ge(s["zero"], 1)
            g.tensor_tensor(cst8[:, 3:4], cst8[:, 2:3], mhalf[:, 0:1], ALU.pow).then_inc(s["cls_p"], 1)
            po.wait_ge(s["cls_d"], 2)
            g.tensor_tensor(cpw[:, 2:4], cpw[:, 0:2], mhalf[:, 0:2], ALU.pow).then_inc(s["cls_p"], 1)

            def columns(m, have2):
                if have2:
                    po.wait_ge(s["z_done"], m.n - 1)
                xv = XS[:, bass.ds(m.n, 1), :, :].rearrange("p b h c -> p (b h) c") if not isinstance(m.n, int) \
                    else XS[:, m.n, :, :]
                x0, x1 = xv[:, :, 0::2], xv[:, :, 1::2]
                dst = Xc[m.p]
                g.tensor_tensor(L1[:, :, :], x0, x1, ALU.add).then_inc(s["xc_l"], 1)
                g.tensor_tensor(dst[:, :, 128:256], x0, x1, ALU.subtract)
                po.wait_ge(s["xc_l"], m.n * 2 + 1)
                g.tensor_tensor(L2[:, :, :], L1[:, :, 0::2], L1[:, :, 1::2], ALU.add).then_inc(s["xc_l"], 1)
                g.tensor_tensor(dst[:, :, 64:128], L1[:, :, 0::2], L1[:, :, 1::2], ALU.subtract)
                po.wait_ge(s["xc_l"], m.n * 2 + 2)
                g.tensor_tensor(dst[:, :, 0:32], L2[:, :, 0::2], L2[:, :, 1::2], ALU.add)
                g.tensor_tensor(dst[:, :, 32:64], L2[:, :, 0::2], L2[:, :, 1::2], ALU.subtract).then_inc(s["xc"], 1)

            def emit(i, k, have, k0):
                m = Img(i, k - 2)
                if have(k - 2):
                    st = ST[m.p]
                    var = st[:, 4:8].rearrange("p (h t) -> p h t", t=2)[:, :, 1]
                    mean = st[:, 4:8].rearrange("p (h t) -> p h t", t=2)[:, :, 0]
                    if k0 >= 4:
                        po.wait_ge(s["base"], m.n - 1)
                        po.wait_ge(s["yp"], m.n - 1)
                    po.wait_ge(s["st1"], m.n + 1)
                    c0 = m.n * 4
                    apart(po)
                    g.tensor_scalar(A1[:, 0:2], var, 1.0, EPS, ALU.mult, ALU.add)
                    g.tensor_scalar(A1[:, 2:4], var, 1.0 + EPS, EPS * EPS, ALU.mult, ALU.add).then_inc(s["pw1_c"], 1)
                    po.wait_ge(s["pw1_c"], c0 + 1)
                    g.tensor_tensor(R4[m.p][:, :], A1[:, :], mhalf[:, :], ALU.pow).then_inc(s["pw1_c"], 1)
                    po.wait_ge(s["pw1_c"], c0 + 2)
                    g.tensor_tensor(N4[m.p][:, :].rearrange("p (a h) -> p a h", a=2),
                                    R4[m.p][:, :].rearrange("p (a h) -> p a h", a=2),
                                    mean.unsqueeze(1).to_broadcast([P, 2, 2]), ALU.mult).then_inc(s["pw1_c"], 1)
                    g.tensor_scalar(O1[m.p][:, :], R4[m.p][:, 0:2], 1.0, 1.0, ALU.mult, ALU.add)
                    g.tensor_copy(st[:, 12:14], R4[m.p][:, 0:2]).then_inc(s["pw1_c"], 1)
                    po.wait_ge(s["pw1_c"], c0 + 3)
                    apart(po)
                    g.tensor_scalar(N4[m.p][:, :], N4[m.p][:, :], -1.0, 0.0, ALU.mult, ALU.add)\
                        .then_inc(s["pw1"], 1)
                    po.wait_ge(s["pw1_c"], c0 + 4)
                    g.tensor_copy(TUG[:, bass.ds(m.n, 1), :, :].rearrange("p b h e -> p (b h) e"), U[m.p][:, :, D:DG])
                    g.tensor_copy(TEG[:, bass.ds(m.n, 1), :, :].rearrange("p b h e -> p (b h) e"), Ex[m.p][:, :, D:DG])
                    g.tensor_copy(TST[:, bass.ds(m.n, 1), :].rearrange("p b k -> p (b k)"), st[:, :])\
                        .then_inc(s["tab"], 1)
                m = Img(i, k)
                if have(k):
                    if k0 >= 2:
                        po.wait_ge(s["hcE"], m.n - 1)
                    po.wait_ge(s["st0"], m.n + 1)
                    st = ST[m.p]
                    var = st[:, 0:4].rearrange("p (h t) -> p h t", t=2)[:, :, 1]
                    mean = st[:, 0:4].rearrange("p (h t) -> p h t", t=2)[:, :, 0]
                    c0 = m.n * 3
                    apart(po)
                    g.tensor_scalar(A0[:, :], var, 1.0, EPS, ALU.mult, ALU.add).then_inc(s["pw0_c"], 1)
                    po.wait_ge(s["pw0_c"], c0 + 1)
                    g.tensor_tensor(st[:, 10:12], A0[:, :], mhalf[:, 0:2], ALU.pow).then_inc(s["pw0_c"], 1)
                    po.wait_ge(s["pw0_c"], c0 + 2)
                    g.tensor_tensor(N0[m.p][:, :], st[:, 10:12], mean, ALU.mult).then_inc(s["pw0_c"], 1)
                    po.wait_ge(s["pw0_c"], c0 + 3)
                    apart(po)
                    g.tensor_scalar(N0[m.p][:, :], N0[m.p][:, :], -1.0, 0.0, ALU.mult, ALU.add)\
                        .then_inc(s["pw0"], 1)
                if have(k + 1):
                    columns(Img(i, k + 1), k0 >= 1)
            po.wait_ge(s["wp"], 1)
            po.wait_ge(s["lg_mm"], 1)
            po.wait_ge(s["ld_x0"], 16)
            po.wait_ge(s["ld_x1"], 16)
            columns(Img(0, 0), False)
            steps(po, emit)

            tok = bass.IndirectOffsetOnAxis

            def gather(eh, count):
                apart(po)
                for t, m in enumerate(SLOTS):
                    g.indirect_dma_start(out=yg[eh][0:m, t, :], out_offset=None, in_=ypre,
                                         in_offset=tok(ap=idx[eh][0:m, t:t + 1], axis=0))\
                        .then_inc(s[f"gat{eh}"], 16)
                    g.indirect_dma_start(out=kv[eh][0:m, t, :], out_offset=None, in_=vtab,
                                         in_offset=tok(ap=idx[eh][0:m, t:t + 1], axis=0))\
                        .then_inc(s[f"kvg{eh}"], 16)

            def scatter(q, eh):
                for t, m in enumerate(SLOTS):
                    po.wait_ge(s["omul"], q * 9 + t + 1)
                    if t == 0:
                        for r in range(3):
                            after(po, f"scat{r}", q * 16 * 3)
                    apart(po)
                    g.indirect_dma_start(out=out_rows, out_offset=tok(ap=idx[eh][0:m, t:t + 1], axis=0),
                                         in_=ob[t % 3][0:m, :], in_offset=None, compute_op=ALU.add)\
                        .then_inc(s[f"scat{t % 3}"], 16)
            po.wait_ge(s["cls_st"], 48)
            for q in range(2):
                po.wait_ge(s[f"base_st{q}"], 16 * NB // 2)
                po.wait_ge(s[f"yp_st{q}"], 16 * NB // 2)
            po.wait_ge(s["vt_st"], 32)
            po.wait_ge(s["ixd"], 1)
            gather(0, 1)
            po.wait_ge(s["ixd"], 2)
            gather(1, 2)
            scatter(0, 0)
            with po.Fori(1, 4) as el:
                po.wait_ge(s["ixd"], el * 2 + 1)
                gather(0, 0)
                scatter(el * 2 - 1, 1)
                po.wait_ge(s["ixd"], el * 2 + 2)
                gather(1, 0)
                scatter(el * 2, 0)
            scatter(NE - 1, 1)

        @block.scalar
        def _(act):
            n = 0
            for lv, W in ((1, Wd3), (2, Wd2), (3, Wd1)):
                rows = D >> lv
                src = W.rearrange("(k y x) j -> y k (x j)", k=3, y=rows)
                for h in range(NH):
                    for r in range(1 << lv):
                        act.dma_start(bands[lv][r::1 << lv, h, :, :], src[h * rows // 2:(h + 1) * rows // 2, :, :])\
                            .then_inc(s["ld_band"], 16)
                        n += 1
            srcA = Wa.rearrange("(y x) j -> y (x j)", y=32)
            for h in range(NH):
                for r in range(8):
                    act.dma_start(bandA[r::8, h, :], srcA[h * 16:(h + 1) * 16, :]).then_inc(s["ld_band"], 16)
                    n += 1
            assert n == 44
            act.dma_start(bandb[:, 0:1], ba.unsqueeze(0).partition_broadcast(NB).rearrange("p a b -> p (a b)")).then_inc(s["ld_band2"], 16)
            for q, b in ((1, bd1), (4, bd2), (7, bd3)):
                act.dma_start(bandb[:, q:q + 3], b.unsqueeze(0).partition_broadcast(NB).rearrange("p a b -> p (a b)")).then_inc(s["ld_band2"], 16)
            act.dma_start(clsb[:, :], cls_tok.rearrange("a b d -> (a b) d").partition_broadcast(P).rearrange("p a d -> p (a d)")).then_inc(s["ld_band3"], 16)
            act.dma_start(gwb[:, :, :], gate_w.unsqueeze(0).partition_broadcast(P).rearrange("p a e d -> p (a e) d")).then_inc(s["ld_band3"], 16)
            A = nc.scalar
            act.wait_ge(s["cls_d"], 3)
            A.activation(cgl[:, :], cgl[:, :], ACT.Tanh).then_inc(s["cls_a"], 1)
            act.wait_ge(s["z_c"], 3)
            A.activation(z2[:, 1:NJ], z2[:, 1:NJ], ACT.Exp)
            A.activation(z2[:, 0:1], zz[:, 0:1], ACT.Exp, scale=-1.0).then_inc(s["z_e"], 1)

            def emit(i, k, have, k0):
                a2, a1, a0 = Img(i, k - 2), Img(i, k - 1), Img(i, k)
                if have(k - 2):
                    if k0 >= 4:
                        act.wait_ge(s["av"], a2.n - 1)
                    act.wait_ge(s["pt"], a2.n + 1)
                    A.activation(PTS[a2.p][:, :], Pb[:, 0:384], ACT.Copy).then_inc(s["pt_ev"], 1)
                if have(k - 1):
                    if k0 >= 3:
                        act.wait_ge(s["sm"], a1.n - 1)
                    act.wait_ge(s["et"], a1.n + 1)
                    A.activation(ET[a1.p][:, :, 1:NT], Tb[:, :].rearrange("p (c t) -> p c t", c=2), ACT.Copy)\
                        .then_inc(s["et_ev"], 1)
                    act.wait_ge(s["er"], a1.n + 1)
                    A.activation(ERT[a1.p][:, :, :], Rb[:, :].rearrange("p (c t) -> p c t", c=2), ACT.Copy)\
                        .then_inc(s["er_ev"], 1)
                if have(k - 2):
                    if k0 >= 4:
                        act.wait_ge(s[f"yp_st{a2.p}"], a2.h * 16)
                    act.wait_ge(s["pw1"], a2.n + 1)
                    for h in range(NH):
                        last = A.activation(Yp[a2.p][:, h, :], H1[a2.p][:, h, :], ACT.Identity,
                                            bias=N4[a2.p][:, 2 + h:3 + h], scale=R4[a2.p][:, 2 + h:3 + h])
                    last.then_inc(s["yp"], 1)
                if have(k):
                    if k0 >= 2:
                        act.wait_ge(s["h1"], a0.n - 1)
                        act.wait_ge(s["av"], a0.n - 1)
                        act.wait_ge(s["tab"], a0.n - 1)
                    act.wait_ge(s["st0_b"], a0.n + 1)
                    A.activation(hc[a0.p][:, :, :], Hb[:, :].rearrange("p (h c) -> p h c", h=NH), ACT.Copy)
                    act.wait_ge(s["pw0"], a0.n + 1)
                    for h in range(NH):
                        last = A.activation(Ex[a0.p][:, h, 0:D], Hb[:, h * D:(h + 1) * D], ACT.Identity,
                                            bias=N0[a0.p][:, h:h + 1], scale=ST[a0.p][:, 10 + h:11 + h])
                    last.then_inc(s["hcE"], 1)
                if have(k - 1):
                    if k0 >= 3:
                        act.wait_ge(s["pt"], a1.n - 1)
                        act.wait_ge(s["u"], a1.n - 1)
                    act.wait_ge(s["nmax"], a1.n + 1)
                    A.activation(Pr[a1.p][:, 0:129], Sb[:, 0:129], ACT.Exp, bias=nmx[a1.p][:, 0:1],
                                 accum_out=rsm[a1.p][:, 0:1])
                    A.activation(Pr[a1.p][:, 129:386], Sb[:, 129:386], ACT.Exp, bias=nmx[a1.p][:, 1:2],
                                 accum_out=rsm[a1.p][:, 1:2]).then_inc(s["pexp"], 1)
            steps(act, emit)
            act.wait_ge(s["gt_c"], 6)
            A.activation(GM[:, :, :, :], GL[:, :, :, :], ACT.Tanh).then_inc(s["gt_t"], 1)

            def hidden(q, eh, e):
                for c, (t0, t1) in enumerate(CHUNKS):
                    w = sum(SLOTS[t0:t1])
                    n0 = q * 3 + c
                    for f in range(8):
                        act.wait_ge(s["hmm"], n0 * 8 + f + 1)
                        apart(act)
                        last = A.activation(hT[(c + eh) % 2][:, f, 0:w], bank[f % 2][:, 0:w], ACT.Gelu_apprx_tanh,
                                            bias=b1s[:, bass.ds(e, 1), f])
                        last.then_inc(s["hact"], 1)
                    for t in range(t0, t1):
                        m = SLOTS[t]
                        act.wait_ge(s["oadd"], q * 9 + t + 1)
                        after(act, f"scat{t % 3}", (q * 3 + t // 3) * 16)
                        apart(act)
                        A.activation(ob[t % 3][0:m, :], ot[t % 2][0:m, :], ACT.Copy,
                                     scale=kv[eh][0:m, t, bass.ds(e, 1)]).then_inc(s["omul"], 1)
            act.wait_ge(s["ld_par"], 80)
            act.wait_ge(s["kvg0"], 16 * 9)
            hidden(0, 0, 0)
            act.wait_ge(s["kvg1"], 16 * 9)
            hidden(1, 1, 4)
            with act.Fori(1, 4) as el:
                act.wait_ge(s["kvg0"], (el + 1) * 16 * 9)
                hidden(el * 2, 0, el)
                act.wait_ge(s["kvg1"], (el + 1) * 16 * 9)
                hidden(el * 2 + 1, 1, el + 4)

        @block.tensor
        def _(pe):
            T = nc.tensor
            pe.wait_ge(s["ld_const"], 16)
            pe.wait_ge(s["cls_t"], 1)
            for c in range(2):
                last = T.transpose(Tb[:, c * P:(c + 1) * P], CX[:, c * P:(c + 1) * P], ident)
            last.then_inc(s["et0"], 1)
            pe.wait_ge(s["wp"], 1)
            for part_, load in ((0, "ld_x0"), (1, "ld_x1")):
                pe.wait_ge(s[load], 16)
                for h in range(NH):
                    for c in range(D // CG):
                        first, final = h == 0 and c == 0, h == NH - 1 and c == D // CG - 1
                        last = T.matmul(Zb[0:CG * NJ, part_ * 128:(part_ + 1) * 128],
                                        WP[:, h, c * CG:(c + 1) * CG, :].rearrange("p c j -> p (c j)"),
                                        XS[:, part_ * 16:(part_ + 1) * 16, h, c * CG:(c + 1) * CG],
                                        start=first, stop=final)
            last.then_inc(s["lg_mm"], 1)
            pe.wait_ge(s["lg_r"], 1)
            T.matmul(Hb[0:NB, 0:NJ], lgr[:, :], cst("pick")[0:CG * NJ, :], start=True, stop=True).then_inc(s["z_mm"], 1)
            pe.wait_ge(s["bw_t"], 1)
            T.transpose(Hb[0:NJ, 32:32 + NB], bw[:, :], ident[0:NB, 0:NB]).then_inc(s["z_mm"], 1)
            pe.wait_ge(s["bw_c"], 1)
            for q in range(LEAF):
                last = T.matmul(Hb[:, 128 + q * NB:128 + (q + 1) * NB], cst("spread")[0:NJ, q * P:(q + 1) * P],
                                bwT[:, :], start=True, stop=True)
            last.then_inc(s["w8_mm"], 1)
            pe.wait_ge(s["cvt"], 1)
            pe.wait_ge(s["ld_par"], 80)
            pe.wait_ge(s["w8"], 1)

            def emit(i, k, have, k0):
                a2, a1, a0 = Img(i, k - 2), Img(i, k - 1), Img(i, k)
                if have(k - 2):
                    if k0 >= 3:
                        pe.wait_ge(s["pt_ev"], a2.n)
                    pe.wait_ge(s["pexp"], a2.n + 1)
                    pe.wait_ge(s["eg_ev"], a2.n + 1)
                    for q, c0 in enumerate((1, 130, 258)):
                        last = T.transpose(Pb[:, q * P:(q + 1) * P], Pr[a2.p][:, c0:c0 + P], ident)
                    last.then_inc(s["pt"], 1)
                if have(k):
                    if k0 >= 1:
                        pe.wait_ge(s["zw"], a0.n)
                    pe.wait_ge(s["xc"], a0.n + 1)
                    T.matmul(Zb[:, :], cst("fwd"), Xc[a0.p].rearrange("p h c -> p (h c)"), start=True, stop=True)\
                        .then_inc(s["z_done"], 1)
                if have(k - 1):
                    if k0 >= 2:
                        pe.wait_ge(s["et_ev"], a1.n)
                    pe.wait_ge(s["hcE"], a1.n + 1)
                    for c in range(2):
                        for h in range(NH):
                            last = T.transpose(Tb[:, c * D + h * P:c * D + (h + 1) * P],
                                               Ex[a1.p][:, h, c * P:(c + 1) * P], ident)
                    last.then_inc(s["et"], 1)
                if have(k - 2):
                    if k0 >= 3:
                        pe.wait_ge(s["u"], a2.n)
                    pe.wait_ge(s["pt_ev"], a2.n + 1)
                    T.matmul(Ab[0][:, 0:DG], PTS[a2.p][:, 0:P], Ex[a2.p][:, 0, :], start=True, stop=True)
                    T.matmul(Ab[1][:, 0:DG], PTS[a2.p][:, P:2 * P], Ex[a2.p][:, 0, :], start=True, stop=False)
                    T.matmul(Ab[1][:, 0:DG], PTS[a2.p][:, 2 * P:3 * P], Ex[a2.p][:, 1, :], start=False, stop=True)\
                        .then_inc(s["av"], 1)
                if have(k - 1):
                    if k0 >= 2:
                        pe.wait_ge(s["er_ev"], a1.n)
                    pe.wait_ge(s["et_ev"], a1.n + 1)
                    for e in range(2):
                        for c in range(2):
                            last = T.matmul(Rb[:, e * D:(e + 1) * D], Rw[:, c, e * P:(e + 1) * P],
                                            ET[a1.p][:, c, 1:NT], start=(c == 0), stop=(c == 1))
                    last.then_inc(s["er"], 1)
                if have(k):
                    if k0 >= 1:
                        pe.wait_ge(s["hcE"], a0.n)
                    pe.wait_ge(s["q"], a0.n + 1)
                    T.matmul(Hb[:, :], cst("inv"), Q[a0.p].rearrange("p h c -> p (h c)"), start=True, stop=True)\
                        .then_inc(s["h0"], 1)
                if have(k - 1):
                    if k0 >= 2:
                        pe.wait_ge(s["pexp"], a1.n)
                        pe.wait_ge(s["pt_ev"], a1.n)
                    for h in range(NH):
                        for c in range(2):
                            last = T.matmul(Pb[:, 400 + h * NE:400 + (h + 1) * NE],
                                            ET[a1.p][:, c, 1 + h * P:1 + (h + 1) * P], gwT[:, c, :],
                                            start=(c == 0), stop=(c == 1))
                    last.then_inc(s["eg"], 1)
                    pe.wait_ge(s["er_ev"], a1.n + 1)
                    for h, (c0, w) in enumerate(((0, 129), (129, 257))):
                        for c in range(2):
                            T.matmul(Sb[:, c0:c0 + w], ERT[a1.p][:, c, h * P:(h + 1) * P], ET[a1.p][:, c, 0:w],
                                     start=(c == 0), stop=False)
                        last = T.matmul(Sb[:, c0 + w - P:c0 + w], identb[:, :], causalb[:, :], start=False, stop=True)
                    last.then_inc(s["sm"], 1)
            steps(pe, emit)

            pe.wait_ge(s["vsp_t"], 1)
            for h in range(NH):
                for eh in range(2):
                    q = 2 * h + eh
                    last = T.transpose(bank[0][:, q * P:(q + 1) * P],
                                       GV[:, h, eh, :, :].rearrange("p e b -> p (e b)"), ident)
            last.then_inc(s["vsp"], 1)
            with pe.Fori(0, BITS) as i:
                pe.wait_ge(s["cn"], i + 1)
                T.matmul(bank[1][:, 0:2], cst("same"), cnt[:, :], start=True, stop=True).then_inc(s["thr"], 1)
            pe.wait_ge(s["tk_c"], 1)
            T.matmul(bank[2][:, 0:2], cst("same"), cgt[:, :], start=True, stop=True)
            T.matmul(bank[3][:, 0:2], cst("before"), tot[:, :], start=True, stop=True).then_inc(s["tk_mm"], 1)
            pe.wait_ge(s["tk_c"], 2)
            T.matmul(bank[4][:, 0:2], cst("before"), tot[:, :], start=True, stop=True).then_inc(s["tk_mm"], 1)

            def places(q):
                pe.wait_ge(s["ohd"], q + 1)
                for t, m in enumerate(SLOTS):
                    if t or not isinstance(q, int) or q:
                        pe.wait_ge(s["smc"], q * 9 + t)
                    T.matmul(bank[7][0:m, 0:NT + 3], oh[:, t * P:t * P + m], TB[:, q_side[0], :], start=True,
                             stop=True).then_inc(s["smm"], 1)
            q_side = [0]

            def expert(q, eh):
                pe.wait_ge(s[f"wld{eh}"], 48 * (q_half[0] + 1))
                pe.wait_ge(s[f"gat{eh}"], 16 * 9 * (q_half[0] + 1))

                def second(c):
                    t0, t1 = CHUNKS[c]
                    pe.wait_ge(s["hact"], (q * 3 + c + 1) * 8)
                    for t in range(t0, t1):
                        m, at = SLOTS[t], sum(SLOTS[t0:t])
                        after(pe, "oadd", q * 9 + t - 1)
                        for f in range(8):
                            last = T.matmul(bank[4 + t % 2][0:m, 0:D], hT[(c + eh) % 2][:, f, at:at + m],
                                            w2s[eh][:, f, :], start=(f == 0), stop=(f == 7))
                        last.then_inc(s["om"], 1)
                for c, (t0, t1) in enumerate(CHUNKS):
                    w = sum(SLOTS[t0:t1])
                    n0 = q * 3 + c
                    after(pe, "yt", n0)
                    for d in range(2):
                        for t in range(t0, t1):
                            m, at = SLOTS[t], (t - t0) * P
                            last = T.transpose(bank[2 + d][:, at:at + m], yg[eh][0:m, t, d * P:(d + 1) * P],
                                               ident[0:m, 0:m])
                    last.then_inc(s["yt_t"], 1)
                    pe.wait_ge(s["yt"], n0 + 1)
                    for f in range(8):
                        if c == 0 and f < 2:
                            after(pe, "hact", n0 * 8 + f - 1)
                        else:
                            pe.wait_ge(s["hact"], n0 * 8 + f - 1)
                        for d in range(2):
                            last = T.matmul(bank[f % 2][:, 0:w], w1s[eh][:, d, f * P:(f + 1) * P], yT[:, d, 0:w],
                                            start=(d == 0), stop=(d == 1))
                        last.then_inc(s["hmm"], 1)
                    second(c)
            q_half = [0]

            def work(q, el, eh, nxt):
                q_half[0] = el
                if nxt:
                    q_side[0] = 1 - eh
                    places(q + 1)
                expert(q, eh)
            q_side[0] = 0
            pe.wait_ge(s["tc"], 1)
            places(0)
            work(0, 0, 0, True)
            with pe.Fori(0, 3) as el:
                work(el * 2 + 1, el, 1, True)
                work(el * 2 + 2, el + 1, 0, True)
            work(NE - 1, 3, 1, False)

        @block.vector
        def _(dve):
            v = nc.vector
            dve.wait_ge(s["ld_const"], 16)
            v.tensor_copy(identb[:, :], ident)
            v.tensor_copy(causalb[:, :], cst("causal")).then_inc(s["cvt"], 1)
            dve.wait_ge(s["ld_band3"], 32)
            k = [0]

            def link(ins):
                k[0] += 1
                ins.then_inc(s["cls_t2"], 1)
                dve.wait_ge(s["cls_t2"], k[0])
            s["cls_t2"] = sem("cls_chain")
            link(v.bn_stats(cbn[:, :], clsb[:, :]))
            link(v.bn_aggr(cst8[:, 0:2], cbn[:, :]))
            v.tensor_scalar(cst8[:, 2:3], cst8[:, 1:2], EPS, None, ALU.add).then_inc(s["cls_d"], 1)
            v.tensor_reduce(sg[:, :], gwb[:, :, :], AX_X, ALU.add)
            dve.wait_ge(s["cls_p"], 1)
            link(v.tensor_scalar(CX[:, 0:D], clsb[:, :], cst8[:, 0:1], cst8[:, 3:4], ALU.subtract, ALU.mult))
            for e in range(NE):
                last = v.tensor_tensor_reduce(out=junk[:, :], in0=CX[:, 0:D], in1=gwb[:, e, :], scale=1.0, scalar=0.0,
                                              op0=ALU.mult, op1=ALU.add, accum_out=CX[:, D + e:D + e + 1])
                last = link(last)
            link(v.tensor_tensor(ch[:, 0:D], clsb[:, :], CX[:, 0:D], ALU.add))
            v.tensor_copy(junk[:, 0:1], CX[:, 0:1]).then_inc(s["cls_t"], 1)
            link(v.bn_stats(cbn[:, :], ch[:, 0:D]))
            for e in range(NE):
                link(v.tensor_tensor_reduce(out=junk[:, :], in0=ch[:, 0:D], in1=gwb[:, e, :], scale=1.0, scalar=0.0,
                                            op0=ALU.mult, op1=ALU.add, accum_out=ch[:, D + e:D + e + 1]))
            link(v.bn_aggr(cst8[:, 4:6], cbn[:, :]))
            v.tensor_scalar(cpw[:, 0:1], cst8[:, 5:6], EPS, None, ALU.add)
            v.tensor_scalar(cpw[:, 1:2], cst8[:, 5:6], 1.0 + EPS, EPS * EPS, ALU.mult, ALU.add).then_inc(s["cls_d"], 1)
            dve.wait_ge(s["cls_p"], 2)
            link(v.tensor_scalar(cyp[:, :], ch[:, 0:D], cst8[:, 4:5], cpw[:, 2:3], ALU.subtract, ALU.mult))
            v.tensor_tensor(cbs[:, :], cyp[:, :], ch[:, 0:D], ALU.add)
            link(v.tensor_scalar(cgl[:, :], sg[:, :], cst8[:, 4:5], None, ALU.mult))
            link(v.tensor_tensor(cgl[:, :], ch[:, D:DG], cgl[:, :], ALU.subtract))
            link(v.tensor_scalar(cgl[:, :], cgl[:, :], cpw[:, 2:3], None, ALU.mult))
            v.tensor_scalar(cyp[:, :], ch[:, 0:D], cst8[:, 4:5], cpw[:, 3:4], ALU.subtract, ALU.mult)\
                .then_inc(s["cls_d"], 1)
            dve.wait_ge(s["cls_a"], 1)
            v.tensor_scalar(vcls[:, :], cgl[:, :], 1.0, 0.5, ALU.add, ALU.mult).then_inc(s["cls_g"], 1)
            dve.wait_ge(s["et0"], 1)
            for q in range(2):
                last = v.tensor_copy(ET[q][:, :, 0], Tb[:, 0:D].rearrange("p (c t) -> p c t", c=2)[:, :, 0])
            link(last)

            dve.wait_ge(s["ld_band"], 16 * 44)
            for h in range(NH):
                for lv in (1, 2, 3):
                    sign = cst("sign")[:, lv - 1:lv]
                    last = v.scalar_tensor_tensor(out=bsum[lv][:, h, :], in0=bands[lv][:, h, 2, :], scalar=sign,
                                                  in1=bands[lv][:, h, 1, :], op0=ALU.mult, op1=ALU.add)
            last.then_inc(s["wp_part"], 1)
            dve.wait_ge(s["wp_part"], 1)
            for h in range(NH):
                for lv in (1, 2, 3):
                    sign = cst("sign")[:, lv - 1:lv]
                    j0 = 1 + 3 * (3 - lv)
                    n = D >> lv
                    dst = WP[:, h, :, j0:j0 + 3].rearrange("p (x s u) j -> p x s u j", x=n, s=2)
                    for q, op in ((0, ALU.add), (1, ALU.subtract)):
                        for u in range(1 << (lv - 1)):
                            v.scalar_tensor_tensor(out=dst[:, :, q, u, :],
                                                   in0=bands[lv][:, h, 0, :].rearrange("p (x j) -> p x j", j=3),
                                                   scalar=sign,
                                                   in1=bsum[lv][:, h, :].rearrange("p (x j) -> p x j", j=3),
                                                   op0=ALU.mult, op1=op)
                last = v.tensor_copy(WP[:, h, :, 0:1].rearrange("p (x u) j -> p x (u j)", u=8),
                                     bandA[:, h, :].unsqueeze(2).to_broadcast([P, 32, 8]))
            last.then_inc(s["wp"], 1)
            dve.wait_ge(s["lg_mm"], 1)
            v.tensor_tensor(LM[:, :, :], Zb[0:CG * NJ, 0:NB * CG].rearrange("p (b c) -> p b c", c=CG),
                            cst("diag")[0:CG * NJ, :].unsqueeze(1).to_broadcast([CG * NJ, NB, CG]), ALU.mult)\
                .then_inc(s["lg_m"], 1)
            dve.wait_ge(s["lg_m"], 1)
            v.tensor_reduce(lgr[:, :], LM[:, :, :], AX_X, ALU.add).then_inc(s["lg_r"], 1)
            dve.wait_ge(s["z_mm"], 1)
            dve.wait_ge(s["ld_band2"], 64)
            v.tensor_tensor(zz[:, :], Hb[0:NB, 0:NJ], bandb[:, :], ALU.add).then_inc(s["z_c"], 1)
            dve.wait_ge(s["z_c"], 1)
            v.tensor_reduce(mx3[:, :], zz[:, 1:NJ].rearrange("p (l j) -> p l j", j=3), AX_X, ALU.max)\
                .then_inc(s["z_c"], 1)
            dve.wait_ge(s["z_c"], 2)
            v.tensor_tensor(z2[:, 1:NJ].rearrange("p (l j) -> p l j", j=3), zz[:, 1:NJ].rearrange("p (l j) -> p l j", j=3),
                            mx3[:, :].unsqueeze(2).to_broadcast([NB, 3, 3]), ALU.subtract).then_inc(s["z_c"], 1)
            dve.wait_ge(s["z_e"], 1)
            v.tensor_reduce(mx3[:, :], z2[:, 1:NJ].rearrange("p (l j) -> p l j", j=3), AX_X, ALU.add)
            link(v.tensor_scalar(bw[:, 0:1], z2[:, 0:1], 1.0, None, ALU.add))
            v.reciprocal(mx3[:, :], mx3[:, :])
            link(v.reciprocal(bw[:, 0:1], bw[:, 0:1]))
            v.tensor_tensor(bw[:, 1:NJ].rearrange("p (l j) -> p l j", j=3), z2[:, 1:NJ].rearrange("p (l j) -> p l j", j=3),
                            mx3[:, :].unsqueeze(2).to_broadcast([NB, 3, 3]), ALU.mult).then_inc(s["bw_t"], 1)
            dve.wait_ge(s["z_mm"], 2)
            v.tensor_copy(bwT[:, :], Hb[0:NJ, 32:32 + NB]).then_inc(s["bw_c"], 1)
            dve.wait_ge(s["w8_mm"], 1)
            for q, (c0, c1) in enumerate(((0, 1), (1, 2), (2, 4), (4, 8))):
                last = v.tensor_copy(W8[:, :, c0:c1],
                                     Hb[:, 128 + q * NB:128 + (q + 1) * NB].unsqueeze(2).to_broadcast([P, NB, c1 - c0]))
            last.then_inc(s["w8"], 1)
            dve.wait_ge(s["w8"], 1)

            def emit(i, k, have, k0):
                a2, a1, a0 = Img(i, k - 2), Img(i, k - 1), Img(i, k)
                if have(k):
                    p = a0.p
                    dve.wait_ge(s["z_done"], a0.n + 1)
                    w = W8[:, bass.ds(a0.n, 1), :].to_broadcast([P, NH, 8]).unsqueeze(3).to_broadcast([P, NH, 8, 32])
                    v.tensor_tensor(Zw[p].rearrange("p h (g c) -> p h g c", g=8),
                                    Zb[:, :].rearrange("p (h g c) -> p h g c", h=NH, g=8), w, ALU.mult)\
                        .then_inc(s["zw"], 1)
                    dve.wait_ge(s["zw"], a0.n + 1)
                    lo, hi = Zw[p][:, :, 0:32], Zw[p][:, :, 32:64]
                    v.tensor_tensor(I2[:, :, 0::2], lo, hi, ALU.add)
                    v.tensor_tensor(I2[:, :, 1::2], lo, hi, ALU.subtract).then_inc(s["inv"], 1)
                    dve.wait_ge(s["inv"], a0.n * 2 + 1)
                    hi = Zw[p][:, :, 64:128]
                    v.tensor_tensor(I1[:, :, 0::2], I2[:, :, :], hi, ALU.add)
                    v.tensor_tensor(I1[:, :, 1::2], I2[:, :, :], hi, ALU.subtract).then_inc(s["inv"], 1)
                    dve.wait_ge(s["inv"], a0.n * 2 + 2)
                    if k0 >= 2:
                        dve.wait_ge(s["h0"], a0.n - 1)
                    hi = Zw[p][:, :, 128:256]
                    v.tensor_tensor(Q[p][:, :, 0::2], I1[:, :, :], hi, ALU.add)
                    v.tensor_tensor(Q[p][:, :, 1::2], I1[:, :, :], hi, ALU.subtract).then_inc(s["q"], 1)
                if have(k - 2):
                    p = a2.p
                    dve.wait_ge(s["pexp"], a2.n + 1)
                    v.reciprocal(ST[p][:, 8:10], rsm[p][:, :]).then_inc(s["rv"], 1)
                    if k0 >= 4:
                        dve.wait_ge(s["tab"], a2.n - 1)
                        dve.wait_ge(s["yp"], a2.n - 1)
                    dve.wait_ge(s["av"], a2.n + 1)
                    for h in range(NH):
                        last = v.scalar_tensor_tensor(out=U[p][:, h, :], in0=CX[:, :],
                                                      scalar=Pr[p][:, 129 * h:129 * h + 1],
                                                      in1=Ab[h][:, 0:DG], op0=ALU.mult, op1=ALU.add)
                    last.then_inc(s["u"], 1)
                    dve.wait_ge(s["u"], a2.n + 1)
                    dve.wait_ge(s["rv"], a2.n + 1)
                    for h in range(NH):
                        last = v.scalar_tensor_tensor(out=H1[p][:, h, :], in0=U[p][:, h, 0:D],
                                                      scalar=ST[p][:, 8 + h:9 + h], in1=hc[p][:, h, :],
                                                      op0=ALU.mult, op1=ALU.add)
                    last.then_inc(s["h1"], 1)
                    dve.wait_ge(s["h1"], a2.n + 1)
                    for h in range(NH):
                        last = v.bn_stats(bn1[:, h, :], H1[p][:, h, :])
                    last.then_inc(s["st1_b"], 1)
                    dve.wait_ge(s["st1_b"], a2.n + 1)
                    apart(dve)
                    for h in range(NH):
                        last = v.bn_aggr(ST[p][:, 4 + 2 * h:6 + 2 * h], bn1[:, h, :])
                    last.then_inc(s["st1"], 1)
                if have(k - 1):
                    if k0 >= 3:
                        dve.wait_ge(s["av"], a1.n - 1)
                        dve.wait_ge(s["tab"], a1.n - 1)
                    dve.wait_ge(s["eg"], a1.n + 1)
                    v.tensor_copy(Ex[a1.p][:, :, D:DG], Pb[:, 400:416].rearrange("p (h e) -> p h e", h=NH))\
                        .then_inc(s["eg_ev"], 1)
                if have(k):
                    p = a0.p
                    dve.wait_ge(s["h0"], a0.n + 1)
                    for h in range(NH):
                        last = v.bn_stats(bn0[:, h, :], Hb[:, h * D:(h + 1) * D])
                    last.then_inc(s["st0_b"], 1)
                    dve.wait_ge(s["st0_b"], a0.n + 1)
                    if k0 >= 2:
                        dve.wait_ge(s["tab"], a0.n - 1)
                    apart(dve)
                    for h in range(NH):
                        last = v.bn_aggr(ST[p][:, 2 * h:2 + 2 * h], bn0[:, h, :])
                    last.then_inc(s["st0"], 1)
                if have(k - 2):
                    p = a2.p
                    if k0 >= 4:
                        dve.wait_ge(s[f"base_st{p}"], a2.h * 16)
                    dve.wait_ge(s["pw1"], a2.n + 1)
                    for h in range(NH):
                        last = v.tensor_scalar(Bs[p][:, h, :], H1[p][:, h, :], O1[p][:, h:h + 1],
                                               N4[p][:, h:h + 1], ALU.mult, ALU.add)
                    last.then_inc(s["base"], 1)
                if have(k - 1):
                    p = a1.p
                    dve.wait_ge(s["sm"], a1.n + 1)
                    v.tensor_reduce(nmx[p][:, 0:1], Sb[:, 0:129], AX_X, ALU.max, negate=True)
                    v.tensor_reduce(nmx[p][:, 1:2], Sb[:, 129:386], AX_X, ALU.max, negate=True)\
                        .then_inc(s["nmax"], 1)
            steps(dve, emit)

            dve.wait_ge(s["tab"], NB)
            sh = [P, NB, NH, NE]

            def col(a, b, step=1):
                return TST[:, :, a:b:step]

            def wide(ap):
                return ap.unsqueeze(3).to_broadcast(sh)
            v.tensor_scalar(sd0[:, :, :], col(1, 4, 2), EPS, None, ALU.add)
            v.tensor_tensor(dm[:, :, :], col(0, 4, 2), col(4, 8, 2), ALU.subtract)
            v.tensor_tensor(GL[:, :, :, :], TUG[:, :, :, :], wide(col(8, 10)), ALU.mult).then_inc(s["gt_c"], 1)
            dve.wait_ge(s["gt_c"], 1)
            v.tensor_tensor(sd0[:, :, :], sd0[:, :, :], col(10, 12), ALU.mult).then_inc(s["gt_c"], 1)
            v.tensor_tensor(GM[:, :, :, :], wide(dm[:, :, :]),
                            sg[:, :].unsqueeze(1).to_broadcast([P, NB * NH, NE]).rearrange("p (b h) e -> p b h e", h=NH),
                            ALU.mult)
            dve.wait_ge(s["gt_c"], 2)
            v.tensor_tensor(TEG[:, :, :, :], TEG[:, :, :, :], wide(sd0[:, :, :]), ALU.mult).then_inc(s["gt_c"], 1)
            dve.wait_ge(s["gt_c"], 3)
            v.tensor_tensor(GL[:, :, :, :], GL[:, :, :, :], TEG[:, :, :, :], ALU.add).then_inc(s["gt_c"], 1)
            dve.wait_ge(s["gt_c"], 4)
            v.tensor_tensor(GL[:, :, :, :], GL[:, :, :, :], GM[:, :, :, :], ALU.add).then_inc(s["gt_c"], 1)
            dve.wait_ge(s["gt_c"], 5)
            v.tensor_tensor(GL[:, :, :, :], GL[:, :, :, :], wide(col(12, 14)), ALU.mult).then_inc(s["gt_c"], 1)
            dve.wait_ge(s["gt_t"], 1)
            for h in range(NH):
                last = v.tensor_scalar(GV[:, h, :, :, :].rearrange("p a e b -> p (a e) b"),
                                       GM[:, :, h, :].rearrange("p b e -> p e b"), 1.0, 0.5, ALU.add, ALU.mult)
            last.then_inc(s["vsp_t"], 1)
            for h in range(NH):
                v.tensor_scalar(GL[:, :, h, :], GM[:, :, h, :], 1.0, 0.5, ALU.add, ALU.mult).then_inc(s["gt_v"], 1)
            v.memset(one[:, :], 1.0)
            v.memset(Tv[:, :], 0.0)
            v.memset(Tc[:, :], 1.0)
            v.memset(bit[:, :], 1.0)
            for e in range(4):
                for eh in range(2):
                    v.tensor_copy(V[32 * e:32 * e + 32, eh, 0:1], vcls[32 * e:32 * e + 32, 4 * eh + e:4 * eh + e + 1])
            dve.wait_ge(s["vsp"], 1)
            last = v.tensor_copy(V[:, :, 1:NT].rearrange("p a (h t) -> p a h t", h=NH),
                                 bank[0][:, :].rearrange("p (h a t) -> p a h t", h=NH, a=2))
            link(last)
            s["step"] = sem("search_step")
            with dve.Fori(0, BITS) as i:
                for eh in range(2):
                    last = v.tensor_scalar(ge[:, eh, :], V[:, eh, :], Tc[:, eh:eh + 1], None, ALU.is_ge, ALU.add,
                                           accum_out=cnt[:, eh:eh + 1])
                last.then_inc(s["cn"], 1)
                dve.wait_ge(s["thr"], i + 1)
                v.scalar_tensor_tensor(out=mm2[:, :], in0=bank[1][:, 0:2], scalar=KTOK - 0.5, in1=bit[:, :],
                                       op0=ALU.is_ge, op1=ALU.mult).then_inc(s["step"], 1)
                dve.wait_ge(s["step"], i * 4 + 1)
                v.tensor_tensor(Tv[:, :], Tv[:, :], mm2[:, :], ALU.add).then_inc(s["step"], 1)
                v.tensor_scalar(bit[:, :], bit[:, :], 0.5, None, ALU.mult).then_inc(s["step"], 1)
                dve.wait_ge(s["step"], i * 4 + 3)
                v.tensor_tensor(Tc[:, :], Tv[:, :], bit[:, :], ALU.add).then_inc(s["step"], 1)
                dve.wait_ge(s["step"], i * 4 + 4)
            for eh in range(2):
                v.tensor_scalar(ge[:, eh, :], V[:, eh, :], Tv[:, eh:eh + 1], None, ALU.is_gt, ALU.add,
                                accum_out=cgt[:, eh:eh + 1])
                link(v.tensor_scalar(eq[:, eh, :], V[:, eh, :], Tv[:, eh:eh + 1], None, ALU.is_equal, ALU.add,
                                     accum_out=tot[:, eh:eh + 1]))
            v.tensor_copy(mm2[:, :], tot[:, :]).then_inc(s["tk_c"], 1)
            for eh in range(2):
                last = v.tensor_tensor_scan(sc[:, eh, :], one[:, :], eq[:, eh, :], 0.0, ALU.mult, ALU.add)
            dve.wait_ge(s["tk_mm"], 1)
            v.tensor_scalar(need[:, :], bank[2][:, 0:2], -1.0, float(KTOK), ALU.mult, ALU.add)
            link(v.tensor_copy(mm2[:, :], bank[3][:, 0:2]))
            link(v.tensor_tensor(need[:, :], need[:, :], mm2[:, :], ALU.subtract))
            for eh in range(2):
                link(v.scalar_tensor_tensor(out=eq[:, eh, :], in0=sc[:, eh, :], scalar=need[:, eh:eh + 1],
                                            in1=eq[:, eh, :], op0=ALU.is_le, op1=ALU.mult))
                link(v.tensor_tensor(ge[:, eh, :], ge[:, eh, :], eq[:, eh, :], ALU.add))
                link(v.tensor_tensor_scan(sc[:, eh, :], one[:, :], ge[:, eh, :], 0.0, ALU.mult, ALU.add))
            v.tensor_copy(tot[:, :], sc[:, :, NT - 1]).then_inc(s["tk_c"], 1)
            v.tensor_tensor(TB[:, :, 0:NT], sc[:, :, :], ge[:, :, :], ALU.subtract)
            v.tensor_copy(TB[:, :, NT:NT + 1], cst("batch").unsqueeze(1).to_broadcast([P, 2, 1]))
            dve.wait_ge(s["tk_mm"], 2)
            link(v.tensor_scalar(beg[:, :], bank[4][:, 0:2], 1.0, None, ALU.mult))
            v.tensor_tensor(fin[:, :], beg[:, :], tot[:, :], ALU.add)
            link(v.tensor_copy(TB[:, :, NT + 1], beg[:, :]))
            link(v.tensor_copy(mm2[:, :], TB[:, :, NT + 1]))
            link(v.tensor_tensor(TB[:, :, NT + 2], beg[:, :], mm2[:, :], ALU.subtract))
            for e in range(5):
                own = cst("owner")[:, e:e + 1]
                v.tensor_scalar(begM[:, e, :], beg[:, :], own, None, ALU.mult)
                last = v.tensor_scalar(finM[:, e, :], fin[:, :], own, None, ALU.mult)
            link(last)
            last = v.tensor_copy(mm2[:, :], beg[:, :])
            last.then_inc(s["tc"], 1)

            s["ohu"] = sem("slots_begun")
            s["row"] = sem("row_chain")

            def places(q, el, eh):
                side = eh
                after(dve, "smm", q * 9)
                v.tensor_scalar(ohu[:, :], iot[:, :], begM[:, bass.ds(el, 1), eh], None, ALU.is_ge)\
                    .then_inc(s["ohu"], 1)
                dve.wait_ge(s["ohu"], q + 1)
                v.scalar_tensor_tensor(out=oh[:, :], in0=iot[:, :], scalar=finM[:, bass.ds(el, 1), eh], in1=ohu[:, :],
                                       op0=ALU.is_lt, op1=ALU.mult).then_inc(s["ohd"], 1)
                for t, m in enumerate(SLOTS):
                    r0 = (q * 9 + t) * 3
                    dve.wait_ge(s["smm"], q * 9 + t + 1)
                    v.tensor_copy(SM[0:m, t, :], bank[7][0:m, NT:NT + 3]).then_inc(s["row"], 1)
                    dve.wait_ge(s["row"], r0 + 1)
                    v.scalar_tensor_tensor(out=rk[0:m, t:t + 1], in0=cst("slot")[0:m, t:t + 1], scalar=SM[0:m, t, 1:2],
                                           in1=SM[0:m, t, 2:3], op0=ALU.subtract, op1=ALU.subtract)\
                        .then_inc(s["row"], 1)
                    dve.wait_ge(s["row"], r0 + 2)
                    v.tensor_scalar(jk[0:m, :], bank[7][0:m, 0:NT], rk[0:m, t:t + 1], None, ALU.is_le, ALU.add,
                                    accum_out=pos[0:m, t:t + 1]).then_inc(s["smc"], 1)
                    dve.wait_ge(s["smc"], q * 9 + t + 1)
                    v.tensor_scalar(rowf[0:m, t:t + 1], SM[0:m, t, 0:1], float(NT), -1.0, ALU.mult, ALU.add)\
                        .then_inc(s["row"], 1)
                    dve.wait_ge(s["row"], r0 + 3)
                    if t == 0:
                        for r in range(3):
                            after(dve, f"scat{r}", (q - 1) * 16 * 3)
                    last = v.tensor_tensor(idx[side][0:m, t:t + 1], rowf[0:m, t:t + 1], pos[0:m, t:t + 1], ALU.add)
                last.then_inc(s["ixd"], 1)

            def expert(q, el, eh):
                def rest(c):
                    t0, t1 = CHUNKS[c]
                    for t in range(t0, t1):
                        m = SLOTS[t]
                        dve.wait_ge(s["om"], q * 9 + t + 1)
                        after(dve, "omul", q * 9 + t - 1)
                        v.tensor_tensor(ot[t % 2][0:m, :], bank[4 + t % 2][0:m, 0:D], b2b[eh][0:m, :], ALU.add)\
                            .then_inc(s["oadd"], 1)
                for c, (t0, t1) in enumerate(CHUNKS):
                    w = sum(SLOTS[t0:t1])
                    n0 = q * 3 + c
                    dve.wait_ge(s["yt_t"], n0 + 1)
                    after(dve, "hmm", n0 * 8)
                    for d in range(2):
                        last = v.tensor_scalar(yT[:, d, 0:w], bank[2 + d][:, 0:w], gam[:, d:d + 1], bet[:, d:d + 1],
                                               ALU.mult, ALU.add)
                    last.then_inc(s["yt"], 1)
                    rest(c)
                v.tensor_copy(mm2[:, :], beg[:, :]).then_inc(s["wfree"], 1)

            dve.wait_ge(s["ld_par"], 80)
            dve.wait_ge(s["zero"], 2)
            places(0, 0, 0)
            places(1, 0, 1)
            dve.wait_ge(s["wld0"], 48)
            expert(0, 0, 0)
            with dve.Fori(0, 3) as el:
                places(el * 2 + 2, el + 1, 0)
                dve.wait_ge(s["wld1"], (el + 1) * 48)
                expert(el * 2 + 1, el, 1)
                places(el * 2 + 3, el + 1, 1)
                dve.wait_ge(s["wld0"], (el + 2) * 48)
                expert(el * 2 + 2, el + 1, 0)
            dve.wait_ge(s["wld1"], 4 * 48)
            expert(NE - 1, 3, 1)


def constants():
    import numpy as np
    c = np.zeros((P, NCONST), np.float32)

    def put(name, a):
        c[:a.shape[0], CONST[name][0]:CONST[name][1]] = a
    put("ident", np.eye(P))
    haar, scale = np.zeros((P, P)), np.zeros(P)
    level = np.zeros(P, int)
    at = 0
    for lv, low in ((3, True), (3, False), (2, False), (1, False)):
        n = 1 << lv
        for y in range(P >> lv):
            haar[at, y * n:(y + 1) * n] = 1
            if not low:
                haar[at, y * n + n // 2:(y + 1) * n] = -1
            scale[at] = 1.0 / n
            level[at] = 0 if low else {3: 1, 2: 2, 1: 3}[lv]
            at += 1
    put("fwd", haar.T)
    put("inv", haar * scale[:, None])
    q = np.arange(P)
    own, img = q // NB, q % NB
    same = own[:, None] == own[None, :]
    put("same", same)
    put("before", same & (img[:, None] < img[None, :]))
    put("causal", np.where(q[None, :] <= q[:, None], 0.0, MASKED))
    put("sign", np.stack([1.0 - 2.0 * ((q >> (lv - 1)) & 1) for lv in (1, 2, 3)], 1))
    put("slot", q[:, None] + P * np.arange(9)[None, :])
    put("batch", img[:, None])
    m = np.arange(CG * NJ)
    put("diag", (m // NJ)[:, None] == np.arange(CG)[None, :])
    lvl = np.array([3] + [3] * 3 + [2] * 3 + [1] * 3)
    put("pick", ((m % NJ)[:, None] == np.arange(NJ)[None, :]) * (0.5 ** lvl)[None, :])
    spread = np.zeros((NJ, LEAF, P))
    first = {1: 1, 2: 4, 3: 7}
    for g in range(LEAF):
        for p in range(P):
            r = level[p]
            if r == 0 and g == 0:
                j = 0
            elif r == g:
                j = first[r] + 2
            elif r > g:
                j = first[r]
            else:
                j = first[g] + 1
            spread[j, g, p] = (1 / 8, 1 / 8, 1 / 4, 1 / 2)[g]
    put("spread", spread.reshape(NJ, LEAF * P))
    put("owner", own[:, None] == np.arange(5)[None, :])
    return c


def kernel(x, cls_tok, L0_tok_Wa, L0_tok_ba, L0_tok_Wd1, L0_tok_bd1, L0_tok_Wd2, L0_tok_bd2, L0_tok_Wd3, L0_tok_bd3,
           L0_attn_R, L0_ffn_gate_w, L0_ffn_ln_gamma, L0_ffn_ln_beta, L0_ffn_fc1s, L0_ffn_b1s, L0_ffn_fc2s, L0_ffn_b2s):
    import numpy as np
    import concourse.bacc as bacc
    from concourse.bass_utils import run_bass_kernel_spmd

    def lay(a, *shape):
        return np.ascontiguousarray(a).reshape(shape)
    arrays = {
        "x": lay(np.asarray(x).reshape(NB, NH, P, D).transpose(2, 0, 1, 3), P, NB * NH * D),
        "cls_tok": np.asarray(cls_tok),
        "Wa": np.asarray(L0_tok_Wa), "ba": np.asarray(L0_tok_ba),
        "Wd1": np.asarray(L0_tok_Wd1), "bd1": np.asarray(L0_tok_bd1),
        "Wd2": np.asarray(L0_tok_Wd2), "bd2": np.asarray(L0_tok_bd2),
        "Wd3": np.asarray(L0_tok_Wd3), "bd3": np.asarray(L0_tok_bd3),
        "R": np.asarray(L0_attn_R),
        "gate_w": np.asarray(L0_ffn_gate_w),
        "gate_wT": lay(np.asarray(L0_ffn_gate_w).T.reshape(2, P, NE).transpose(1, 0, 2), P, 2, NE),
        "gamma": lay(np.asarray(L0_ffn_ln_gamma).reshape(2, P).T, P, 2),
        "beta": lay(np.asarray(L0_ffn_ln_beta).reshape(2, P).T, P, 2),
        "fc1T": lay(np.asarray(L0_ffn_fc1s).transpose(0, 2, 1).reshape(NE, 2, P, NF).transpose(0, 2, 1, 3), NE, P, 2 * NF),
        "b1": lay(np.asarray(L0_ffn_b1s).reshape(NE, 8, P).transpose(2, 0, 1), P, NE, 8),
        "fc2T": lay(np.asarray(L0_ffn_fc2s).transpose(0, 2, 1).reshape(NE, 8, P, D).transpose(0, 2, 1, 3), NE, P, 8 * D),
        "b2": np.asarray(L0_ffn_b2s),
        "const": constants(),
    }
    arrays = {k: np.ascontiguousarray(a) for k, a in arrays.items()}
    nc = bacc.Bacc("TRN2", target_bir_lowering=False, num_devices=1)
    args = [nc.dram_tensor(f"in_{k}", a.shape, mybir.dt.from_np(a.dtype), kind="ExternalInput").ap()
            for k, a in arrays.items()]
    out = nc.dram_tensor("out_0", (NB, NT, D), F32, kind="ExternalOutput").ap()
    build_program(nc, *args, out)
    r = run_bass_kernel_spmd(nc, [{f"in_{k}": a for k, a in arrays.items()}], core_ids=[0])
    return r.results[0]["out_0"]
```

```python
from contextlib import ExitStack

import concourse.bass as bass
from concourse import mybir

ALU = mybir.AluOpType
ACT = mybir.ActivationFunctionType
AX_X = mybir.AxisListType.X
F32 = mybir.dt.float32
BF16 = mybir.dt.bfloat16
I32 = mybir.dt.int32

P = 128
NB = 32
NH = 2
D = 256
NT = 257
NE = 8
NF = 1024
KTOK = NB * NT // NE
NJ = 10
CG = 8
DG = D + NE
LEAF = 4
SLOTS = [P] * 8 + [KTOK - 8 * P]
CHUNKS = [(0, 3), (3, 6), (6, 9)]
EPS = 1e-5
MASKED = -1.0e9
BITS = 26

CONST = {}
_at = 0
for _name, _n in [("ident", P), ("fwd", P), ("inv", P), ("same", P), ("before", P), ("causal", P),
                  ("sign", 3), ("slot", 9), ("batch", 1), ("diag", CG), ("pick", NJ), ("spread", 4 * P),
                  ("owner", 5)]:
    CONST[_name] = (_at, _at + _n)
    _at += _n
NCONST = _at


def build_program(nc, x, cls_tok, Wa, ba, Wd1, bd1, Wd2, bd2, Wd3, bd3, R, gate_w, gate_wT, gamma, beta,
                  fc1T, b1, fc2T, b2, const, out, debug=None):
    ctx = ExitStack()
    with ctx:
        def sb(name, shape, dt=F32):
            return ctx.enter_context(nc.sbuf_tensor(name, shape, dt))

        def sem(name):
            return ctx.enter_context(nc.semaphore(name))

        rows = nc.dram_tensor("rows", [NB * NT, DG], F32).ap()
        out_rows = out.rearrange("b t d -> (b t) d")

        bank = [ctx.enter_context(nc.psum_tensor(f"bank{i}", [P, 512], F32)) for i in range(8)]
        Zb, Hb, Tb, Rb, Sb, Pb, Ab0, Ab1 = bank
        Ab = [Ab0, Ab1]

        C = sb("C", [P, NCONST])

        def cst(name):
            return C[:, CONST[name][0]:CONST[name][1]]
        ident = cst("ident")
        identb = sb("identb", [P, P], BF16)
        causalb = sb("causalb", [P, P], BF16)
        Rw = sb("Rw", [P, 2, D])
        gwT = sb("gwT", [P, 2, NE])
        gam = sb("gam", [P, 2])
        bet = sb("bet", [P, 2])
        b1s = sb("b1s", [P, NE, 8])
        bandb = sb("bandb", [NB, NJ])
        mhalf = sb("mhalf", [P, 6])
        BIG = sb("BIG", [P, NB * NH * D])
        XS = BIG[:, :].rearrange("p (b h c) -> p b h c", b=NB, h=NH)
        o = [0]

        def part(n):
            o[0] += n
            return BIG[:, o[0] - n:o[0]]
        w1s = [part(2 * NF).rearrange("p (c f) -> p c f", c=2) for _ in range(2)]
        w2s = [part(8 * D).rearrange("p (c d) -> p c d", c=8) for _ in range(2)]
        yg = [part(9 * DG).rearrange("p (t d) -> p t d", t=9) for _ in range(2)]
        assert o[0] <= NB * NH * D
        ARENA = sb("ARENA", [P, 10816])
        a = [0]

        def cut(n):
            a[0] += n
            assert a[0] <= 10816, a[0]
            return ARENA[:, a[0] - n:a[0]]
        WP = cut(NH * D * NJ).rearrange("p (h c j) -> p h c j", h=NH, c=D)
        bands = {lv: cut(NH * 3 * (D >> lv) * 3).rearrange("p (h k m) -> p h k m", h=NH, k=3) for lv in (1, 2, 3)}
        bsum = {lv: cut(NH * (D >> lv) * 3).rearrange("p (h m) -> p h m", h=NH) for lv in (1, 2, 3)}
        bandA = cut(NH * 32).rearrange("p (h m) -> p h m", h=NH)
        a[0] = 0
        Xc = [cut(NH * D).rearrange("p (h c) -> p h c", h=NH) for _ in range(2)]
        L1 = cut(NH * 128).rearrange("p (h c) -> p h c", h=NH)
        L2 = cut(NH * 64).rearrange("p (h c) -> p h c", h=NH)
        Zw = cut(NH * D).rearrange("p (h c) -> p h c", h=NH)
        I2 = cut(NH * 64).rearrange("p (h c) -> p h c", h=NH)
        I1 = cut(NH * 128).rearrange("p (h c) -> p h c", h=NH)
        Q = [cut(NH * D).rearrange("p (h c) -> p h c", h=NH) for _ in range(2)]
        Ex = [cut(NH * DG).rearrange("p (h c) -> p h c", h=NH) for _ in range(4)]
        ERT = [cut(2 * D).rearrange("p (c t) -> p c t", c=2) for _ in range(2)]
        Pr = [cut(388) for _ in range(2)]
        PTS = [cut(384) for _ in range(2)]
        U = [cut(NH * DG).rearrange("p (h c) -> p h c", h=NH) for _ in range(2)]
        ET = [sb(f"ET{i}", [P, 2, NT]) for i in range(2)]
        H1 = [sb(f"H1{i}", [P, NH, D]) for i in range(2)]
        Bs = [sb(f"Bs{i}", [P, NH, D]) for i in range(2)]
        Yp = [sb(f"Yp{i}", [P, NH, D]) for i in range(2)]
        bn0 = sb("bn0", [P, NH, 6])
        bn1 = sb("bn1", [P, NH, 6])
        ST = [sb(f"ST{i}", [P, 16]) for i in range(2)]
        A6 = sb("A6", [P, 6])
        N6 = [sb(f"N6{i}", [P, 6]) for i in range(2)]
        O1 = [sb(f"O1{i}", [P, 2]) for i in range(2)]
        hc = [sb(f"hc{i}", [P, NH, D]) for i in range(4)]
        nmx = [sb(f"nmx{i}", [P, 2]) for i in range(2)]
        rsm = [sb(f"rsm{i}", [P, 2]) for i in range(2)]
        W8 = sb("W8", [P, NB, 8])
        TUG = sb("TUG", [P, NB, NH, NE])
        TEG = sb("TEG", [P, NB, NH, NE])
        TST = sb("TST", [P, NB + 4, 16])
        LM = sb("LM", [CG * NJ, NB, CG])
        lgr = sb("lgr", [CG * NJ, NB])
        zz = sb("zz", [NB, NJ])
        z2 = sb("z2", [NB, NJ])
        bw = sb("bw", [NB, NJ])
        mx3 = sb("mx3", [NB, 3])
        bwT = sb("bwT", [NJ, NB])
        gwb = sb("gwb", [P, NE, D])
        clsb = sb("clsb", [P, D])
        CX = sb("CX", [P, DG])
        ch = sb("ch", [P, DG])
        cbs = sb("cbs", [P, D])
        cyp = sb("cyp", [P, D])
        junk = sb("junk", [P, D])
        cst8 = sb("cst8", [P, 24])
        cbn = sb("cbn", [P, 6])
        cpw = sb("cpw", [P, 4])
        sg = sb("sg", [P, NE])
        cgl = sb("cgl", [P, NE])
        vcls = sb("vcls", [P, NE])
        GL = sb("GL", [P, NB, NH, NE])
        GM = sb("GM", [P, NB, NH, NE])
        sd0 = sb("sd0", [P, NB, NH])
        dm = sb("dm", [P, NB, NH])
        GV = sb("GV", [P, NH, 2, 4, NB])
        V = sb("V", [P, 2, NT])
        ge = sb("ge", [P, 2, NT])
        eq = sb("eq", [P, 2, NT])
        sc = sb("sc", [P, 2, NT])
        one = sb("one", [P, NT])
        Tv = sb("Tv", [P, 2])
        Tc = sb("Tc", [P, 2])
        bit = sb("bit", [P, 2])
        cnt = sb("cnt", [P, 2])
        mm2 = sb("mm2", [P, 2])
        cgt = sb("cgt", [P, 2])
        need = sb("need", [P, 2])
        tot = sb("tot", [P, 2])
        beg = sb("beg", [P, 2])
        fin = sb("fin", [P, 2])
        begM = sb("begM", [P, 5, 2])
        finM = sb("finM", [P, 5, 2])
        TB = sb("TB", [P, 2, NT + 3], BF16)
        iot = sb("iot", [P, KTOK])
        ohu = sb("ohu", [P, KTOK], BF16)
        oh = sb("oh", [P, KTOK], BF16)
        SM = sb("SM", [P, 9, 3])
        rk = sb("rk", [P, 9])
        pos = sb("pos", [P, 9])
        jk = sb("jk", [P, NT], BF16)
        rowf = sb("rowf", [P, 9])
        idx = [sb(f"idx{i}", [P, 9], I32) for i in range(2)]
        sidx = [sb(f"sidx{i}", [P, 9], I32) for i in range(2)]
        yT = sb("yT", [P, 2, 384])
        hT = [ARENA[:, i * 3072:(i + 1) * 3072].rearrange("p (f t) -> p f t", f=8) for i in range(2)]
        ob = [ARENA[:, 6144 + i * D:6144 + (i + 1) * D] for i in range(3)]
        b2b = [sb(f"b2b{i}", [P, D]) for i in range(2)]
        ot = [sb(f"ot{i}", [P, D]) for i in range(2)]

        names = """ld_const ld_x0 ld_x1 ld_par ld_band ld_band2 ld_band3 cvt wp wp_part lg_mm lg_m lg_r z_mm z_c z_e bw_t bw_c w8_mm w8
            cls_d cls_p cls_a cls_t et0 cls_st cls_g zero
            xc xc_l z_done zw inv q h0 st0_b st0 var pow nrm hcE et et_ev er er_ev eg eg_ev sm nmax pexp pt pt_ev av u h1 rv
            st1_b st1 tug base yp tab base_st0 base_st1 yp_st0 yp_st1
            gt_c gt_t gt_v vt_st vsp_t vsp thr tc cn tk_c tk_mm
            ohd smm smc ixc ixd wld0 wld1 gat00 gat01 gat02 gat10 gat11 gat12 yt_t yt hmm hact om oadd omul scat0 scat1 scat2 idc""".split()
        s = {n: sem(n) for n in names}

        def after(eng, name, count):
            if not isinstance(count, int) or count > 0:
                eng.wait_ge(s[name], count)

        def apart(eng):
            eng.nop(nofuse=True)

        LAG = 4
        UNROLL = 4

        class Step:
            def __init__(self, i, k):
                self.n, self.p, self.r = i * UNROLL + k, k % 2, k % 4
                self.h = i * (UNROLL // 2) + k // 2

        HEAD, TAIL = 4, 28

        def steps(eng, emit):
            def images(i, k, bounded):
                return [Step(i, k)] + [Step(i, k + d) if not bounded or 0 <= k + d < NB else None
                                       for d in range(1, -LAG - 1, -1)]
            for k in range(HEAD):
                emit(*images(0, k, True))
            with eng.Fori(HEAD // UNROLL, TAIL // UNROLL) as i:
                for k in range(UNROLL):
                    emit(*images(i, k, False))
            for k in range(TAIL, NB + LAG):
                emit(*images(0, k, True))

        class Job:
            def __init__(self, el, k):
                self.el, self.eh, self.c = el + k // 6, k // 3 % 2, k % 3
                self.q, self.j, self.p = self.el * 2 + self.eh, el * 6 + k, k % 2
                self.e = self.el + 4 * self.eh
                self.t0, self.t1 = CHUNKS[self.c]
                self.w = sum(SLOTS[self.t0:self.t1])

        def jobs(eng, emit):
            def one(el, k):
                if isinstance(el, int) and el == 0 and k < 3:
                    tiles = [[(3, t) for t in range(9)], [(6, t) for t in range(5)], [(6, t) for t in range(5, 9)]][k]
                else:
                    far = k // 3 * 3 + 6
                    tiles = [(far, t) for t in range(*CHUNKS[k % 3])]
                last = isinstance(el, int) and el == 3
                emit(Job(el, k - 1) if k or not isinstance(el, int) or el else None, Job(el, k),
                     Job(el, k + 1) if not last or k < 5 else None,
                     [(Job(el, f), t) for f, t in tiles if not last])
            for k in range(6):
                one(0, k)
            with eng.Fori(1, 3) as el:
                for k in range(6):
                    one(el, k)
            for k in range(6):
                one(3, k)
            emit(Job(3, 5), None, None, [])

        block = ctx.enter_context(nc.Block())

        @block.sync
        def _(sp):
            sp.dma_start(C[:, :], const).then_inc(s["ld_const"], 16)
            sp.dma_start(BIG[:, 0:16 * 512], x[:, 0:16 * 512]).then_inc(s["ld_x0"], 16)
            sp.dma_start(BIG[:, 16 * 512:], x[:, 16 * 512:]).then_inc(s["ld_x1"], 16)
            sp.dma_start(Rw[:, :, :], R.rearrange("(c p) e -> p c e", p=P)).then_inc(s["ld_par"], 16)
            sp.dma_start(gwT[:, :, :], gate_wT).then_inc(s["ld_par"], 16)
            sp.dma_start(gam[:, :], gamma).then_inc(s["ld_par"], 16)
            sp.dma_start(bet[:, :], beta).then_inc(s["ld_par"], 16)
            sp.dma_start(b1s[:, :, :], b1).then_inc(s["ld_par"], 16)
            after(sp, "cls_g", 1)
            cls_out = out.rearrange("b t d -> b (t d)")[:, 0:D]
            cls_rows = rows.rearrange("(b t) d -> b (t d)", b=NB)
            sp.dma_start(cls_out, cbs[0:NB, :]).then_inc(s["cls_st"], 16)
            sp.dma_start(cls_rows[:, 0:D], cyp[0:NB, :]).then_inc(s["cls_st"], 16)
            sp.dma_start(cls_rows[:, D:DG], vcls[0:NB, :]).then_inc(s["cls_st"], 16)

            out_img = out.rearrange("b t d -> b (t d)")
            rows_img = rows.rearrange("(b t) d -> b (t d)", b=NB)

            def emit(_t, _nxt, _a, _b, _c, _d, m):
                if m:
                    dst = out_img[bass.ds(m.n, 1), D:].rearrange("b (h p d) -> p (b h) d", h=NH, p=P)
                    sp.wait_ge(s["base"], m.n + 1)
                    sp.dma_start(dst, Bs[m.p][:, :, :]).then_inc(s[f"base_st{m.p}"], 16)
                    dst = rows_img[bass.ds(m.n, 1), DG:].rearrange("b (h p d) -> p (b h) d", h=NH, p=P)[:, :, 0:D]
                    sp.wait_ge(s["yp"], m.n + 1)
                    sp.dma_start(dst, Yp[m.p][:, :, :]).then_inc(s[f"yp_st{m.p}"], 16)
            steps(sp, emit)
            vt = rows_img[:, DG:].rearrange("b (h p e) -> p b h e", h=NH, p=P)[:, :, :, D:DG]
            sp.wait_ge(s["gt_v"], 2)
            for h in range(NH):
                sp.dma_start(vt[:, :, h, :], GL[:, :, h, :]).then_inc(s["vt_st"], 16)

            def weights(el, eh, used):
                after(sp, "oadd", used)
                e = el + 4 * eh
                sp.dma_start(w1s[eh][:, :, :], fc1T[bass.ds(e, 1), :, :].rearrange("e p (c f) -> p (e c) f", c=2))\
                    .then_inc(s[f"wld{eh}"], 16)
                sp.dma_start(w2s[eh][:, :, :], fc2T[bass.ds(e, 1), :, :].rearrange("e p (c d) -> p (e c) d", c=8))\
                    .then_inc(s[f"wld{eh}"], 16)
                sp.dma_start(b2b[eh][:, :], b2[bass.ds(e, 1), :].partition_broadcast(P).rearrange("p e d -> p (e d)"))\
                    .then_inc(s[f"wld{eh}"], 16)
            sp.wait_ge(s["xc"], NB)
            weights(0, 0, 0)
            weights(0, 1, 0)
            with sp.Fori(1, 4) as el:
                weights(el, 0, (el * 2 - 1) * 9)
                weights(el, 1, el * 2 * 9)
            for r in range(3):
                sp.wait_ge(s[f"scat{r}"], 16 * 3 * NE)

        @block.gpsimd
        def _(po):
            g = nc.gpsimd
            g.memset(mhalf[:, :], -0.5).then_inc(s["zero"], 1)
            g.iota(iot[:, :], [[1, KTOK]], base=0, channel_multiplier=0, allow_small_or_imprecise_dtypes=True)\
                .then_inc(s["zero"], 1)
            po.wait_ge(s["cls_d"], 1)
            po.wait_ge(s["zero"], 1)
            g.tensor_tensor(cst8[:, 3:4], cst8[:, 2:3], mhalf[:, 0:1], ALU.pow).then_inc(s["cls_p"], 1)
            po.wait_ge(s["cls_d"], 2)
            g.tensor_tensor(cpw[:, 2:4], cpw[:, 0:2], mhalf[:, 0:2], ALU.pow).then_inc(s["cls_p"], 1)

            def columns(m):
                after(po, "xc", m.n)
                after(po, "z_done", m.n - 1)
                xv = XS[:, bass.ds(m.n, 1), :, :].rearrange("p b h c -> p (b h) c") if not isinstance(m.n, int) \
                    else XS[:, m.n, :, :]
                x0, x1 = xv[:, :, 0::2], xv[:, :, 1::2]
                dst = Xc[m.p]
                g.tensor_tensor(L1[:, :, :], x0, x1, ALU.add).then_inc(s["xc_l"], 1)
                g.tensor_tensor(dst[:, :, 128:256], x0, x1, ALU.subtract)
                po.wait_ge(s["xc_l"], m.n * 2 + 1)
                g.tensor_tensor(L2[:, :, :], L1[:, :, 0::2], L1[:, :, 1::2], ALU.add).then_inc(s["xc_l"], 1)
                g.tensor_tensor(dst[:, :, 64:128], L1[:, :, 0::2], L1[:, :, 1::2], ALU.subtract)
                po.wait_ge(s["xc_l"], m.n * 2 + 2)
                g.tensor_tensor(dst[:, :, 0:32], L2[:, :, 0::2], L2[:, :, 1::2], ALU.add)
                g.tensor_tensor(dst[:, :, 32:64], L2[:, :, 0::2], L2[:, :, 1::2], ALU.subtract).then_inc(s["xc"], 1)

            def emit(t, nxt, _a, b, _c, _d, m):
                if b:
                    after(po, "hcE", b.n - 1)
                po.wait_ge(s["var"], t.n + 1)
                g.tensor_tensor(ST[t.p][:, 8:14], A6[:, :], mhalf[:, :], ALU.pow).then_inc(s["pow"], 1)
                if nxt:
                    columns(nxt)
                po.wait_ge(s["pow"], t.n + 1)
                g.tensor_copy(TST[:, bass.ds(t.n, 1), :].rearrange("p b k -> p (b k)"), ST[t.p][:, :])\
                    .then_inc(s["tab"], 1)
            po.wait_ge(s["wp"], 1)
            po.wait_ge(s["lg_mm"], 1)
            po.wait_ge(s["ld_x0"], 16)
            po.wait_ge(s["ld_x1"], 16)
            columns(Step(0, 0))
            steps(po, emit)

            tok = bass.IndirectOffsetOnAxis

            def gather(job):
                eh = job.eh
                for t, m in enumerate(SLOTS):
                    po.wait_ge(s["ixd"], job.q * 9 + t + 1)
                    apart(po)
                    g.indirect_dma_start(out=yg[eh][0:m, t, :], out_offset=None, in_=rows,
                                         in_offset=tok(ap=idx[eh][0:m, t:t + 1], axis=0))\
                        .then_inc(s[f"gat{eh}{t // 3}"], 16)
                if not isinstance(job.q, int) or job.q > 1:
                    for r in range(3):
                        po.wait_ge(s[f"scat{r}"], (job.q - 1) * 48)
                apart(po)
                g.tensor_copy(sidx[eh][:, 0:8], idx[eh][:, 0:8])
                g.tensor_copy(sidx[eh][0:SLOTS[8], 8:9], idx[eh][0:SLOTS[8], 8:9]).then_inc(s["idc"], 1)

            def scatter(job):
                for t in range(job.t0, job.t1):
                    m = SLOTS[t]
                    po.wait_ge(s["omul"], job.q * 9 + t + 1)
                    if t == 0:
                        po.wait_ge(s["idc"], job.q + 1)
                        for r in range(3):
                            after(po, f"scat{r}", job.q * 48)
                    apart(po)
                    g.indirect_dma_start(out=out_rows, out_offset=tok(ap=sidx[job.eh][0:m, t:t + 1], axis=0),
                                         in_=ob[t % 3][0:m, :], in_offset=None, compute_op=ALU.add)\
                        .then_inc(s[f"scat{t % 3}"], 16)
            po.wait_ge(s["cls_st"], 48)
            for q in range(2):
                po.wait_ge(s[f"base_st{q}"], 16 * NB // 2)
                po.wait_ge(s[f"yp_st{q}"], 16 * NB // 2)
            po.wait_ge(s["vt_st"], 32)
            gather(Job(0, 0))

            def emit(prev, cur, nxt, _tiles):
                if prev:
                    scatter(prev)
                if cur and cur.c == 0 and (nxt and not (isinstance(cur.el, int) and cur.el == 3 and cur.eh)):
                    gather(Job(cur.el, cur.eh * 3 + 3))
            jobs(po, emit)

        @block.scalar
        def _(act):
            n = 0
            for lv, W in ((1, Wd3), (2, Wd2), (3, Wd1)):
                rows = D >> lv
                src = W.rearrange("(k y x) j -> y k (x j)", k=3, y=rows)
                for h in range(NH):
                    for r in range(1 << lv):
                        act.dma_start(bands[lv][r::1 << lv, h, :, :], src[h * rows // 2:(h + 1) * rows // 2, :, :])\
                            .then_inc(s["ld_band"], 16)
                        n += 1
            srcA = Wa.rearrange("(y x) j -> y (x j)", y=32)
            for h in range(NH):
                for r in range(8):
                    act.dma_start(bandA[r::8, h, :], srcA[h * 16:(h + 1) * 16, :]).then_inc(s["ld_band"], 16)
                    n += 1
            assert n == 44
            act.dma_start(bandb[:, 0:1], ba.unsqueeze(0).partition_broadcast(NB).rearrange("p a b -> p (a b)")).then_inc(s["ld_band2"], 16)
            for q, b in ((1, bd1), (4, bd2), (7, bd3)):
                act.dma_start(bandb[:, q:q + 3], b.unsqueeze(0).partition_broadcast(NB).rearrange("p a b -> p (a b)")).then_inc(s["ld_band2"], 16)
            act.dma_start(clsb[:, :], cls_tok.rearrange("a b d -> (a b) d").partition_broadcast(P).rearrange("p a d -> p (a d)")).then_inc(s["ld_band3"], 16)
            act.dma_start(gwb[:, :, :], gate_w.unsqueeze(0).partition_broadcast(P).rearrange("p a e d -> p (a e) d")).then_inc(s["ld_band3"], 16)
            A = nc.scalar
            act.wait_ge(s["cls_d"], 3)
            A.activation(cgl[:, :], cgl[:, :], ACT.Tanh).then_inc(s["cls_a"], 1)
            act.wait_ge(s["z_c"], 3)
            A.activation(z2[:, 1:NJ], z2[:, 1:NJ], ACT.Exp)
            A.activation(z2[:, 0:1], zz[:, 0:1], ACT.Exp, scale=-1.0).then_inc(s["z_e"], 1)

            def emit(t, _nxt, _a, b, c, d, m):
                if d:
                    after(act, "pt", d.n - 1)
                    after(act, "u", d.n - 1)
                    after(act, "rv", d.n - 1)
                    act.wait_ge(s["nmax"], d.n + 1)
                    A.activation(Pr[d.p][:, 0:129], Sb[:, 0:129], ACT.Exp, bias=nmx[d.p][:, 0:1],
                                 accum_out=rsm[d.p][:, 0:1])
                    A.activation(Pr[d.p][:, 129:386], Sb[:, 129:386], ACT.Exp, bias=nmx[d.p][:, 1:2],
                                 accum_out=rsm[d.p][:, 1:2]).then_inc(s["pexp"], 1)
                if c:
                    after(act, "sm", c.n - 1)
                    act.wait_ge(s["et"], c.n + 1)
                    A.activation(ET[c.p][:, :, 1:NT], Tb[:, :].rearrange("p (c t) -> p c t", c=2), ACT.Copy)\
                        .then_inc(s["et_ev"], 1)
                if d:
                    after(act, "av", d.n - 1)
                    act.wait_ge(s["pt"], d.n + 1)
                    A.activation(PTS[d.p][:, :], Pb[:, 0:384], ACT.Copy).then_inc(s["pt_ev"], 1)
                if b:
                    after(act, "h1", b.n - 3)
                    act.wait_ge(s["st0_b"], b.n + 1)
                    A.activation(hc[b.r][:, :, :], Hb[:, :].rearrange("p (h c) -> p h c", h=NH), ACT.Copy)
                if c:
                    act.wait_ge(s["er"], c.n + 1)
                    A.activation(ERT[c.p][:, :, :], Rb[:, :].rearrange("p (c t) -> p c t", c=2), ACT.Copy)\
                        .then_inc(s["er_ev"], 1)
                if b:
                    after(act, "av", b.n - 3)
                    act.wait_ge(s["nrm"], t.n + 1)
                    for h in range(NH):
                        last = A.activation(Ex[b.r][:, h, 0:D], Hb[:, h * D:(h + 1) * D], ACT.Identity,
                                            bias=N6[t.p][:, h:h + 1], scale=ST[t.p][:, 8 + h:9 + h])
                    last.then_inc(s["hcE"], 1)
                if m:
                    after(act, f"yp_st{m.p}", m.h * 16)
                    act.wait_ge(s["nrm"], t.n + 1)
                    for h in range(NH):
                        last = A.activation(Yp[m.p][:, h, :], H1[m.p][:, h, :], ACT.Identity,
                                            bias=N6[t.p][:, 4 + h:5 + h], scale=ST[t.p][:, 12 + h:13 + h])
                    last.then_inc(s["yp"], 1)
            steps(act, emit)
            act.wait_ge(s["gt_c"], 6)
            A.activation(GM[:, :, :, :], GL[:, :, :, :], ACT.Tanh).then_inc(s["gt_t"], 1)

            def emit(prev, cur, _nxt, _tiles):
                if cur:
                    for f in range(8):
                        act.wait_ge(s["hmm"], cur.j * 8 + f + 1)
                        apart(act)
                        A.activation(hT[cur.p][:, f, 0:cur.w], bank[f % 2][:, 0:cur.w], ACT.Gelu_apprx_tanh,
                                     bias=b1s[:, bass.ds(cur.e, 1), f]).then_inc(s["hact"], 1)
                if prev:
                    for t in range(prev.t0, prev.t1):
                        m = SLOTS[t]
                        act.wait_ge(s["oadd"], prev.q * 9 + t + 1)
                        after(act, f"scat{t % 3}", (prev.q * 3 + t // 3) * 16)
                        apart(act)
                        A.activation(ob[t % 3][0:m, :], ot[t % 2][0:m, :], ACT.Copy,
                                     scale=yg[prev.eh][0:m, t, bass.ds(prev.e + D, 1)]).then_inc(s["omul"], 1)
            act.wait_ge(s["ld_par"], 80)
            jobs(act, emit)

        @block.tensor
        def _(pe):
            T = nc.tensor
            pe.wait_ge(s["ld_const"], 16)
            pe.wait_ge(s["cls_t"], 1)
            for c in range(2):
                last = T.transpose(Tb[:, c * P:(c + 1) * P], CX[:, c * P:(c + 1) * P], ident)
            last.then_inc(s["et0"], 1)
            pe.wait_ge(s["wp"], 1)
            for part_, load in ((0, "ld_x0"), (1, "ld_x1")):
                pe.wait_ge(s[load], 16)
                for h in range(NH):
                    for c in range(D // CG):
                        first, final = h == 0 and c == 0, h == NH - 1 and c == D // CG - 1
                        last = T.matmul(Zb[0:CG * NJ, part_ * 128:(part_ + 1) * 128],
                                        WP[:, h, c * CG:(c + 1) * CG, :].rearrange("p c j -> p (c j)"),
                                        XS[:, part_ * 16:(part_ + 1) * 16, h, c * CG:(c + 1) * CG],
                                        start=first, stop=final)
            last.then_inc(s["lg_mm"], 1)
            pe.wait_ge(s["lg_r"], 1)
            T.matmul(Hb[0:NB, 0:NJ], lgr[:, :], cst("pick")[0:CG * NJ, :], start=True, stop=True).then_inc(s["z_mm"], 1)
            pe.wait_ge(s["bw_t"], 1)
            T.transpose(Hb[0:NJ, 32:32 + NB], bw[:, :], ident[0:NB, 0:NB]).then_inc(s["z_mm"], 1)
            pe.wait_ge(s["bw_c"], 1)
            for q in range(LEAF):
                last = T.matmul(Hb[:, 128 + q * NB:128 + (q + 1) * NB], cst("spread")[0:NJ, q * P:(q + 1) * P],
                                bwT[:, :], start=True, stop=True)
            last.then_inc(s["w8_mm"], 1)
            pe.wait_ge(s["cvt"], 1)
            pe.wait_ge(s["ld_par"], 80)
            pe.wait_ge(s["w8"], 1)

            def emit(_t, _nxt, a, b, c, d, _m):
                if b:
                    after(pe, "hcE", b.n)
                    pe.wait_ge(s["q"], b.n + 1)
                    T.matmul(Hb[:, :], cst("inv"), Q[b.p].rearrange("p h c -> p (h c)"), start=True, stop=True)\
                        .then_inc(s["h0"], 1)
                if c:
                    after(pe, "et_ev", c.n)
                    pe.wait_ge(s["hcE"], c.n + 1)
                    for j in range(2):
                        for h in range(NH):
                            last = T.transpose(Tb[:, j * D + h * P:j * D + (h + 1) * P],
                                               Ex[c.r][:, h, j * P:(j + 1) * P], ident)
                    last.then_inc(s["et"], 1)
                if d:
                    after(pe, "pt_ev", d.n)
                    pe.wait_ge(s["eg_ev"], d.n + 1)
                    pe.wait_ge(s["pexp"], d.n + 1)
                    for q, c0 in enumerate((1, 130, 258)):
                        last = T.transpose(Pb[:, q * P:(q + 1) * P], Pr[d.p][:, c0:c0 + P], ident)
                    last.then_inc(s["pt"], 1)
                if a:
                    after(pe, "zw", a.n)
                    pe.wait_ge(s["xc"], a.n + 1)
                    T.matmul(Zb[:, :], cst("fwd"), Xc[a.p].rearrange("p h c -> p (h c)"), start=True, stop=True)\
                        .then_inc(s["z_done"], 1)
                if c:
                    after(pe, "er_ev", c.n)
                    pe.wait_ge(s["et_ev"], c.n + 1)
                    for e in range(2):
                        for j in range(2):
                            last = T.matmul(Rb[:, e * D:(e + 1) * D], Rw[:, j, e * P:(e + 1) * P],
                                            ET[c.p][:, j, 1:NT], start=(j == 0), stop=(j == 1))
                    last.then_inc(s["er"], 1)
                if d:
                    after(pe, "u", d.n)
                    pe.wait_ge(s["pt_ev"], d.n + 1)
                    T.matmul(Ab[0][:, 0:DG], PTS[d.p][:, 0:P], Ex[d.r][:, 0, :], start=True, stop=True)
                    T.matmul(Ab[1][:, 0:DG], PTS[d.p][:, P:2 * P], Ex[d.r][:, 0, :], start=True, stop=False)
                    T.matmul(Ab[1][:, 0:DG], PTS[d.p][:, 2 * P:3 * P], Ex[d.r][:, 1, :], start=False, stop=True)\
                        .then_inc(s["av"], 1)
                if c:
                    for h in range(NH):
                        for j in range(2):
                            last = T.matmul(Pb[:, 400 + h * NE:400 + (h + 1) * NE],
                                            ET[c.p][:, j, 1 + h * P:1 + (h + 1) * P], gwT[:, j, :],
                                            start=(j == 0), stop=(j == 1))
                    last.then_inc(s["eg"], 1)
                    after(pe, "pexp", c.n)
                    pe.wait_ge(s["er_ev"], c.n + 1)
                    for h, (c0, w) in enumerate(((0, 129), (129, 257))):
                        for j in range(2):
                            T.matmul(Sb[:, c0:c0 + w], ERT[c.p][:, j, h * P:(h + 1) * P], ET[c.p][:, j, 0:w],
                                     start=(j == 0), stop=False)
                        last = T.matmul(Sb[:, c0 + w - P:c0 + w], identb[:, :], causalb[:, :], start=False, stop=True)
                    last.then_inc(s["sm"], 1)
            steps(pe, emit)

            pe.wait_ge(s["vsp_t"], 1)
            for h in range(NH):
                for eh in range(2):
                    q = 2 * h + eh
                    last = T.transpose(bank[0][:, q * P:(q + 1) * P],
                                       GV[:, h, eh, :, :].rearrange("p e b -> p (e b)"), ident)
            last.then_inc(s["vsp"], 1)
            with pe.Fori(0, BITS) as i:
                pe.wait_ge(s["cn"], i + 1)
                T.matmul(bank[1][:, 0:2], cst("same"), cnt[:, :], start=True, stop=True).then_inc(s["thr"], 1)
            pe.wait_ge(s["tk_c"], 1)
            T.matmul(bank[2][:, 0:2], cst("same"), cgt[:, :], start=True, stop=True)
            T.matmul(bank[3][:, 0:2], cst("before"), tot[:, :], start=True, stop=True).then_inc(s["tk_mm"], 1)
            pe.wait_ge(s["tk_c"], 2)
            T.matmul(bank[4][:, 0:2], cst("before"), tot[:, :], start=True, stop=True).then_inc(s["tk_mm"], 1)

            def place(job, t):
                n, m = job.q * 9 + t, SLOTS[t]
                if t == 0:
                    pe.wait_ge(s["ohd"], job.q + 1)
                after(pe, "smc", n - (t > 0))
                T.matmul(bank[6 + t % 2][0:m, 0:NT + 3], oh[:, t * P:t * P + m], TB[:, job.eh, :], start=True,
                         stop=True).then_inc(s["smm"], 1)

            def turn(job):
                after(pe, "yt", job.j)
                pe.wait_ge(s[f"gat{job.eh}{job.c}"], 48 * (job.el + 1))
                for d in range(2):
                    for t in range(job.t0, job.t1):
                        m, at = SLOTS[t], (t - job.t0) * P
                        last = T.transpose(bank[2 + d][:, at:at + m], yg[job.eh][0:m, t, d * P:(d + 1) * P],
                                           ident[0:m, 0:m])
                last.then_inc(s["yt_t"], 1)

            def emit(prev, cur, nxt, tiles):
                if cur:
                    pe.wait_ge(s[f"wld{cur.eh}"], 48 * (cur.el + 1))
                    pe.wait_ge(s["yt"], cur.j + 1)
                    for f in range(8):
                        after(pe, "hact", cur.j * 8 + f - 1)
                        for d in range(2):
                            last = T.matmul(bank[f % 2][:, 0:cur.w], w1s[cur.eh][:, d, f * P:(f + 1) * P],
                                            yT[:, d, 0:cur.w], start=(d == 0), stop=(d == 1))
                        last.then_inc(s["hmm"], 1)
                        for i, (job, t) in enumerate(tiles):
                            if (i + 1) * 8 // (len(tiles) + 1) == f:
                                place(job, t)
                if nxt:
                    turn(nxt)
                if prev:
                    pe.wait_ge(s["hact"], (prev.j + 1) * 8)
                    for t in range(prev.t0, prev.t1):
                        m, at = SLOTS[t], (t - prev.t0) * P
                        after(pe, "oadd", prev.q * 9 + t - 1)
                        for f in range(8):
                            last = T.matmul(bank[4 + t % 2][0:m, 0:D], hT[prev.p][:, f, at:at + m],
                                            w2s[prev.eh][:, f, :], start=(f == 0), stop=(f == 7))
                        last.then_inc(s["om"], 1)
            pe.wait_ge(s["tc"], 1)
            for t in range(9):
                place(Job(0, 0), t)
            turn(Job(0, 0))
            jobs(pe, emit)

        @block.vector
        def _(dve):
            v = nc.vector
            dve.wait_ge(s["ld_const"], 16)
            v.tensor_copy(identb[:, :], ident)
            v.tensor_copy(causalb[:, :], cst("causal")).then_inc(s["cvt"], 1)
            dve.wait_ge(s["ld_band3"], 32)
            k = [0]

            def link(ins):
                k[0] += 1
                ins.then_inc(s["cls_t2"], 1)
                dve.wait_ge(s["cls_t2"], k[0])
            s["cls_t2"] = sem("cls_chain")
            link(v.bn_stats(cbn[:, :], clsb[:, :]))
            link(v.bn_aggr(cst8[:, 0:2], cbn[:, :]))
            v.tensor_scalar(cst8[:, 2:3], cst8[:, 1:2], EPS, None, ALU.add).then_inc(s["cls_d"], 1)
            v.tensor_reduce(sg[:, :], gwb[:, :, :], AX_X, ALU.add)
            dve.wait_ge(s["cls_p"], 1)
            link(v.tensor_scalar(CX[:, 0:D], clsb[:, :], cst8[:, 0:1], cst8[:, 3:4], ALU.subtract, ALU.mult))
            for e in range(NE):
                last = v.tensor_tensor_reduce(out=junk[:, :], in0=CX[:, 0:D], in1=gwb[:, e, :], scale=1.0, scalar=0.0,
                                              op0=ALU.mult, op1=ALU.add, accum_out=CX[:, D + e:D + e + 1])
                last = link(last)
            link(v.tensor_tensor(ch[:, 0:D], clsb[:, :], CX[:, 0:D], ALU.add))
            v.tensor_copy(junk[:, 0:1], CX[:, 0:1]).then_inc(s["cls_t"], 1)
            link(v.bn_stats(cbn[:, :], ch[:, 0:D]))
            for e in range(NE):
                link(v.tensor_tensor_reduce(out=junk[:, :], in0=ch[:, 0:D], in1=gwb[:, e, :], scale=1.0, scalar=0.0,
                                            op0=ALU.mult, op1=ALU.add, accum_out=ch[:, D + e:D + e + 1]))
            link(v.bn_aggr(cst8[:, 4:6], cbn[:, :]))
            v.tensor_scalar(cpw[:, 0:1], cst8[:, 5:6], EPS, None, ALU.add)
            v.tensor_scalar(cpw[:, 1:2], cst8[:, 5:6], 1.0 + EPS, EPS * EPS, ALU.mult, ALU.add).then_inc(s["cls_d"], 1)
            dve.wait_ge(s["cls_p"], 2)
            link(v.tensor_scalar(cyp[:, :], ch[:, 0:D], cst8[:, 4:5], cpw[:, 2:3], ALU.subtract, ALU.mult))
            v.tensor_tensor(cbs[:, :], cyp[:, :], ch[:, 0:D], ALU.add)
            link(v.tensor_scalar(cgl[:, :], sg[:, :], cst8[:, 4:5], None, ALU.mult))
            link(v.tensor_tensor(cgl[:, :], ch[:, D:DG], cgl[:, :], ALU.subtract))
            link(v.tensor_scalar(cgl[:, :], cgl[:, :], cpw[:, 2:3], None, ALU.mult))
            v.tensor_scalar(cyp[:, :], ch[:, 0:D], cst8[:, 4:5], cpw[:, 3:4], ALU.subtract, ALU.mult)\
                .then_inc(s["cls_d"], 1)
            dve.wait_ge(s["cls_a"], 1)
            v.tensor_scalar(vcls[:, :], cgl[:, :], 1.0, 0.5, ALU.add, ALU.mult).then_inc(s["cls_g"], 1)
            dve.wait_ge(s["et0"], 1)
            for q in range(2):
                last = v.tensor_copy(ET[q][:, :, 0], Tb[:, 0:D].rearrange("p (c t) -> p c t", c=2)[:, :, 0])
            link(last)

            dve.wait_ge(s["ld_band"], 16 * 44)
            for h in range(NH):
                for lv in (1, 2, 3):
                    sign = cst("sign")[:, lv - 1:lv]
                    last = v.scalar_tensor_tensor(out=bsum[lv][:, h, :], in0=bands[lv][:, h, 2, :], scalar=sign,
                                                  in1=bands[lv][:, h, 1, :], op0=ALU.mult, op1=ALU.add)
            last.then_inc(s["wp_part"], 1)
            dve.wait_ge(s["wp_part"], 1)
            for h in range(NH):
                for lv in (1, 2, 3):
                    sign = cst("sign")[:, lv - 1:lv]
                    j0 = 1 + 3 * (3 - lv)
                    n = D >> lv
                    dst = WP[:, h, :, j0:j0 + 3].rearrange("p (x s u) j -> p x s u j", x=n, s=2)
                    for q, op in ((0, ALU.add), (1, ALU.subtract)):
                        for u in range(1 << (lv - 1)):
                            v.scalar_tensor_tensor(out=dst[:, :, q, u, :],
                                                   in0=bands[lv][:, h, 0, :].rearrange("p (x j) -> p x j", j=3),
                                                   scalar=sign,
                                                   in1=bsum[lv][:, h, :].rearrange("p (x j) -> p x j", j=3),
                                                   op0=ALU.mult, op1=op)
                last = v.tensor_copy(WP[:, h, :, 0:1].rearrange("p (x u) j -> p x (u j)", u=8),
                                     bandA[:, h, :].unsqueeze(2).to_broadcast([P, 32, 8]))
            last.then_inc(s["wp"], 1)
            dve.wait_ge(s["lg_mm"], 1)
            v.tensor_tensor(LM[:, :, :], Zb[0:CG * NJ, 0:NB * CG].rearrange("p (b c) -> p b c", c=CG),
                            cst("diag")[0:CG * NJ, :].unsqueeze(1).to_broadcast([CG * NJ, NB, CG]), ALU.mult)\
                .then_inc(s["lg_m"], 1)
            dve.wait_ge(s["lg_m"], 1)
            v.tensor_reduce(lgr[:, :], LM[:, :, :], AX_X, ALU.add).then_inc(s["lg_r"], 1)
            dve.wait_ge(s["z_mm"], 1)
            dve.wait_ge(s["ld_band2"], 64)
            v.tensor_tensor(zz[:, :], Hb[0:NB, 0:NJ], bandb[:, :], ALU.add).then_inc(s["z_c"], 1)
            dve.wait_ge(s["z_c"], 1)
            v.tensor_reduce(mx3[:, :], zz[:, 1:NJ].rearrange("p (l j) -> p l j", j=3), AX_X, ALU.max)\
                .then_inc(s["z_c"], 1)
            dve.wait_ge(s["z_c"], 2)
            v.tensor_tensor(z2[:, 1:NJ].rearrange("p (l j) -> p l j", j=3), zz[:, 1:NJ].rearrange("p (l j) -> p l j", j=3),
                            mx3[:, :].unsqueeze(2).to_broadcast([NB, 3, 3]), ALU.subtract).then_inc(s["z_c"], 1)
            dve.wait_ge(s["z_e"], 1)
            v.tensor_reduce(mx3[:, :], z2[:, 1:NJ].rearrange("p (l j) -> p l j", j=3), AX_X, ALU.add)
            link(v.tensor_scalar(bw[:, 0:1], z2[:, 0:1], 1.0, None, ALU.add))
            v.reciprocal(mx3[:, :], mx3[:, :])
            link(v.reciprocal(bw[:, 0:1], bw[:, 0:1]))
            v.tensor_tensor(bw[:, 1:NJ].rearrange("p (l j) -> p l j", j=3), z2[:, 1:NJ].rearrange("p (l j) -> p l j", j=3),
                            mx3[:, :].unsqueeze(2).to_broadcast([NB, 3, 3]), ALU.mult).then_inc(s["bw_t"], 1)
            dve.wait_ge(s["z_mm"], 2)
            v.tensor_copy(bwT[:, :], Hb[0:NJ, 32:32 + NB]).then_inc(s["bw_c"], 1)
            dve.wait_ge(s["w8_mm"], 1)
            for q, (c0, c1) in enumerate(((0, 1), (1, 2), (2, 4), (4, 8))):
                last = v.tensor_copy(W8[:, :, c0:c1],
                                     Hb[:, 128 + q * NB:128 + (q + 1) * NB].unsqueeze(2).to_broadcast([P, NB, c1 - c0]))
            last.then_inc(s["w8"], 1)
            dve.wait_ge(s["w8"], 1)
            for q in range(2):
                link(v.memset(ST[q][:, :], 1.0))

            def emit(t, _nxt, a, b, c, d, m):
                st = ST[t.p]
                after(dve, "tab", t.n - 1)
                if b:
                    dve.wait_ge(s["h0"], b.n + 1)
                    for h in range(NH):
                        last = v.bn_stats(bn0[:, h, :], Hb[:, h * D:(h + 1) * D])
                    last.then_inc(s["st0_b"], 1)
                    dve.wait_ge(s["st0_b"], b.n + 1)
                    apart(dve)
                    for h in range(NH):
                        last = v.bn_aggr(st[:, 2 * h:2 + 2 * h], bn0[:, h, :])
                    last.then_inc(s["st0"], 1)
                    dve.wait_ge(s["st0"], b.n + 1)
                if m:
                    dve.wait_ge(s["st1"], m.n + 1)
                after(dve, "pow", t.n)
                v.tensor_scalar(A6[:, 0:4], st[:, 1:8:2], EPS, None, ALU.add)
                v.tensor_scalar(A6[:, 4:6], st[:, 5:8:2], 1.0 + EPS, EPS * EPS, ALU.mult, ALU.add)\
                    .then_inc(s["var"], 1)
                if a:
                    dve.wait_ge(s["z_done"], a.n + 1)
                    w = W8[:, bass.ds(a.n, 1), :].to_broadcast([P, NH, 8]).unsqueeze(3).to_broadcast([P, NH, 8, 32])
                    v.tensor_tensor(Zw.rearrange("p h (g c) -> p h g c", g=8),
                                    Zb[:, :].rearrange("p (h g c) -> p h g c", h=NH, g=8), w, ALU.mult)\
                        .then_inc(s["zw"], 1)
                    dve.wait_ge(s["zw"], a.n + 1)
                    lo, hi = Zw[:, :, 0:32], Zw[:, :, 32:64]
                    v.tensor_tensor(I2[:, :, 0::2], lo, hi, ALU.add)
                    v.tensor_tensor(I2[:, :, 1::2], lo, hi, ALU.subtract).then_inc(s["inv"], 1)
                    dve.wait_ge(s["inv"], a.n * 2 + 1)
                    hi = Zw[:, :, 64:128]
                    v.tensor_tensor(I1[:, :, 0::2], I2[:, :, :], hi, ALU.add)
                    v.tensor_tensor(I1[:, :, 1::2], I2[:, :, :], hi, ALU.subtract).then_inc(s["inv"], 1)
                if b:
                    after(dve, "hcE", b.n - 1)
                dve.wait_ge(s["pow"], t.n + 1)
                v.scalar_tensor_tensor(out=N6[t.p][:, 0:4], in0=st[:, 8:12], scalar=-1.0, in1=st[:, 0:8:2],
                                       op0=ALU.mult, op1=ALU.mult)
                v.scalar_tensor_tensor(out=N6[t.p][:, 4:6], in0=st[:, 12:14], scalar=-1.0, in1=st[:, 4:8:2],
                                       op0=ALU.mult, op1=ALU.mult)
                v.tensor_scalar(O1[t.p][:, :], st[:, 10:12], 1.0, None, ALU.add).then_inc(s["nrm"], 1)
                if a:
                    dve.wait_ge(s["inv"], a.n * 2 + 2)
                    after(dve, "h0", a.n - 1)
                    hi = Zw[:, :, 128:256]
                    v.tensor_tensor(Q[a.p][:, :, 0::2], I1[:, :, :], hi, ALU.add)
                    v.tensor_tensor(Q[a.p][:, :, 1::2], I1[:, :, :], hi, ALU.subtract).then_inc(s["q"], 1)
                if m:
                    after(dve, f"base_st{m.p}", m.h * 16)
                    dve.wait_ge(s["nrm"], t.n + 1)
                    for h in range(NH):
                        last = v.tensor_scalar(Bs[m.p][:, h, :], H1[m.p][:, h, :], O1[t.p][:, h:h + 1],
                                               N6[t.p][:, 2 + h:3 + h], ALU.mult, ALU.add)
                    last.then_inc(s["base"], 1)
                if d:
                    st_next = ST[1 - t.p]
                    dve.wait_ge(s["pexp"], d.n + 1)
                    after(dve, "tab", t.n)
                    v.reciprocal(st_next[:, 14:16], rsm[d.p][:, :]).then_inc(s["rv"], 1)
                    dve.wait_ge(s["av"], d.n + 1)
                    for h in range(NH):
                        last = v.scalar_tensor_tensor(out=U[d.p][:, h, :], in0=CX[:, :],
                                                      scalar=Pr[d.p][:, 129 * h:129 * h + 1],
                                                      in1=Ab[h][:, 0:DG], op0=ALU.mult, op1=ALU.add)
                    last.then_inc(s["u"], 1)
                    after(dve, "yp", d.n - 1)
                    dve.wait_ge(s["u"], d.n + 1)
                    dve.wait_ge(s["rv"], d.n + 1)
                    for h in range(NH):
                        last = v.scalar_tensor_tensor(out=H1[d.p][:, h, :], in0=U[d.p][:, h, 0:D],
                                                      scalar=st_next[:, 14 + h:15 + h], in1=hc[d.r][:, h, :],
                                                      op0=ALU.mult, op1=ALU.add)
                    last.then_inc(s["h1"], 1)
                    v.tensor_copy(TUG[:, bass.ds(d.n, 1), :, :].rearrange("p b h e -> p (b h) e"), U[d.p][:, :, D:DG])\
                        .then_inc(s["tug"], 1)
                if c:
                    dve.wait_ge(s["eg"], c.n + 1)
                    v.tensor_copy(TEG[:, bass.ds(c.n, 1), :, :].rearrange("p b h e -> p (b h) e"),
                                  Pb[:, 400:416].rearrange("p (h e) -> p h e", h=NH))
                    v.tensor_copy(Ex[c.r][:, :, D:DG], Pb[:, 400:416].rearrange("p (h e) -> p h e", h=NH))\
                        .then_inc(s["eg_ev"], 1)
                    dve.wait_ge(s["sm"], c.n + 1)
                    v.tensor_reduce(nmx[c.p][:, 0:1], Sb[:, 0:129], AX_X, ALU.max, negate=True)
                    v.tensor_reduce(nmx[c.p][:, 1:2], Sb[:, 129:386], AX_X, ALU.max, negate=True)\
                        .then_inc(s["nmax"], 1)
                if d:
                    dve.wait_ge(s["h1"], d.n + 1)
                    for h in range(NH):
                        last = v.bn_stats(bn1[:, h, :], H1[d.p][:, h, :])
                    last.then_inc(s["st1_b"], 1)
                    dve.wait_ge(s["st1_b"], d.n + 1)
                    apart(dve)
                    for h in range(NH):
                        last = v.bn_aggr(ST[1 - t.p][:, 4 + 2 * h:6 + 2 * h], bn1[:, h, :])
                    last.then_inc(s["st1"], 1)
            steps(dve, emit)

            dve.wait_ge(s["tab"], NB + LAG)
            dve.wait_ge(s["tug"], NB)
            sh = [P, NB, NH, NE]

            def col(a, b, step=1, late=LAG):
                return TST[:, late:late + NB, a:b:step]

            def wide(ap):
                return ap.unsqueeze(3).to_broadcast(sh)
            v.tensor_scalar(sd0[:, :, :], col(1, 4, 2, 1), EPS, None, ALU.add)
            v.tensor_tensor(dm[:, :, :], col(0, 4, 2, 1), col(4, 8, 2), ALU.subtract)
            v.tensor_tensor(GL[:, :, :, :], TUG[:, :, :, :], wide(col(14, 16)), ALU.mult).then_inc(s["gt_c"], 1)
            dve.wait_ge(s["gt_c"], 1)
            v.tensor_tensor(sd0[:, :, :], sd0[:, :, :], col(8, 10, 1, 1), ALU.mult).then_inc(s["gt_c"], 1)
            v.tensor_tensor(GM[:, :, :, :], wide(dm[:, :, :]),
                            sg[:, :].unsqueeze(1).to_broadcast([P, NB * NH, NE]).rearrange("p (b h) e -> p b h e", h=NH),
                            ALU.mult)
            dve.wait_ge(s["gt_c"], 2)
            v.tensor_tensor(TEG[:, :, :, :], TEG[:, :, :, :], wide(sd0[:, :, :]), ALU.mult).then_inc(s["gt_c"], 1)
            dve.wait_ge(s["gt_c"], 3)
            v.tensor_tensor(GL[:, :, :, :], GL[:, :, :, :], TEG[:, :, :, :], ALU.add).then_inc(s["gt_c"], 1)
            dve.wait_ge(s["gt_c"], 4)
            v.tensor_tensor(GL[:, :, :, :], GL[:, :, :, :], GM[:, :, :, :], ALU.add).then_inc(s["gt_c"], 1)
            dve.wait_ge(s["gt_c"], 5)
            v.tensor_tensor(GL[:, :, :, :], GL[:, :, :, :], wide(col(10, 12)), ALU.mult).then_inc(s["gt_c"], 1)
            dve.wait_ge(s["gt_t"], 1)
            for h in range(NH):
                last = v.tensor_scalar(GV[:, h, :, :, :].rearrange("p a e b -> p (a e) b"),
                                       GM[:, :, h, :].rearrange("p b e -> p e b"), 1.0, 0.5, ALU.add, ALU.mult)
            last.then_inc(s["vsp_t"], 1)
            for h in range(NH):
                v.tensor_scalar(GL[:, :, h, :], GM[:, :, h, :], 1.0, 0.5, ALU.add, ALU.mult).then_inc(s["gt_v"], 1)
            v.memset(one[:, :], 1.0)
            v.memset(Tv[:, :], 0.0)
            v.memset(Tc[:, :], 1.0)
            v.memset(bit[:, :], 1.0)
            for e in range(4):
                for eh in range(2):
                    v.tensor_copy(V[32 * e:32 * e + 32, eh, 0:1], vcls[32 * e:32 * e + 32, 4 * eh + e:4 * eh + e + 1])
            dve.wait_ge(s["vsp"], 1)
            last = v.tensor_copy(V[:, :, 1:NT].rearrange("p a (h t) -> p a h t", h=NH),
                                 bank[0][:, :].rearrange("p (h a t) -> p a h t", h=NH, a=2))
            link(last)
            s["step"] = sem("search_step")
            with dve.Fori(0, BITS) as i:
                for eh in range(2):
                    last = v.tensor_scalar(ge[:, eh, :], V[:, eh, :], Tc[:, eh:eh + 1], None, ALU.is_ge, ALU.add,
                                           accum_out=cnt[:, eh:eh + 1])
                last.then_inc(s["cn"], 1)
                dve.wait_ge(s["thr"], i + 1)
                v.scalar_tensor_tensor(out=mm2[:, :], in0=bank[1][:, 0:2], scalar=KTOK - 0.5, in1=bit[:, :],
                                       op0=ALU.is_ge, op1=ALU.mult).then_inc(s["step"], 1)
                dve.wait_ge(s["step"], i * 4 + 1)
                v.tensor_tensor(Tv[:, :], Tv[:, :], mm2[:, :], ALU.add).then_inc(s["step"], 1)
                v.tensor_scalar(bit[:, :], bit[:, :], 0.5, None, ALU.mult).then_inc(s["step"], 1)
                dve.wait_ge(s["step"], i * 4 + 3)
                v.tensor_tensor(Tc[:, :], Tv[:, :], bit[:, :], ALU.add).then_inc(s["step"], 1)
                dve.wait_ge(s["step"], i * 4 + 4)
            for eh in range(2):
                v.tensor_scalar(ge[:, eh, :], V[:, eh, :], Tv[:, eh:eh + 1], None, ALU.is_gt, ALU.add,
                                accum_out=cgt[:, eh:eh + 1])
                link(v.tensor_scalar(eq[:, eh, :], V[:, eh, :], Tv[:, eh:eh + 1], None, ALU.is_equal, ALU.add,
                                     accum_out=tot[:, eh:eh + 1]))
            v.tensor_copy(mm2[:, :], tot[:, :]).then_inc(s["tk_c"], 1)
            for eh in range(2):
                last = v.tensor_tensor_scan(sc[:, eh, :], one[:, :], eq[:, eh, :], 0.0, ALU.mult, ALU.add)
            dve.wait_ge(s["tk_mm"], 1)
            v.tensor_scalar(need[:, :], bank[2][:, 0:2], -1.0, float(KTOK), ALU.mult, ALU.add)
            link(v.tensor_copy(mm2[:, :], bank[3][:, 0:2]))
            link(v.tensor_tensor(need[:, :], need[:, :], mm2[:, :], ALU.subtract))
            for eh in range(2):
                link(v.scalar_tensor_tensor(out=eq[:, eh, :], in0=sc[:, eh, :], scalar=need[:, eh:eh + 1],
                                            in1=eq[:, eh, :], op0=ALU.is_le, op1=ALU.mult))
                link(v.tensor_tensor(ge[:, eh, :], ge[:, eh, :], eq[:, eh, :], ALU.add))
                link(v.tensor_tensor_scan(sc[:, eh, :], one[:, :], ge[:, eh, :], 0.0, ALU.mult, ALU.add))
            v.tensor_copy(tot[:, :], sc[:, :, NT - 1]).then_inc(s["tk_c"], 1)
            v.tensor_tensor(TB[:, :, 0:NT], sc[:, :, :], ge[:, :, :], ALU.subtract)
            v.tensor_copy(TB[:, :, NT:NT + 1], cst("batch").unsqueeze(1).to_broadcast([P, 2, 1]))
            dve.wait_ge(s["tk_mm"], 2)
            link(v.tensor_scalar(beg[:, :], bank[4][:, 0:2], 1.0, None, ALU.mult))
            v.tensor_tensor(fin[:, :], beg[:, :], tot[:, :], ALU.add)
            link(v.tensor_copy(TB[:, :, NT + 1], beg[:, :]))
            link(v.tensor_copy(mm2[:, :], TB[:, :, NT + 1]))
            link(v.tensor_tensor(TB[:, :, NT + 2], beg[:, :], mm2[:, :], ALU.subtract))
            for e in range(5):
                own = cst("owner")[:, e:e + 1]
                v.tensor_scalar(begM[:, e, :], beg[:, :], own, None, ALU.mult)
                last = v.tensor_scalar(finM[:, e, :], fin[:, :], own, None, ALU.mult)
            link(last)
            v.memset(jk[:, :], 0.0).then_inc(s["tc"], 1)

            s["ohu"] = sem("slots_begun")
            s["row"] = sem("row_chain")

            def place(job, t):
                m, n = SLOTS[t], job.q * 9 + t
                if t == 0:
                    after(dve, "smm", n)
                    v.tensor_scalar(ohu[:, :], iot[:, :], begM[:, bass.ds(job.el, 1), job.eh], None, ALU.is_ge)\
                        .then_inc(s["ohu"], 1)
                    dve.wait_ge(s["ohu"], job.q + 1)
                    v.scalar_tensor_tensor(out=oh[:, :], in0=iot[:, :], scalar=finM[:, bass.ds(job.el, 1), job.eh],
                                           in1=ohu[:, :], op0=ALU.is_lt, op1=ALU.mult).then_inc(s["ohd"], 1)
                    if not isinstance(job.q, int) or job.q > 1:
                        for c in range(3):
                            dve.wait_ge(s[f"gat{job.eh}{c}"], 48 * job.el)
                        dve.wait_ge(s["idc"], job.q - 1)
                r0 = n * 3
                B = bank[6 + t % 2]
                dve.wait_ge(s["smm"], n + 1)
                v.tensor_copy(SM[0:m, t, :], B[0:m, NT:NT + 3]).then_inc(s["row"], 1)
                dve.wait_ge(s["row"], r0 + 1)
                v.scalar_tensor_tensor(out=rk[0:m, t:t + 1], in0=cst("slot")[0:m, t:t + 1], scalar=SM[0:m, t, 1:2],
                                       in1=SM[0:m, t, 2:3], op0=ALU.subtract, op1=ALU.subtract)\
                    .then_inc(s["row"], 1)
                dve.wait_ge(s["row"], r0 + 2)
                v.tensor_scalar(jk[0:m, :], B[0:m, 0:NT], rk[0:m, t:t + 1], None, ALU.is_le, ALU.add,
                                accum_out=pos[0:m, t:t + 1]).then_inc(s["smc"], 1)
                v.tensor_scalar(rowf[0:m, t:t + 1], SM[0:m, t, 0:1], float(NT), -1.0, ALU.mult, ALU.add)\
                    .then_inc(s["row"], 1)
                dve.wait_ge(s["smc"], n + 1)
                dve.wait_ge(s["row"], r0 + 3)
                v.tensor_tensor(idx[job.eh][0:m, t:t + 1], rowf[0:m, t:t + 1], pos[0:m, t:t + 1], ALU.add)\
                    .then_inc(s["ixd"], 1)

            def scaled(job):
                dve.wait_ge(s["yt_t"], job.j + 1)
                for d in range(2):
                    last = v.tensor_scalar(yT[:, d, 0:job.w], bank[2 + d][:, 0:job.w], gam[:, d:d + 1],
                                           bet[:, d:d + 1], ALU.mult, ALU.add)
                last.then_inc(s["yt"], 1)

            def emit(prev, cur, nxt, tiles):
                for job, t in tiles:
                    place(job, t)
                if nxt:
                    scaled(nxt)
                if prev:
                    if prev.c == 0:
                        dve.wait_ge(s[f"wld{prev.eh}"], (prev.el + 1) * 48)
                    for t in range(prev.t0, prev.t1):
                        m = SLOTS[t]
                        dve.wait_ge(s["om"], prev.q * 9 + t + 1)
                        after(dve, "omul", prev.q * 9 + t - 1)
                        v.tensor_tensor(ot[t % 2][0:m, :], bank[4 + t % 2][0:m, 0:D], b2b[prev.eh][0:m, :], ALU.add)\
                            .then_inc(s["oadd"], 1)
            dve.wait_ge(s["ld_par"], 80)
            dve.wait_ge(s["zero"], 2)
            for t in range(9):
                place(Job(0, 0), t)
            scaled(Job(0, 0))
            jobs(dve, emit)


def constants():
    import numpy as np
    c = np.zeros((P, NCONST), np.float32)

    def put(name, a):
        c[:a.shape[0], CONST[name][0]:CONST[name][1]] = a
    put("ident", np.eye(P))
    haar, scale = np.zeros((P, P)), np.zeros(P)
    level = np.zeros(P, int)
    at = 0
    for lv, low in ((3, True), (3, False), (2, False), (1, False)):
        n = 1 << lv
        for y in range(P >> lv):
            haar[at, y * n:(y + 1) * n] = 1
            if not low:
                haar[at, y * n + n // 2:(y + 1) * n] = -1
            scale[at] = 1.0 / n
            level[at] = 0 if low else {3: 1, 2: 2, 1: 3}[lv]
            at += 1
    put("fwd", haar.T)
    put("inv", haar * scale[:, None])
    q = np.arange(P)
    own, img = q // NB, q % NB
    same = own[:, None] == own[None, :]
    put("same", same)
    put("before", same & (img[:, None] < img[None, :]))
    put("causal", np.where(q[None, :] <= q[:, None], 0.0, MASKED))
    put("sign", np.stack([1.0 - 2.0 * ((q >> (lv - 1)) & 1) for lv in (1, 2, 3)], 1))
    put("slot", q[:, None] + P * np.arange(9)[None, :])
    put("batch", img[:, None])
    m = np.arange(CG * NJ)
    put("diag", (m // NJ)[:, None] == np.arange(CG)[None, :])
    lvl = np.array([3] + [3] * 3 + [2] * 3 + [1] * 3)
    put("pick", ((m % NJ)[:, None] == np.arange(NJ)[None, :]) * (0.5 ** lvl)[None, :])
    spread = np.zeros((NJ, LEAF, P))
    first = {1: 1, 2: 4, 3: 7}
    for g in range(LEAF):
        for p in range(P):
            r = level[p]
            if r == 0 and g == 0:
                j = 0
            elif r == g:
                j = first[r] + 2
            elif r > g:
                j = first[r]
            else:
                j = first[g] + 1
            spread[j, g, p] = (1 / 8, 1 / 8, 1 / 4, 1 / 2)[g]
    put("spread", spread.reshape(NJ, LEAF * P))
    put("owner", own[:, None] == np.arange(5)[None, :])
    return c


def kernel(x, cls_tok, L0_tok_Wa, L0_tok_ba, L0_tok_Wd1, L0_tok_bd1, L0_tok_Wd2, L0_tok_bd2, L0_tok_Wd3, L0_tok_bd3,
           L0_attn_R, L0_ffn_gate_w, L0_ffn_ln_gamma, L0_ffn_ln_beta, L0_ffn_fc1s, L0_ffn_b1s, L0_ffn_fc2s, L0_ffn_b2s):
    import numpy as np
    import concourse.bacc as bacc
    from concourse.bass_utils import run_bass_kernel_spmd

    def lay(a, *shape):
        return np.ascontiguousarray(a).reshape(shape)
    arrays = {
        "x": lay(np.asarray(x).reshape(NB, NH, P, D).transpose(2, 0, 1, 3), P, NB * NH * D),
        "cls_tok": np.asarray(cls_tok),
        "Wa": np.asarray(L0_tok_Wa), "ba": np.asarray(L0_tok_ba),
        "Wd1": np.asarray(L0_tok_Wd1), "bd1": np.asarray(L0_tok_bd1),
        "Wd2": np.asarray(L0_tok_Wd2), "bd2": np.asarray(L0_tok_bd2),
        "Wd3": np.asarray(L0_tok_Wd3), "bd3": np.asarray(L0_tok_bd3),
        "R": np.asarray(L0_attn_R),
        "gate_w": np.asarray(L0_ffn_gate_w),
        "gate_wT": lay(np.asarray(L0_ffn_gate_w).T.reshape(2, P, NE).transpose(1, 0, 2), P, 2, NE),
        "gamma": lay(np.asarray(L0_ffn_ln_gamma).reshape(2, P).T, P, 2),
        "beta": lay(np.asarray(L0_ffn_ln_beta).reshape(2, P).T, P, 2),
        "fc1T": lay(np.asarray(L0_ffn_fc1s).transpose(0, 2, 1).reshape(NE, 2, P, NF).transpose(0, 2, 1, 3), NE, P, 2 * NF),
        "b1": lay(np.asarray(L0_ffn_b1s).reshape(NE, 8, P).transpose(2, 0, 1), P, NE, 8),
        "fc2T": lay(np.asarray(L0_ffn_fc2s).transpose(0, 2, 1).reshape(NE, 8, P, D).transpose(0, 2, 1, 3), NE, P, 8 * D),
        "b2": np.asarray(L0_ffn_b2s),
        "const": constants(),
    }
    arrays = {k: np.ascontiguousarray(a) for k, a in arrays.items()}
    nc = bacc.Bacc("TRN2", target_bir_lowering=False, num_devices=1)
    args = [nc.dram_tensor(f"in_{k}", a.shape, mybir.dt.from_np(a.dtype), kind="ExternalInput").ap()
            for k, a in arrays.items()]
    out = nc.dram_tensor("out_0", (NB, NT, D), F32, kind="ExternalOutput").ap()
    build_program(nc, *args, out)
    r = run_bass_kernel_spmd(nc, [{f"in_{k}": a for k, a in arrays.items()}], core_ids=[0])
    return r.results[0]["out_0"]
```

```python
from contextlib import ExitStack

import concourse.bass as bass
from concourse import mybir

ALU = mybir.AluOpType
ACT = mybir.ActivationFunctionType
AX_X = mybir.AxisListType.X
F32 = mybir.dt.float32
F32R = mybir.dt.float32r
BF16 = mybir.dt.bfloat16
F16 = mybir.dt.float16
I32 = mybir.dt.int32

P = 128
NB = 32
NH = 2
D = 256
NT = 257
NE = 8
NF = 1024
KTOK = NB * NT // NE
NJ = 10
CG = 8
DG = D + NE
LEAF = 4
SLOTS = [P] * 8 + [KTOK - 8 * P]
CHUNKS = [(0, 3), (3, 6), (6, 9)]
TAIL_W = sum(SLOTS[6:])
EPS = 1e-5
MASKED = -1.0e9
PARTS = ((0, 0), (0, 1), (1, 0))
TESTS = 13
BITS = 26

CONST = {}
_at = 0
for _name, _n in [("ident", P), ("fwd", P), ("inv", P), ("same", P), ("before", P), ("causal", P),
                  ("sign", 3), ("slot", 9), ("batch", 1), ("diag", CG), ("pick", NJ), ("spread", 4 * P),
                  ("owner", 5), ("rep1", P), ("rep2", P), ("rep3", 2 * P)]:
    CONST[_name] = (_at, _at + _n)
    _at += _n
NCONST = _at


def build_program(nc, x, cls_tok, Wa, ba, Wd1, bd1, Wd2, bd2, Wd3, bd3, R, gate_w, gate_wT, gamma, beta,
                  fc1T, b1, fc2T, b2, b2T, const, out, debug=None):
    ctx = ExitStack()
    with ctx:
        def sb(name, shape, dt=F32):
            return ctx.enter_context(nc.sbuf_tensor(name, shape, dt))

        def sem(name):
            return ctx.enter_context(nc.semaphore(name))

        rows = nc.dram_tensor("rows", [NB * NT, DG], F32).ap()
        out_rows = out.rearrange("b t d -> (b t) d")

        bank = [ctx.enter_context(nc.psum_tensor(f"bank{i}", [P, 512], F32)) for i in range(8)]
        Zb, Hb, Tb, Rb, Sb, Pb, Ab0, Ab1 = bank
        Ab = [Ab0, Ab1]

        Lb = [bank[0], bank[1], bank[6]]

        RB = [{1: [bank[3 * h + k][:, 0:384] for k in range(3)], 3: [bank[3 * h + k][:, 384:480] for k in range(3)],
               2: [bank[6][:, 0:192], bank[6][:, 192:384], bank[7][:, 0:192]]} for h in range(NH)]
        RA = [bank[3 * h][:, 480:512] for h in range(NH)]

        C = sb("C", [P, NCONST])

        def cst(name):
            return C[:, CONST[name][0]:CONST[name][1]]
        ident = cst("ident")
        identb = sb("identb", [P, P], BF16)
        causalb = sb("causalb", [P, P], BF16)
        Rw = sb("Rw", [P, 2, D])
        gwT = sb("gwT", [P, 2, NE])
        gam = sb("gam", [P, 2])
        bet = sb("bet", [P, 2])
        b1s = sb("b1s", [P, NE, 8])
        b2c = sb("b2c", [P, NE, 2])
        bandb = sb("bandb", [NB, NJ])
        mhalf = sb("mhalf", [P, 6])
        GL = sb("GL", [P, NB, NH, NE])
        GM = sb("GM", [P, NB, NH, NE])
        sd0 = sb("sd0", [P, NB, NH])
        dm = sb("dm", [P, NB, NH])
        GV = sb("GV", [P, NH, 2, 4, NB])
        V = sb("V", [P, 2, NT])
        ge = sb("ge", [P, 2, NT])
        eq = sb("eq", [P, 2, NT])
        sc = sb("sc", [P, 2, NT])
        one = sb("one", [P, NT])
        Tv = sb("Tv", [P, 2])
        Tc = sb("Tc", [P, 2])
        Tn = sb("Tn", [P, 2])
        Tp = sb("Tp", [P, 2])
        bit = sb("bit", [P, 2])
        cnt = sb("cnt", [P, 2], F16)
        sameh = sb("sameh", [P, P], F16)
        mm2 = sb("mm2", [P, 2])
        cgt = sb("cgt", [P, 2])
        need = sb("need", [P, 2])
        tot = sb("tot", [P, 2])
        beg = sb("beg", [P, 2])
        fin = sb("fin", [P, 2])
        begM = sb("begM", [P, 5, 2])
        finM = sb("finM", [P, 5, 2])
        TB = sb("TB", [P, 2, NT + 3], BF16)
        iot = sb("iot", [P, KTOK])
        ohu = sb("ohu", [P, KTOK], BF16)
        oh = sb("oh", [P, KTOK], BF16)
        SM = sb("SM", [P, 9, 3])
        rk = sb("rk", [P, 9])
        pos = sb("pos", [P, 9])
        jk = sb("jk", [P, NT], BF16)
        rowf = sb("rowf", [P, 9])
        idx = [sb(f"idx{i}", [P, 9], I32) for i in range(2)]
        sidx = [sb(f"sidx{i}", [P, 9], I32) for i in range(2)]
        b2b = [sb(f"b2b{i}", [P, D]) for i in range(2)]
        ot = [sb(f"ot{i}", [P, D]) for i in range(2)]
        bn0 = sb("bn0", [P, NH, 6])
        bn1 = sb("bn1", [P, NH, 6])
        sg = sb("sg", [P, NE])
        vcls = sb("vcls", [P, NE])
        cbs = sb("cbs", [P, D])
        cyp = sb("cyp", [P, D])
        phase = ExitStack()

        def sb(name, shape, dt=F32):
            return phase.enter_context(nc.sbuf_tensor(name, shape, dt))
        BIG = sb("BIG", [P, NB * NH * D])
        XS = BIG[:, :].rearrange("p (h g b c) -> p h g b c", h=NH, b=NB, c=CG)
        ARENA = sb("ARENA", [P, 10816])
        a = [0]

        def cut(n):
            a[0] += n
            assert a[0] <= 10816, a[0]
            return ARENA[:, a[0] - n:a[0]]
        WP = cut(NH * D * NJ).rearrange("p (h c j) -> p h c j", h=NH, c=D)
        bsum = [{lv: cut((D >> lv) * 3) for lv in (1, 2, 3)} for _ in range(NH)]
        band = {lv: cut(3 * (D >> lv) * 3).rearrange("p (k m) -> p k m", k=3) for lv in (1, 2, 3)}
        bandA = cut(32)
        Xc = [cut(NH * D).rearrange("p (h c) -> p h c", h=NH) for _ in range(2)]
        L1 = cut(NH * 128).rearrange("p (h c) -> p h c", h=NH)
        L2 = cut(NH * 64).rearrange("p (h c) -> p h c", h=NH)
        late, a[0] = a[0], 0
        Zw = cut(NH * D).rearrange("p (h c) -> p h c", h=NH)
        I2 = cut(NH * 64).rearrange("p (h c) -> p h c", h=NH)
        I1 = cut(NH * 128).rearrange("p (h c) -> p h c", h=NH)
        Q = [cut(NH * D).rearrange("p (h c) -> p h c", h=NH) for _ in range(2)]
        Ex = [cut(NH * DG).rearrange("p (h c) -> p h c", h=NH) for _ in range(4)]
        ERT = [cut(2 * D).rearrange("p (c t) -> p c t", c=2) for _ in range(2)]
        PTS = [cut(384) for _ in range(2)]
        U = [cut(NH * DG).rearrange("p (h c) -> p h c", h=NH) for _ in range(2)]
        assert a[0] <= late - 2 * NH * D - NH * 192
        a[0] = late
        Pr = [cut(388) for _ in range(2)]
        hc = [sb(f"hc{i}", [P, NH, D]) for i in range(4)]
        gwb = sb("gwb", [P, NE, D])
        clsb = sb("clsb", [P, D])
        ET = [sb(f"ET{i}", [P, 2, NT]) for i in range(2)]
        H1 = [sb(f"H1{i}", [P, NH, D]) for i in range(2)]
        Bs = [sb(f"Bs{i}", [P, NH, D]) for i in range(2)]
        Yp = [sb(f"Yp{i}", [P, NH, D]) for i in range(2)]
        ST = [sb(f"ST{i}", [P, 16]) for i in range(2)]
        A6 = sb("A6", [P, 6])
        N6 = [sb(f"N6{i}", [P, 6]) for i in range(2)]
        O1 = [sb(f"O1{i}", [P, 2]) for i in range(2)]
        nmx = [sb(f"nmx{i}", [P, 2]) for i in range(2)]
        rsm = [sb(f"rsm{i}", [P, 2]) for i in range(2)]
        W8 = sb("W8", [P, NB, 8])
        TUG = sb("TUG", [P, NB, NH, NE])
        TEG = sb("TEG", [P, NB, NH, NE])
        TST = sb("TST", [P, NB + 4, 16])
        LM = sb("LM", [CG * NJ, NB, CG])
        lgr = sb("lgr", [CG * NJ, NB])
        zz = sb("zz", [NB, NJ])
        z2 = sb("z2", [NB, NJ])
        bw = sb("bw", [NB, NJ])
        mx3 = sb("mx3", [NB, 3])
        bwT = sb("bwT", [NJ, NB])
        CX = sb("CX", [P, DG])
        ch = sb("ch", [P, DG])
        junk = sb("junk", [P, D])
        cst8 = sb("cst8", [P, 24])
        cbn = sb("cbn", [P, 6])
        cpw = sb("cpw", [P, 4])
        cgl = sb("cgl", [P, NE])
        phase.close()
        WH = [[ctx.enter_context(nc.sbuf_tensor(f"w{l}{'hl'[i]}{eh}", [P, k, n], F32R)) for i in range(2)]
              for l, k, n in ((1, 2, NF), (2, 8, D)) for eh in range(2)]
        w1s, w2s = WH[0:2], WH[2:4]
        hT = [[ctx.enter_context(nc.sbuf_tensor(f"h{'hl'[i]}{p}", [P, 8, 384], F32R)) for i in range(2)]
              for p in range(2)]
        yT = [None, None]
        yT[0] = ctx.enter_context(nc.sbuf_tensor("yh", [P, 2, 384], F32R))
        raw = ctx.enter_context(nc.sbuf_tensor("raw", [P, 2 * NF], F32))
        yT[1] = ctx.enter_context(nc.sbuf_tensor("yl", [P, 2, 384], F32R))
        yr = ctx.enter_context(nc.sbuf_tensor("yr", [P, 2, 384], F32))
        oT = ctx.enter_context(nc.sbuf_tensor("oT", [P, 2, TAIL_W], F32))
        hr = [ctx.enter_context(nc.sbuf_tensor(f"hr{i}", [P, 384], F32)) for i in range(2)]
        ob = [ctx.enter_context(nc.sbuf_tensor(f"ob{i}", [P, D], F32)) for i in range(3)]
        yg = [ctx.enter_context(nc.sbuf_tensor(f"yg{i}", [P, 9, DG], F32)) for i in range(2)]

        names = """ld_const ld_x0 ld_x1 ld_x2 ld_x3 ld_par ld_band0 ld_band1 ld_band2 ld_band3 ld_bias ld_cls cvt wp wp_part wp_v rep lg_mm lg_m lg_r z_mm z_c z_e bw_t bw_c w8_mm w8
            cls_d cls_p cls_a cls_t et0 cls_st cls_g zero
            xc xc_l z_done zw inv q h0 st0_b st0 var pow nrm hcE et et_ev er er_ev eg eg_ev sm nmax pexp pt pt_ev av u h1 rv
            st1_b st1 tug teg base yp tab base_st0 base_st1 yp_st0 yp_st1
            gt_c gt_t gt_v vt_st vsp_t vsp thr tc cn tk_c tk_mm
            ohd smm smc ixc ixd wld bld0 bld1 whi wlo hhi hlo yhi yr gat00 gat01 gat02 gat10 gat11 gat12 yt_t yt hmm hact om oadd omul omt oev obk scat0 scat1 scat2 idc""".split()
        s = {n: sem(n) for n in names}

        def after(eng, name, count):
            if not isinstance(count, int) or count > 0:
                eng.wait_ge(s[name], count)

        def apart(eng):
            eng.nop(nofuse=True)

        LAG = 4
        UNROLL = 4

        class Step:
            def __init__(self, i, k):
                self.n, self.p, self.r = i * UNROLL + k, k % 2, k % 4
                self.h = i * (UNROLL // 2) + k // 2

        HEAD, TAIL = 4, 28

        def steps(eng, emit):
            def images(i, k, bounded):
                return [Step(i, k)] + [Step(i, k + d) if not bounded or 0 <= k + d < NB else None
                                       for d in range(1, -LAG - 1, -1)]
            for k in range(HEAD):
                emit(*images(0, k, True))
            with eng.Fori(HEAD // UNROLL, TAIL // UNROLL) as i:
                for k in range(UNROLL):
                    emit(*images(i, k, False))
            for k in range(TAIL, NB + LAG):
                emit(*images(0, k, True))

        class Job:
            def __init__(self, el, k):
                self.el, self.eh, self.c = el + k // 6, k // 3 % 2, k % 3
                self.q, self.j, self.p = self.el * 2 + self.eh, el * 6 + k, k % 2
                self.e = self.el + 4 * self.eh
                self.q_next = not (isinstance(self.q, int) and self.q == NE - 1)
                self.t0, self.t1 = CHUNKS[self.c]
                self.w = sum(SLOTS[self.t0:self.t1])

        def place_bank(job, t):
            return bank[6 + t % 2] if isinstance(job.q, int) and job.q == 0 else bank[7]

        def early(prev, tiles):
            return tiles[:max(0, len(tiles) - 3)] if prev else tiles

        def spread(tiles, at, steps_):
            return [tile for i, tile in enumerate(tiles) if (i + 1) * steps_ // (len(tiles) + 1) == at]

        def back_bank(t):
            return bank[4 + t % 2][:, 0:D] if t < 8 else bank[4][:, D:2 * D]

        def jobs(eng, emit):
            def one(el, k):
                if isinstance(el, int) and el == 0 and k < 3:
                    both = [(3, t) for t in range(9)] + [(6, t) for t in range(9)]
                    tiles = both[(0, 7, 12)[k]:(7, 12, 18)[k]]
                else:
                    far = k // 3 * 3 + 6
                    tiles = [(far, t) for t in range(*((0, 2), (2, 5), (5, 9))[k % 3])]
                last = isinstance(el, int) and el == 3
                emit(Job(el, k - 1) if k or not isinstance(el, int) or el else None, Job(el, k),
                     Job(el, k + 1) if not last or k < 5 else None,
                     [(Job(el, f), t) for f, t in tiles if not last])
            for k in range(6):
                one(0, k)
            with eng.Fori(1, 3) as el:
                for k in range(6):
                    one(el, k)
            for k in range(6):
                one(3, k)
            emit(Job(3, 5), None, None, [])

        block = ctx.enter_context(nc.Block())

        @block.sync
        def _(sp):
            sp.dma_start(C[:, :], const).then_inc(s["ld_const"], 16)
            for lv, W in ((1, Wd3), (3, Wd1), (2, Wd2)):
                rows_ = D >> lv
                sp.dma_start(band[lv][0:rows_, :, :], W.rearrange("(k y x) j -> y k (x j)", k=3, y=rows_))\
                    .then_inc(s[f"ld_band{lv}"], 16)
            sp.dma_start(bandA[0:32, :], Wa.rearrange("(y x) j -> y (x j)", y=32)).then_inc(s["ld_band0"], 16)
            n = NB * NH * D // 4
            for q in range(4):
                sp.dma_start(BIG[:, q * n:(q + 1) * n], x[:, q * n:(q + 1) * n]).then_inc(s[f"ld_x{q}"], 16)
                if q == 0:
                    sp.dma_start(clsb[:, :], cls_tok.rearrange("a b d -> (a b) d").partition_broadcast(P)
                                 .rearrange("p a d -> p (a d)")).then_inc(s["ld_cls"], 16)
                    sp.dma_start(gwb[:, :, :], gate_w.unsqueeze(0).partition_broadcast(P)
                                 .rearrange("p a e d -> p (a e) d")).then_inc(s["ld_cls"], 16)
            sp.dma_start(Rw[:, :, :], R.rearrange("(c p) e -> p c e", p=P)).then_inc(s["ld_par"], 16)
            sp.dma_start(gwT[:, :, :], gate_wT).then_inc(s["ld_par"], 16)
            sp.dma_start(gam[:, :], gamma).then_inc(s["ld_par"], 16)
            sp.dma_start(bet[:, :], beta).then_inc(s["ld_par"], 16)
            sp.dma_start(b1s[:, :, :], b1).then_inc(s["ld_par"], 16)
            sp.dma_start(b2c[:, :, :], b2T).then_inc(s["ld_par"], 16)
            after(sp, "cls_g", 1)
            cls_out = out.rearrange("b t d -> b (t d)")[:, 0:D]
            cls_rows = rows.rearrange("(b t) d -> b (t d)", b=NB)
            sp.dma_start(cls_out, cbs[0:NB, :]).then_inc(s["cls_st"], 16)
            sp.dma_start(cls_rows[:, 0:D], cyp[0:NB, :]).then_inc(s["cls_st"], 16)
            sp.dma_start(cls_rows[:, D:DG], vcls[0:NB, :]).then_inc(s["cls_st"], 16)

            out_img = out.rearrange("b t d -> b (t d)")
            rows_img = rows.rearrange("(b t) d -> b (t d)", b=NB)

            def emit(_t, _nxt, _a, _b, _c, _d, m):
                if m:
                    dst = out_img[bass.ds(m.n, 1), D:].rearrange("b (h p d) -> p (b h) d", h=NH, p=P)
                    sp.wait_ge(s["base"], m.n + 1)
                    sp.dma_start(dst, Bs[m.p][:, :, :]).then_inc(s[f"base_st{m.p}"], 16)
                    dst = rows_img[bass.ds(m.n, 1), DG:].rearrange("b (h p d) -> p (b h) d", h=NH, p=P)[:, :, 0:D]
                    sp.wait_ge(s["yp"], m.n + 1)
                    sp.dma_start(dst, Yp[m.p][:, :, :]).then_inc(s[f"yp_st{m.p}"], 16)
            steps(sp, emit)
            def weights(el, eh, layer):
                q, e = el * 2 + eh, el + 4 * eh
                after(sp, "wlo", q * 2 + layer)
                if layer == 0:
                    sp.dma_start(raw[:, :], fc1T[bass.ds(e, 1), :, :].rearrange("e p c -> p (e c)"))\
                        .then_inc(s["wld"], 16)
                else:
                    sp.dma_start(raw[:, :], fc2T[bass.ds(e, 1), :, :].rearrange("e p c -> p (e c)"))\
                        .then_inc(s["wld"], 16)
                    after(sp, "oadd", (q - 1) * 6)
                    sp.dma_start(b2b[eh][:, :], b2[bass.ds(e, 1), :].partition_broadcast(P).rearrange("p e d -> p (e d)"))\
                        .then_inc(s[f"bld{eh}"], 16)
            sp.wait_ge(s["cls_g"], 1)
            weights(0, 0, 0)
            vt = rows_img[:, DG:].rearrange("b (h p e) -> p b h e", h=NH, p=P)[:, :, :, D:DG]
            sp.wait_ge(s["gt_v"], 2)
            for h in range(NH):
                sp.dma_start(vt[:, :, h, :], GL[:, :, h, :]).then_inc(s["vt_st"], 16)
            weights(0, 0, 1)
            weights(0, 1, 0)
            weights(0, 1, 1)
            with sp.Fori(1, 4) as el:
                for eh in range(2):
                    for layer in range(2):
                        weights(el, eh, layer)
            for r in range(3):
                sp.wait_ge(s[f"scat{r}"], 16 * 3 * NE)

        @block.gpsimd
        def _(po):
            g = nc.gpsimd
            g.memset(mhalf[:, :], -0.5).then_inc(s["zero"], 1)
            g.iota(iot[:, :], [[1, KTOK]], base=0, channel_multiplier=0, allow_small_or_imprecise_dtypes=True)\
                .then_inc(s["zero"], 1)
            po.wait_ge(s["cls_d"], 1)
            po.wait_ge(s["zero"], 1)
            g.tensor_tensor(cst8[:, 3:4], cst8[:, 2:3], mhalf[:, 0:1], ALU.pow).then_inc(s["cls_p"], 1)
            po.wait_ge(s["cls_d"], 2)
            g.tensor_tensor(cpw[:, 2:4], cpw[:, 0:2], mhalf[:, 0:2], ALU.pow).then_inc(s["cls_p"], 1)

            def columns(m):
                after(po, "xc", m.n)
                after(po, "z_done", m.n - 1)
                xv = XS[:, :, :, bass.ds(m.n, 1), :].rearrange("p h g b c -> p h g (b c)")
                x0, x1 = xv[:, :, :, 0::2], xv[:, :, :, 1::2]
                dst = Xc[m.p]
                g.tensor_tensor(L1.rearrange("p h (g c) -> p h g c", c=CG // 2), x0, x1, ALU.add).then_inc(s["xc_l"], 1)
                g.tensor_tensor(dst[:, :, 128:256].rearrange("p h (g c) -> p h g c", c=CG // 2), x0, x1, ALU.subtract)
                po.wait_ge(s["xc_l"], m.n * 2 + 1)
                g.tensor_tensor(L2[:, :, :], L1[:, :, 0::2], L1[:, :, 1::2], ALU.add).then_inc(s["xc_l"], 1)
                g.tensor_tensor(dst[:, :, 64:128], L1[:, :, 0::2], L1[:, :, 1::2], ALU.subtract)
                po.wait_ge(s["xc_l"], m.n * 2 + 2)
                g.tensor_tensor(dst[:, :, 0:32], L2[:, :, 0::2], L2[:, :, 1::2], ALU.add)
                g.tensor_tensor(dst[:, :, 32:64], L2[:, :, 0::2], L2[:, :, 1::2], ALU.subtract).then_inc(s["xc"], 1)

            def emit(t, nxt, _a, b, _c, _d, m):
                if b:
                    after(po, "hcE", b.n - 1)
                po.wait_ge(s["var"], t.n + 1)
                g.tensor_tensor(ST[t.p][:, 8:14], A6[:, :], mhalf[:, :], ALU.pow).then_inc(s["pow"], 1)
                if nxt:
                    columns(nxt)
                po.wait_ge(s["pow"], t.n + 1)
                g.tensor_copy(TST[:, bass.ds(t.n, 1), :].rearrange("p b k -> p (b k)"), ST[t.p][:, :])\
                    .then_inc(s["tab"], 1)
            for q in range(4):
                po.wait_ge(s[f"ld_x{q}"], 16)
            columns(Step(0, 0))
            steps(po, emit)

            def low(eh, q, layer):
                hi, lo = (w1s, w2s)[layer][eh]
                po.wait_ge(s["whi"], q * 2 + layer + 1)
                g.tensor_tensor(lo[:, :, :].rearrange("p a b -> p (a b)"), raw[:, :],
                                hi[:, :, :].rearrange("p a b -> p (a b)"), ALU.subtract).then_inc(s["wlo"], 1)

            low(0, 0, 0)
            low(0, 0, 1)
            tok = bass.IndirectOffsetOnAxis

            def gather(job):
                eh = job.eh
                for t, m in enumerate(SLOTS):
                    po.wait_ge(s["ixd"], job.q * 9 + t + 1)
                    apart(po)
                    g.indirect_dma_start(out=yg[eh][0:m, t, :], out_offset=None, in_=rows,
                                         in_offset=tok(ap=idx[eh][0:m, t:t + 1], axis=0))\
                        .then_inc(s[f"gat{eh}{t // 3}"], 16)
                if not isinstance(job.q, int) or job.q > 1:
                    for r in range(3):
                        po.wait_ge(s[f"scat{r}"], (job.q - 1) * 48)
                apart(po)
                g.tensor_copy(sidx[eh][:, 0:8], idx[eh][:, 0:8])
                g.tensor_copy(sidx[eh][0:SLOTS[8], 8:9], idx[eh][0:SLOTS[8], 8:9]).then_inc(s["idc"], 1)

            def scatter(job):
                for t in range(job.t0, job.t1):
                    m = SLOTS[t]
                    po.wait_ge(s["omul"], job.q * 9 + t + 1)
                    if t == 0:
                        po.wait_ge(s["idc"], job.q + 1)
                        for r in range(3):
                            after(po, f"scat{r}", job.q * 48)
                    apart(po)
                    g.indirect_dma_start(out=out_rows, out_offset=tok(ap=sidx[job.eh][0:m, t:t + 1], axis=0),
                                         in_=ob[t % 3][0:m, :], in_offset=None, compute_op=ALU.add)\
                        .then_inc(s[f"scat{t % 3}"], 16)
            po.wait_ge(s["cls_st"], 48)
            for q in range(2):
                po.wait_ge(s[f"base_st{q}"], 16 * NB // 2)
                po.wait_ge(s[f"yp_st{q}"], 16 * NB // 2)
            po.wait_ge(s["vt_st"], 32)
            gather(Job(0, 0))

            def emit(prev, cur, nxt, _tiles):
                if prev:
                    scatter(prev)
                if nxt and cur.q_next and cur.c != 1:
                    low(1 - cur.eh, cur.q + 1, cur.c // 2)
                if cur and cur.c == 0 and cur.q_next:
                    gather(Job(cur.el, cur.eh * 3 + 3))
            jobs(po, emit)

        @block.scalar
        def _(act):
            act.dma_start(bandb[:, 0:1], ba.unsqueeze(0).partition_broadcast(NB).rearrange("p a b -> p (a b)"))\
                .then_inc(s["ld_bias"], 16)
            for q, b in ((1, bd1), (4, bd2), (7, bd3)):
                act.dma_start(bandb[:, q:q + 3], b.unsqueeze(0).partition_broadcast(NB)
                              .rearrange("p a b -> p (a b)")).then_inc(s["ld_bias"], 16)
            A = nc.scalar
            for h in range(NH):
                for n, levels in enumerate(((1, 3), (2,))):
                    act.wait_ge(s["rep"], 2 * h + n + 1)
                    for lv in levels:
                        last = A.activation(bsum[h][lv], RB[h][lv][1], ACT.Copy)
                    last.then_inc(s["wp_v"], 1)
            act.wait_ge(s["cls_d"], 3)
            A.activation(cgl[:, :], cgl[:, :], ACT.Tanh).then_inc(s["cls_a"], 1)
            act.wait_ge(s["z_c"], 3)
            A.activation(z2[:, 1:NJ], z2[:, 1:NJ], ACT.Exp)
            A.activation(z2[:, 0:1], zz[:, 0:1], ACT.Exp, scale=-1.0).then_inc(s["z_e"], 1)

            def emit(t, _nxt, _a, b, c, d, m):
                if d:
                    after(act, "pt", d.n - 1)
                    after(act, "u", d.n - 1)
                    after(act, "rv", d.n - 1)
                    act.wait_ge(s["nmax"], d.n + 1)
                    A.activation(Pr[d.p][:, 0:129], Sb[:, 0:129], ACT.Exp, bias=nmx[d.p][:, 0:1],
                                 accum_out=rsm[d.p][:, 0:1])
                    A.activation(Pr[d.p][:, 129:386], Sb[:, 129:386], ACT.Exp, bias=nmx[d.p][:, 1:2],
                                 accum_out=rsm[d.p][:, 1:2]).then_inc(s["pexp"], 1)
                if c:
                    after(act, "sm", c.n - 1)
                    act.wait_ge(s["et"], c.n + 1)
                    A.activation(ET[c.p][:, :, 1:NT], Tb[:, :].rearrange("p (c t) -> p c t", c=2), ACT.Copy)\
                        .then_inc(s["et_ev"], 1)
                if d:
                    after(act, "av", d.n - 1)
                    act.wait_ge(s["pt"], d.n + 1)
                    A.activation(PTS[d.p][:, :], Pb[:, 0:384], ACT.Copy).then_inc(s["pt_ev"], 1)
                if b:
                    after(act, "h1", b.n - 3)
                    act.wait_ge(s["st0_b"], b.n + 1)
                    A.activation(hc[b.r][:, :, :], Hb[:, :].rearrange("p (h c) -> p h c", h=NH), ACT.Copy)
                if c:
                    act.wait_ge(s["er"], c.n + 1)
                    A.activation(ERT[c.p][:, :, :], Rb[:, :].rearrange("p (c t) -> p c t", c=2), ACT.Copy)\
                        .then_inc(s["er_ev"], 1)
                if b:
                    after(act, "av", b.n - 3)
                    act.wait_ge(s["nrm"], t.n + 1)
                    for h in range(NH):
                        last = A.activation(Ex[b.r][:, h, 0:D], Hb[:, h * D:(h + 1) * D], ACT.Identity,
                                            bias=N6[t.p][:, h:h + 1], scale=ST[t.p][:, 8 + h:9 + h])
                    last.then_inc(s["hcE"], 1)
                if m:
                    after(act, f"yp_st{m.p}", m.h * 16)
                    act.wait_ge(s["nrm"], t.n + 1)
                    for h in range(NH):
                        last = A.activation(Yp[m.p][:, h, :], H1[m.p][:, h, :], ACT.Identity,
                                            bias=N6[t.p][:, 4 + h:5 + h], scale=ST[t.p][:, 12 + h:13 + h])
                    last.then_inc(s["yp"], 1)
                    after(act, f"base_st{m.p}", m.h * 16)
                    for h in range(NH):
                        last = A.activation(Bs[m.p][:, h, :], H1[m.p][:, h, :], ACT.Identity,
                                            bias=N6[t.p][:, 2 + h:3 + h], scale=O1[t.p][:, h:h + 1])
                    last.then_inc(s["base"], 1)
            steps(act, emit)

            def high(eh, q, layer):
                hi = (w1s, w2s)[layer][eh][0]
                act.wait_ge(s["wld"], (q * 2 + layer + 1) * 16)
                A.activation(hi[:, :, :].rearrange("p a b -> p (a b)"), raw[:, :], ACT.Copy).then_inc(s["whi"], 1)

            def high_rows(job):
                act.wait_ge(s["yr"], job.j + 1)
                after(act, "hmm", job.j * 8)
                A.activation(yT[0][:, :, 0:job.w], yr[:, :, 0:job.w], ACT.Copy).then_inc(s["yhi"], 1)
            act.wait_ge(s["gt_c"], 6)
            A.activation(GM[:, :, :, :], GL[:, :, :, :], ACT.Tanh).then_inc(s["gt_t"], 1)

            def emit(prev, cur, nxt, _tiles):
                if cur:
                    for f in range(8):
                        n = cur.j * 8 + f + 1
                        after(act, "hlo", n - 2)
                        act.wait_ge(s["hmm"], n)
                        apart(act)
                        A.activation(hr[f % 2][:, 0:cur.w], Lb[f % 3][:, 0:cur.w], ACT.Gelu_apprx_tanh,
                                     bias=b1s[:, bass.ds(cur.e, 1), f]).then_inc(s["hact"], 1)
                        act.wait_ge(s["hact"], n)
                        A.activation(hT[cur.p][0][:, f, 0:cur.w], hr[f % 2][:, 0:cur.w], ACT.Copy)\
                            .then_inc(s["hhi"], 1)
                if nxt:
                    high_rows(nxt)
                if cur and cur.q_next and cur.c != 1:
                    high(1 - cur.eh, cur.q + 1, cur.c // 2)
                if prev:
                    for t in range(prev.t0, prev.t1):
                        m = SLOTS[t]
                        if prev.c < 2:
                            act.wait_ge(s["oadd"], prev.q * 6 + t + 1)
                            src = ot[t % 2][0:m, :]
                        else:
                            act.wait_ge(s["obk"], prev.q + 1)
                            src = back_bank(t)[0:m, :]
                        after(act, f"scat{t % 3}", (prev.q * 3 + t // 3) * 16)
                        apart(act)
                        A.activation(ob[t % 3][0:m, :], src, ACT.Copy,
                                     scale=yg[prev.eh][0:m, t, bass.ds(prev.e + D, 1)]).then_inc(s["omul"], 1)
            act.wait_ge(s["xc"], NB)
            high(0, 0, 0)
            high(0, 0, 1)
            act.wait_ge(s["ld_par"], 96)
            high_rows(Job(0, 0))
            jobs(act, emit)

        @block.tensor
        def _(pe):
            T = nc.tensor
            pe.wait_ge(s["ld_const"], 16)

            def repeat(lv, h, out_, k):
                r = D >> lv + 1
                if lv == 3:
                    w, src = cst("rep3")[0:32, h * P:(h + 1) * P], slice(0, 32)
                else:
                    w, src = cst(f"rep{lv}")[h * r:(h + 1) * r, :], slice(h * r, (h + 1) * r)
                return T.matmul(out_, w, (bandA[src, :] if k is None else band[lv][src, k, :]), start=True, stop=True)
            for h in range(NH):
                for lv in (1, 3):
                    if h == 0:
                        pe.wait_ge(s[f"ld_band{lv}"], 16)
                    for k in range(3):
                        repeat(lv, h, RB[h][lv][k], k)
                if h == 0:
                    pe.wait_ge(s["ld_band0"], 16)
                repeat(3, h, RA[h], None).then_inc(s["rep"], 1)
                if h == 0:
                    pe.wait_ge(s["ld_band2"], 16)
                else:
                    pe.wait_ge(s["wp"], 1)
                for k in range(3):
                    last = repeat(2, h, RB[h][2][k], k)
                last.then_inc(s["rep"], 1)
            ng = D // CG
            for h in range(NH):
                pe.wait_ge(s["wp"], h + 1)
                for c in range(ng):
                    if c % (ng // 2) == 0:
                        pe.wait_ge(s[f"ld_x{2 * h + c // (ng // 2)}"], 16)
                    last = T.matmul(Zb[0:CG * NJ, 0:NB * CG], WP[:, h, c * CG:(c + 1) * CG, :].rearrange("p c j -> p (c j)"),
                                    XS[:, h, c, :, :].rearrange("p b c -> p (b c)"),
                                    start=(h == 0 and c == 0), stop=(h == NH - 1 and c == ng - 1))
            last.then_inc(s["lg_mm"], 1)
            pe.wait_ge(s["cls_t"], 1)
            for c in range(2):
                last = T.transpose(Tb[:, c * P:(c + 1) * P], CX[:, c * P:(c + 1) * P], ident)
            last.then_inc(s["et0"], 1)
            pe.wait_ge(s["lg_r"], 1)
            T.matmul(Hb[0:NB, 0:NJ], lgr[:, :], cst("pick")[0:CG * NJ, :], start=True, stop=True).then_inc(s["z_mm"], 1)
            pe.wait_ge(s["bw_t"], 1)
            T.transpose(Hb[0:NJ, 32:32 + NB], bw[:, :], ident[0:NB, 0:NB]).then_inc(s["z_mm"], 1)
            pe.wait_ge(s["bw_c"], 1)
            for q in range(LEAF):
                last = T.matmul(Hb[:, 128 + q * NB:128 + (q + 1) * NB], cst("spread")[0:NJ, q * P:(q + 1) * P],
                                bwT[:, :], start=True, stop=True)
            last.then_inc(s["w8_mm"], 1)
            pe.wait_ge(s["cvt"], 1)
            pe.wait_ge(s["ld_par"], 96)

            def emit(_t, _nxt, a, b, c, d, _m):
                if b:
                    after(pe, "hcE", b.n)
                    pe.wait_ge(s["q"], b.n + 1)
                    T.matmul(Hb[:, :], cst("inv"), Q[b.p].rearrange("p h c -> p (h c)"), start=True, stop=True)\
                        .then_inc(s["h0"], 1)
                if c:
                    after(pe, "et_ev", c.n)
                    pe.wait_ge(s["hcE"], c.n + 1)
                    for j in range(2):
                        for h in range(NH):
                            last = T.transpose(Tb[:, j * D + h * P:j * D + (h + 1) * P],
                                               Ex[c.r][:, h, j * P:(j + 1) * P], ident)
                    last.then_inc(s["et"], 1)
                if a:
                    after(pe, "zw", a.n * 2)
                    pe.wait_ge(s["xc"], a.n + 1)
                    T.matmul(Zb[:, :], cst("fwd"), Xc[a.p].rearrange("p h c -> p (h c)"), start=True, stop=True)\
                        .then_inc(s["z_done"], 1)
                if d:
                    after(pe, "pt_ev", d.n)
                    pe.wait_ge(s["eg_ev"], d.n + 1)
                    pe.wait_ge(s["pexp"], d.n + 1)
                    for q, c0 in enumerate((1, 130, 258)):
                        last = T.transpose(Pb[:, q * P:(q + 1) * P], Pr[d.p][:, c0:c0 + P], ident)
                    last.then_inc(s["pt"], 1)
                if c:
                    after(pe, "er_ev", c.n)
                    pe.wait_ge(s["et_ev"], c.n + 1)
                    for e in range(2):
                        for j in range(2):
                            last = T.matmul(Rb[:, e * D:(e + 1) * D], Rw[:, j, e * P:(e + 1) * P],
                                            ET[c.p][:, j, 1:NT], start=(j == 0), stop=(j == 1))
                    last.then_inc(s["er"], 1)
                if d:
                    after(pe, "u", d.n)
                    pe.wait_ge(s["pt_ev"], d.n + 1)
                    T.matmul(Ab[0][:, 0:DG], PTS[d.p][:, 0:P], Ex[d.r][:, 0, :], start=True, stop=True)
                    T.matmul(Ab[1][:, 0:DG], PTS[d.p][:, P:2 * P], Ex[d.r][:, 0, :], start=True, stop=False)
                    T.matmul(Ab[1][:, 0:DG], PTS[d.p][:, 2 * P:3 * P], Ex[d.r][:, 1, :], start=False, stop=True)\
                        .then_inc(s["av"], 1)
                if c:
                    for h in range(NH):
                        for j in range(2):
                            last = T.matmul(Pb[:, 400 + h * NE:400 + (h + 1) * NE],
                                            ET[c.p][:, j, 1 + h * P:1 + (h + 1) * P], gwT[:, j, :],
                                            start=(j == 0), stop=(j == 1))
                    last.then_inc(s["eg"], 1)
                    after(pe, "pexp", c.n)
                    pe.wait_ge(s["er_ev"], c.n + 1)
                    for h, (c0, w) in enumerate(((0, 129), (129, 257))):
                        for j in range(2):
                            T.matmul(Sb[:, c0:c0 + w], ERT[c.p][:, j, h * P:(h + 1) * P], ET[c.p][:, j, 0:w],
                                     start=(j == 0), stop=False)
                        last = T.matmul(Sb[:, c0 + w - P:c0 + w], identb[:, :], causalb[:, :], start=False, stop=True)
                    last.then_inc(s["sm"], 1)
            steps(pe, emit)

            pe.wait_ge(s["vsp_t"], 1)
            for h in range(NH):
                for eh in range(2):
                    q = 2 * h + eh
                    last = T.transpose(bank[0][:, q * P:(q + 1) * P],
                                       GV[:, h, eh, :, :].rearrange("p e b -> p (e b)"), ident)
            last.then_inc(s["vsp"], 1)
            with pe.Fori(0, BITS // TESTS) as i:
                for u in range(TESTS):
                    pe.wait_ge(s["cn"], i * TESTS + u + 1)
                    T.matmul(bank[1][:, 0:2], sameh[:, :], cnt[:, :], start=True, stop=True).then_inc(s["thr"], 1)
            pe.wait_ge(s["tk_c"], 1)
            T.matmul(bank[2][:, 0:2], cst("same"), cgt[:, :], start=True, stop=True)
            T.matmul(bank[3][:, 0:2], cst("before"), tot[:, :], start=True, stop=True).then_inc(s["tk_mm"], 1)
            pe.wait_ge(s["tk_c"], 2)
            T.matmul(bank[4][:, 0:2], cst("before"), tot[:, :], start=True, stop=True).then_inc(s["tk_mm"], 1)

            def place(job, t):
                n, m = job.q * 9 + t, SLOTS[t]
                if t == 0:
                    pe.wait_ge(s["ohd"], job.q + 1)
                after(pe, "smc", n - 1 if isinstance(job.q, int) and job.q == 0 else n)
                T.matmul(place_bank(job, t)[0:m, 0:NT + 3], oh[:, t * P:t * P + m], TB[:, job.eh, :], start=True,
                         stop=True).then_inc(s["smm"], 1)

            def turn(job):
                after(pe, "yt", job.j)
                pe.wait_ge(s[f"gat{job.eh}{job.c}"], 48 * (job.el + 1))
                for d in range(2):
                    for t in range(job.t0, job.t1):
                        m, at = SLOTS[t], (t - job.t0) * P
                        last = T.transpose(bank[2 + d][:, at:at + m], yg[job.eh][0:m, t, d * P:(d + 1) * P],
                                           ident[0:m, 0:m])
                last.then_inc(s["yt_t"], 1)

            def emit(prev, cur, nxt, tiles):
                if cur:
                    if cur.c == 0:
                        pe.wait_ge(s["wlo"], cur.q * 2 + 1)
                    pe.wait_ge(s["yt"], cur.j + 1)
                    for f in range(8):
                        after(pe, "hact", cur.j * 8 + max(0, f - 2))
                        if f == 2 and isinstance(cur.j, int) and cur.j == 0:
                            pe.wait_ge(s["smc"], 9)
                        for n, (d, i, k) in enumerate((d, i, k) for d in range(2) for i, k in PARTS):
                            last = T.matmul(Lb[f % 3][:, 0:cur.w], w1s[cur.eh][i][:, d, f * P:(f + 1) * P],
                                            yT[k][:, d, 0:cur.w], start=(n == 0), stop=(n == 5))
                        last.then_inc(s["hmm"], 1)
                        for tile in spread(early(prev, tiles), f, 8):
                            place(*tile)
                if nxt:
                    turn(nxt)
                if prev:
                    if prev.c == 0:
                        pe.wait_ge(s["wlo"], prev.q * 2 + 2)
                    pe.wait_ge(s["hlo"], (prev.j + 1) * 8)
                    for t in range(prev.t0, prev.t1) if prev.c < 2 else ():
                        at = (t - prev.t0) * P
                        after(pe, "oadd", prev.q * 6 + t - 1)
                        if t < 2:
                            after(pe, "omul", prev.q * 9)
                        for n, (f, i, k) in enumerate((f, i, k) for f in range(8) for i, k in PARTS):
                            last = T.matmul(bank[4 + t % 2][:, 0:D], hT[prev.p][i][:, f, at:at + P],
                                            w2s[prev.eh][k][:, f, :], start=(n == 0), stop=(n == 23))
                        last.then_inc(s["om"], 1)
                        for tile in spread(tiles[-3:], t - prev.t0, 3):
                            place(*tile)
                    if prev.c == 2:
                        for d in range(2):
                            after(pe, "oadd", prev.q * 6 + 5 + d)
                            for n, (f, i, k) in enumerate((f, i, k) for f in range(8) for i, k in PARTS):
                                last = T.matmul(bank[4 + d][:, 0:TAIL_W], w2s[prev.eh][i][:, f, d * P:(d + 1) * P],
                                                hT[prev.p][k][:, f, 0:TAIL_W], start=(n == 0), stop=(n == 23))
                            last.then_inc(s["omt"], 1)
                            for tile in spread(tiles, d, 2):
                                place(*tile)
                        pe.wait_ge(s["oev"], prev.q * 2 + 2)
                        for d in range(2):
                            for t in range(prev.t0, prev.t1):
                                m, at = SLOTS[t], (t - prev.t0) * P
                                last = T.transpose(back_bank(t)[0:m, d * P:(d + 1) * P], oT[:, d, at:at + m], ident)
                        last.then_inc(s["obk"], 1)
            pe.wait_ge(s["tc"], 1)
            for t in range(9):
                place(Job(0, 0), t)
                if t == 5:
                    turn(Job(0, 0))
            jobs(pe, emit)

        @block.vector
        def _(dve):
            v = nc.vector
            dve.wait_ge(s["ld_const"], 16)
            v.tensor_copy(identb[:, :], ident)
            v.tensor_copy(sameh[:, :], cst("same"))
            v.tensor_copy(causalb[:, :], cst("causal")).then_inc(s["cvt"], 1)
            parts = [0]

            def weights_as_image(lv, h):
                B, sign = RB[h][lv], cst("sign")[:, lv - 1:lv]
                bs = bsum[h][lv]
                v.scalar_tensor_tensor(out=bs, in0=B[2], scalar=sign, in1=bs, op0=ALU.mult, op1=ALU.add)\
                    .then_inc(s["wp_part"], 1)
                parts[0] += 1
                dve.wait_ge(s["wp_part"], parts[0])
                j0 = 1 + 3 * (3 - lv)
                dst = WP[:, h, :, j0:j0 + 3].rearrange("p (x s u) j -> p x s u j", x=D >> lv, s=2)
                for q, op in ((0, ALU.add), (1, ALU.subtract)):
                    for u in range(1 << (lv - 1)):
                        last = v.scalar_tensor_tensor(out=dst[:, :, q, u, :], in0=B[0].rearrange("p (x j) -> p x j", j=3),
                                                      scalar=sign, in1=bs.rearrange("p (x j) -> p x j", j=3),
                                                      op0=ALU.mult, op1=op)
                return last
            for h in range(NH):
                dve.wait_ge(s["wp_v"], 2 * h + 1)
                weights_as_image(1, h)
                weights_as_image(3, h)
                v.tensor_copy(WP[:, h, :, 0:1].rearrange("p (x u) j -> p x (u j)", u=8),
                              RA[h].unsqueeze(2).to_broadcast([P, 32, 8]))
                dve.wait_ge(s["wp_v"], 2 * h + 2)
                last = weights_as_image(2, h)
                last.then_inc(s["wp"], 1)
            dve.wait_ge(s["ld_cls"], 32)
            k = [0]

            def link(ins):
                k[0] += 1
                ins.then_inc(s["cls_t2"], 1)
                dve.wait_ge(s["cls_t2"], k[0])
            s["cls_t2"] = sem("cls_chain")
            link(v.bn_stats(cbn[:, :], clsb[:, :]))
            link(v.bn_aggr(cst8[:, 0:2], cbn[:, :]))
            v.tensor_scalar(cst8[:, 2:3], cst8[:, 1:2], EPS, None, ALU.add).then_inc(s["cls_d"], 1)
            v.tensor_reduce(sg[:, :], gwb[:, :, :], AX_X, ALU.add)
            dve.wait_ge(s["cls_p"], 1)
            link(v.tensor_scalar(CX[:, 0:D], clsb[:, :], cst8[:, 0:1], cst8[:, 3:4], ALU.subtract, ALU.mult))
            for e in range(NE):
                last = v.tensor_tensor_reduce(out=junk[:, :], in0=CX[:, 0:D], in1=gwb[:, e, :], scale=1.0, scalar=0.0,
                                              op0=ALU.mult, op1=ALU.add, accum_out=CX[:, D + e:D + e + 1])
                last = link(last)
            link(v.tensor_tensor(ch[:, 0:D], clsb[:, :], CX[:, 0:D], ALU.add))
            v.tensor_copy(junk[:, 0:1], CX[:, 0:1]).then_inc(s["cls_t"], 1)
            link(v.bn_stats(cbn[:, :], ch[:, 0:D]))
            for e in range(NE):
                link(v.tensor_tensor_reduce(out=junk[:, :], in0=ch[:, 0:D], in1=gwb[:, e, :], scale=1.0, scalar=0.0,
                                            op0=ALU.mult, op1=ALU.add, accum_out=ch[:, D + e:D + e + 1]))
            link(v.bn_aggr(cst8[:, 4:6], cbn[:, :]))
            v.tensor_scalar(cpw[:, 0:1], cst8[:, 5:6], EPS, None, ALU.add)
            v.tensor_scalar(cpw[:, 1:2], cst8[:, 5:6], 1.0 + EPS, EPS * EPS, ALU.mult, ALU.add).then_inc(s["cls_d"], 1)
            dve.wait_ge(s["cls_p"], 2)
            link(v.tensor_scalar(cyp[:, :], ch[:, 0:D], cst8[:, 4:5], cpw[:, 2:3], ALU.subtract, ALU.mult))
            v.tensor_tensor(cbs[:, :], cyp[:, :], ch[:, 0:D], ALU.add)
            link(v.tensor_scalar(cgl[:, :], sg[:, :], cst8[:, 4:5], None, ALU.mult))
            link(v.tensor_tensor(cgl[:, :], ch[:, D:DG], cgl[:, :], ALU.subtract))
            link(v.tensor_scalar(cgl[:, :], cgl[:, :], cpw[:, 2:3], None, ALU.mult))
            v.tensor_scalar(cyp[:, :], ch[:, 0:D], cst8[:, 4:5], cpw[:, 3:4], ALU.subtract, ALU.mult)\
                .then_inc(s["cls_d"], 1)
            dve.wait_ge(s["cls_a"], 1)
            v.tensor_scalar(vcls[:, :], cgl[:, :], 1.0, 0.5, ALU.add, ALU.mult).then_inc(s["cls_g"], 1)
            dve.wait_ge(s["cls_g"], 1)
            v.memset(one[:, :], 1.0)
            v.memset(Tv[:, :], 0.0)
            v.memset(Tc[:, :], 1.0)
            v.memset(bit[:, :], 1.0)
            for e in range(4):
                for eh in range(2):
                    v.tensor_copy(V[32 * e:32 * e + 32, eh, 0:1], vcls[32 * e:32 * e + 32, 4 * eh + e:4 * eh + e + 1])
            dve.wait_ge(s["lg_mm"], 1)
            v.tensor_tensor(LM[:, :, :], Zb[0:CG * NJ, 0:NB * CG].rearrange("p (b c) -> p b c", c=CG),
                            cst("diag")[0:CG * NJ, :].unsqueeze(1).to_broadcast([CG * NJ, NB, CG]), ALU.mult)\
                .then_inc(s["lg_m"], 1)
            dve.wait_ge(s["lg_m"], 1)
            v.tensor_reduce(lgr[:, :], LM[:, :, :], AX_X, ALU.add).then_inc(s["lg_r"], 1)
            dve.wait_ge(s["et0"], 1)
            for q in range(2):
                last = v.tensor_copy(ET[q][:, :, 0], Tb[:, 0:D].rearrange("p (c t) -> p c t", c=2)[:, :, 0])
            link(last)
            for q in range(2):
                link(v.memset(ST[q][:, :], 1.0))
            dve.wait_ge(s["z_mm"], 1)
            dve.wait_ge(s["ld_bias"], 64)
            v.tensor_tensor(zz[:, :], Hb[0:NB, 0:NJ], bandb[:, :], ALU.add).then_inc(s["z_c"], 1)
            dve.wait_ge(s["z_c"], 1)
            v.tensor_reduce(mx3[:, :], zz[:, 1:NJ].rearrange("p (l j) -> p l j", j=3), AX_X, ALU.max)\
                .then_inc(s["z_c"], 1)
            dve.wait_ge(s["z_c"], 2)
            v.tensor_tensor(z2[:, 1:NJ].rearrange("p (l j) -> p l j", j=3), zz[:, 1:NJ].rearrange("p (l j) -> p l j", j=3),
                            mx3[:, :].unsqueeze(2).to_broadcast([NB, 3, 3]), ALU.subtract).then_inc(s["z_c"], 1)
            dve.wait_ge(s["z_e"], 1)
            v.tensor_reduce(mx3[:, :], z2[:, 1:NJ].rearrange("p (l j) -> p l j", j=3), AX_X, ALU.add)
            link(v.tensor_scalar(bw[:, 0:1], z2[:, 0:1], 1.0, None, ALU.add))
            v.reciprocal(mx3[:, :], mx3[:, :])
            link(v.reciprocal(bw[:, 0:1], bw[:, 0:1]))
            v.tensor_tensor(bw[:, 1:NJ].rearrange("p (l j) -> p l j", j=3), z2[:, 1:NJ].rearrange("p (l j) -> p l j", j=3),
                            mx3[:, :].unsqueeze(2).to_broadcast([NB, 3, 3]), ALU.mult).then_inc(s["bw_t"], 1)
            dve.wait_ge(s["z_mm"], 2)
            v.tensor_copy(bwT[:, :], Hb[0:NJ, 32:32 + NB]).then_inc(s["bw_c"], 1)
            dve.wait_ge(s["w8_mm"], 1)
            for q, (c0, c1) in enumerate(((0, 1), (1, 2), (2, 4), (4, 8))):
                last = v.tensor_copy(W8[:, :, c0:c1],
                                     Hb[:, 128 + q * NB:128 + (q + 1) * NB].unsqueeze(2).to_broadcast([P, NB, c1 - c0]))
            last.then_inc(s["w8"], 1)
            dve.wait_ge(s["w8"], 1)
            def emit(t, _nxt, a, b, c, d, m):
                st = ST[t.p]
                after(dve, "tab", t.n - 1)
                if b:
                    dve.wait_ge(s["h0"], b.n + 1)
                    for h in range(NH):
                        last = v.bn_stats(bn0[:, h, :], Hb[:, h * D:(h + 1) * D])
                    last.then_inc(s["st0_b"], 1)
                if d:
                    dve.wait_ge(s["eg_ev"], d.n + 1)
                    v.tensor_copy(TEG[:, bass.ds(d.n, 1), :, :].rearrange("p b h e -> p (b h) e"), Ex[d.r][:, :, D:DG])\
                        .then_inc(s["teg"], 1)
                if b:
                    dve.wait_ge(s["st0_b"], b.n + 1)
                    apart(dve)
                    for h in range(NH):
                        last = v.bn_aggr(st[:, 2 * h:2 + 2 * h], bn0[:, h, :])
                    last.then_inc(s["st0"], 1)
                if d:
                    dve.wait_ge(s["pexp"], d.n + 1)
                    after(dve, "tab", t.n)
                    v.reciprocal(ST[1 - t.p][:, 14:16], rsm[d.p][:, :]).then_inc(s["rv"], 1)
                if b:
                    dve.wait_ge(s["st0"], b.n + 1)
                if m:
                    dve.wait_ge(s["st1"], m.n + 1)
                after(dve, "pow", t.n)
                v.tensor_scalar(A6[:, 0:4], st[:, 1:8:2], EPS, None, ALU.add)
                v.tensor_scalar(A6[:, 4:6], st[:, 5:8:2], 1.0 + EPS, EPS * EPS, ALU.mult, ALU.add)\
                    .then_inc(s["var"], 1)
                if a:
                    dve.wait_ge(s["z_done"], a.n + 1)
                    for g0, g1 in ((0, 2), (2, 8)):
                        w = W8[:, bass.ds(a.n, 1), g0:g1].to_broadcast([P, NH, g1 - g0]).unsqueeze(3)\
                            .to_broadcast([P, NH, g1 - g0, 32])
                        v.tensor_tensor(Zw.rearrange("p h (g c) -> p h g c", g=8)[:, :, g0:g1, :],
                                        Zb[:, :].rearrange("p (h g c) -> p h g c", h=NH, g=8)[:, :, g0:g1, :], w,
                                        ALU.mult).then_inc(s["zw"], 1)
                    dve.wait_ge(s["zw"], a.n * 2 + 1)
                    lo, hi = Zw[:, :, 0:32], Zw[:, :, 32:64]
                    v.tensor_tensor(I2[:, :, 0::2], lo, hi, ALU.add)
                    v.tensor_tensor(I2[:, :, 1::2], lo, hi, ALU.subtract).then_inc(s["inv"], 1)
                    dve.wait_ge(s["zw"], a.n * 2 + 2)
                    dve.wait_ge(s["inv"], a.n * 2 + 1)
                    hi = Zw[:, :, 64:128]
                    v.tensor_tensor(I1[:, :, 0::2], I2[:, :, :], hi, ALU.add)
                    v.tensor_tensor(I1[:, :, 1::2], I2[:, :, :], hi, ALU.subtract).then_inc(s["inv"], 1)
                if b:
                    after(dve, "hcE", b.n - 1)
                dve.wait_ge(s["pow"], t.n + 1)
                v.scalar_tensor_tensor(out=N6[t.p][:, 0:4], in0=st[:, 8:12], scalar=-1.0, in1=st[:, 0:8:2],
                                       op0=ALU.mult, op1=ALU.mult)
                v.scalar_tensor_tensor(out=N6[t.p][:, 4:6], in0=st[:, 12:14], scalar=-1.0, in1=st[:, 4:8:2],
                                       op0=ALU.mult, op1=ALU.mult)
                v.tensor_scalar(O1[t.p][:, :], st[:, 10:12], 1.0, None, ALU.add).then_inc(s["nrm"], 1)
                if a:
                    dve.wait_ge(s["inv"], a.n * 2 + 2)
                    after(dve, "h0", a.n - 1)
                    hi = Zw[:, :, 128:256]
                    v.tensor_tensor(Q[a.p][:, :, 0::2], I1[:, :, :], hi, ALU.add)
                    v.tensor_tensor(Q[a.p][:, :, 1::2], I1[:, :, :], hi, ALU.subtract).then_inc(s["q"], 1)
                if d:
                    st_next = ST[1 - t.p]
                    dve.wait_ge(s["av"], d.n + 1)
                    for h in range(NH):
                        last = v.scalar_tensor_tensor(out=U[d.p][:, h, :], in0=CX[:, :],
                                                      scalar=Pr[d.p][:, 129 * h:129 * h + 1],
                                                      in1=Ab[h][:, 0:DG], op0=ALU.mult, op1=ALU.add)
                    last.then_inc(s["u"], 1)
                    after(dve, "base", d.n - 1)
                    dve.wait_ge(s["u"], d.n + 1)
                    dve.wait_ge(s["rv"], d.n + 1)
                    for h in range(NH):
                        last = v.scalar_tensor_tensor(out=H1[d.p][:, h, :], in0=U[d.p][:, h, 0:D],
                                                      scalar=st_next[:, 14 + h:15 + h], in1=hc[d.r][:, h, :],
                                                      op0=ALU.mult, op1=ALU.add)
                    last.then_inc(s["h1"], 1)
                if c:
                    dve.wait_ge(s["eg"], c.n + 1)
                    v.tensor_copy(Ex[c.r][:, :, D:DG], Pb[:, 400:416].rearrange("p (h e) -> p h e", h=NH))\
                        .then_inc(s["eg_ev"], 1)
                    dve.wait_ge(s["sm"], c.n + 1)
                    v.tensor_reduce(nmx[c.p][:, 0:1], Sb[:, 0:129], AX_X, ALU.max, negate=True)
                    v.tensor_reduce(nmx[c.p][:, 1:2], Sb[:, 129:386], AX_X, ALU.max, negate=True)\
                        .then_inc(s["nmax"], 1)
                if d:
                    dve.wait_ge(s["h1"], d.n + 1)
                    for h in range(NH):
                        last = v.bn_stats(bn1[:, h, :], H1[d.p][:, h, :])
                    last.then_inc(s["st1_b"], 1)
                    v.tensor_copy(TUG[:, bass.ds(d.n, 1), :, :].rearrange("p b h e -> p (b h) e"), U[d.p][:, :, D:DG])\
                        .then_inc(s["tug"], 1)
                    dve.wait_ge(s["st1_b"], d.n + 1)
                    apart(dve)
                    for h in range(NH):
                        last = v.bn_aggr(ST[1 - t.p][:, 4 + 2 * h:6 + 2 * h], bn1[:, h, :])
                    last.then_inc(s["st1"], 1)
            steps(dve, emit)

            dve.wait_ge(s["tab"], NB + LAG)
            dve.wait_ge(s["tug"], NB)
            dve.wait_ge(s["teg"], NB)
            sh = [P, NB, NH, NE]

            def col(a, b, step=1, late=LAG):
                return TST[:, late:late + NB, a:b:step]

            def wide(ap):
                return ap.unsqueeze(3).to_broadcast(sh)
            v.tensor_scalar(sd0[:, :, :], col(1, 4, 2, 1), EPS, None, ALU.add)
            v.tensor_tensor(dm[:, :, :], col(0, 4, 2, 1), col(4, 8, 2), ALU.subtract)
            v.tensor_tensor(GL[:, :, :, :], TUG[:, :, :, :], wide(col(14, 16)), ALU.mult).then_inc(s["gt_c"], 1)
            dve.wait_ge(s["gt_c"], 1)
            v.tensor_tensor(sd0[:, :, :], sd0[:, :, :], col(8, 10, 1, 1), ALU.mult).then_inc(s["gt_c"], 1)
            v.tensor_tensor(GM[:, :, :, :], wide(dm[:, :, :]),
                            sg[:, :].unsqueeze(1).to_broadcast([P, NB * NH, NE]).rearrange("p (b h) e -> p b h e", h=NH),
                            ALU.mult)
            dve.wait_ge(s["gt_c"], 2)
            v.tensor_tensor(TEG[:, :, :, :], TEG[:, :, :, :], wide(sd0[:, :, :]), ALU.mult).then_inc(s["gt_c"], 1)
            dve.wait_ge(s["gt_c"], 3)
            v.tensor_tensor(GL[:, :, :, :], GL[:, :, :, :], TEG[:, :, :, :], ALU.add).then_inc(s["gt_c"], 1)
            dve.wait_ge(s["gt_c"], 4)
            v.tensor_tensor(GL[:, :, :, :], GL[:, :, :, :], GM[:, :, :, :], ALU.add).then_inc(s["gt_c"], 1)
            dve.wait_ge(s["gt_c"], 5)
            v.tensor_tensor(GL[:, :, :, :], GL[:, :, :, :], wide(col(10, 12)), ALU.mult).then_inc(s["gt_c"], 1)
            dve.wait_ge(s["gt_t"], 1)
            for h in range(NH):
                last = v.tensor_scalar(GV[:, h, :, :, :].rearrange("p a e b -> p (a e) b"),
                                       GM[:, :, h, :].rearrange("p b e -> p e b"), 1.0, 0.5, ALU.add, ALU.mult)
            last.then_inc(s["vsp_t"], 1)
            for h in range(NH):
                v.tensor_scalar(GL[:, :, h, :], GM[:, :, h, :], 1.0, 0.5, ALU.add, ALU.mult).then_inc(s["gt_v"], 1)
            dve.wait_ge(s["vsp"], 1)
            last = v.tensor_copy(V[:, :, 1:NT].rearrange("p a (h t) -> p a h t", h=NH),
                                 bank[0][:, :].rearrange("p (h a t) -> p a h t", h=NH, a=2))
            link(last)
            s["step"] = sem("search_step")
            def test(n):
                for eh in range(2):
                    last = v.tensor_scalar(ge[:, eh, :], V[:, eh, :], Tc[:, eh:eh + 1], None, ALU.is_ge, ALU.add,
                                           accum_out=cnt[:, eh:eh + 1])
                last.then_inc(s["cn"], 1)
                dve.wait_ge(s["step"], n * 6)
                v.scalar_tensor_tensor(out=Tn[:, :], in0=bit[:, :], scalar=0.5, in1=Tv[:, :], op0=ALU.mult, op1=ALU.add)\
                    .then_inc(s["step"], 1)
                dve.wait_ge(s["thr"], n + 1)
                v.scalar_tensor_tensor(out=mm2[:, :], in0=bank[1][:, 0:2], scalar=KTOK - 0.5, in1=bit[:, :],
                                       op0=ALU.is_ge, op1=ALU.mult).then_inc(s["step"], 1)
                v.scalar_tensor_tensor(out=Tp[:, :], in0=bank[1][:, 0:2], scalar=KTOK - 0.5, in1=Tc[:, :],
                                       op0=ALU.is_ge, op1=ALU.mult).then_inc(s["step"], 1)
                dve.wait_ge(s["step"], n * 6 + 3)
                v.tensor_tensor(Tc[:, :], Tn[:, :], mm2[:, :], ALU.add).then_inc(s["step"], 1)
                v.tensor_scalar(bit[:, :], bit[:, :], 0.5, None, ALU.mult).then_inc(s["step"], 1)
                v.tensor_tensor(Tv[:, :], Tv[:, :], Tp[:, :], ALU.max).then_inc(s["step"], 1)
                dve.wait_ge(s["step"], n * 6 + 4)
            with dve.Fori(0, BITS // TESTS) as i:
                for u in range(TESTS):
                    test(i * TESTS + u)
            dve.wait_ge(s["step"], BITS * 6)
            for eh in range(2):
                v.tensor_scalar(ge[:, eh, :], V[:, eh, :], Tv[:, eh:eh + 1], None, ALU.is_gt, ALU.add,
                                accum_out=cgt[:, eh:eh + 1])
                last = v.tensor_scalar(eq[:, eh, :], V[:, eh, :], Tv[:, eh:eh + 1], None, ALU.is_equal, ALU.add,
                                       accum_out=tot[:, eh:eh + 1])
            last.then_inc(s["tk_c"], 1)
            dve.wait_ge(s["tk_c"], 1)
            for eh in range(2):
                last = v.tensor_tensor_scan(sc[:, eh, :], one[:, :], eq[:, eh, :], 0.0, ALU.mult, ALU.add)
            dve.wait_ge(s["tk_mm"], 1)
            v.tensor_scalar(need[:, :], bank[2][:, 0:2], -1.0, float(KTOK), ALU.mult, ALU.add)
            link(v.tensor_copy(mm2[:, :], bank[3][:, 0:2]))
            link(v.tensor_tensor(need[:, :], need[:, :], mm2[:, :], ALU.subtract))
            for eh in range(2):
                last = v.scalar_tensor_tensor(out=eq[:, eh, :], in0=sc[:, eh, :], scalar=need[:, eh:eh + 1],
                                              in1=eq[:, eh, :], op0=ALU.is_le, op1=ALU.mult)
            link(last)
            link(v.tensor_tensor(ge[:, :, :], ge[:, :, :], eq[:, :, :], ALU.add))
            for eh in range(2):
                last = v.tensor_tensor_scan(sc[:, eh, :], one[:, :], ge[:, eh, :], 0.0, ALU.mult, ALU.add)
            link(last)
            v.tensor_copy(tot[:, :], sc[:, :, NT - 1]).then_inc(s["tk_c"], 1)
            v.tensor_tensor(TB[:, :, 0:NT], sc[:, :, :], ge[:, :, :], ALU.subtract)
            v.tensor_copy(TB[:, :, NT:NT + 1], cst("batch").unsqueeze(1).to_broadcast([P, 2, 1]))
            dve.wait_ge(s["tk_mm"], 2)
            link(v.tensor_scalar(beg[:, :], bank[4][:, 0:2], 1.0, None, ALU.mult))
            v.tensor_tensor(fin[:, :], beg[:, :], tot[:, :], ALU.add)
            link(v.tensor_copy(TB[:, :, NT + 1], beg[:, :]))
            link(v.tensor_copy(mm2[:, :], TB[:, :, NT + 1]))
            link(v.tensor_tensor(TB[:, :, NT + 2], beg[:, :], mm2[:, :], ALU.subtract))
            for e in range(2):
                last = v.tensor_tensor((begM, finM)[e][:, :, :], (beg, fin)[e][:, :].unsqueeze(1).to_broadcast([P, 5, 2]),
                                       cst("owner").unsqueeze(2).to_broadcast([P, 5, 2]), ALU.mult)
            last.then_inc(s["tc"], 1)
            dve.wait_ge(s["tc"], 1)

            s["ohu"] = sem("slots_begun")
            s["row"] = sem("row_chain")

            def one_hot(job):
                after(dve, "smm", job.q * 9)
                v.tensor_scalar(ohu[:, :], iot[:, :], begM[:, bass.ds(job.el, 1), job.eh], None, ALU.is_ge)\
                    .then_inc(s["ohu"], 1)
                dve.wait_ge(s["ohu"], job.q + 1)
                v.scalar_tensor_tensor(out=oh[:, :], in0=iot[:, :], scalar=finM[:, bass.ds(job.el, 1), job.eh],
                                       in1=ohu[:, :], op0=ALU.is_lt, op1=ALU.mult).then_inc(s["ohd"], 1)

            def place(job, t):
                m, n = SLOTS[t], job.q * 9 + t
                if t == 0:
                    if not isinstance(job.q, int) or job.q > 1:
                        for c in range(3):
                            dve.wait_ge(s[f"gat{job.eh}{c}"], 48 * job.el)
                        dve.wait_ge(s["idc"], job.q - 1)
                r0 = n * 3
                B = place_bank(job, t)
                dve.wait_ge(s["smm"], n + 1)
                v.tensor_copy(SM[0:m, t, :], B[0:m, NT:NT + 3]).then_inc(s["row"], 1)
                dve.wait_ge(s["row"], r0 + 1)
                v.scalar_tensor_tensor(out=rk[0:m, t:t + 1], in0=cst("slot")[0:m, t:t + 1], scalar=SM[0:m, t, 1:2],
                                       in1=SM[0:m, t, 2:3], op0=ALU.subtract, op1=ALU.subtract)\
                    .then_inc(s["row"], 1)
                dve.wait_ge(s["row"], r0 + 2)
                v.tensor_scalar(jk[0:m, :], B[0:m, 0:NT], rk[0:m, t:t + 1], None, ALU.is_le, ALU.add,
                                accum_out=pos[0:m, t:t + 1]).then_inc(s["smc"], 1)
                v.tensor_scalar(rowf[0:m, t:t + 1], SM[0:m, t, 0:1], float(NT), -1.0, ALU.mult, ALU.add)\
                    .then_inc(s["row"], 1)
                dve.wait_ge(s["smc"], n + 1)
                dve.wait_ge(s["row"], r0 + 3)
                v.tensor_tensor(idx[job.eh][0:m, t:t + 1], rowf[0:m, t:t + 1], pos[0:m, t:t + 1], ALU.add)\
                    .then_inc(s["ixd"], 1)
                if t == 8 and job.q_next:
                    one_hot(Job(job.el, job.eh * 3 + 3))

            def scaled(job):
                dve.wait_ge(s["yt_t"], job.j + 1)
                for d in range(2):
                    last = v.tensor_scalar(yr[:, d, 0:job.w], bank[2 + d][:, 0:job.w], gam[:, d:d + 1],
                                           bet[:, d:d + 1], ALU.mult, ALU.add)
                last.then_inc(s["yr"], 1)

            def low_rows(job):
                dve.wait_ge(s["yhi"], job.j + 1)
                v.tensor_tensor(yT[1][:, :, 0:job.w], yr[:, :, 0:job.w], yT[0][:, :, 0:job.w], ALU.subtract)\
                    .then_inc(s["yt"], 1)

            def emit(prev, cur, nxt, tiles):
                if cur:
                    for f in range(8):
                        n = cur.j * 8 + f + 1
                        dve.wait_ge(s["hhi"], n)
                        v.tensor_tensor(hT[cur.p][1][:, f, 0:cur.w], hr[f % 2][:, 0:cur.w],
                                        hT[cur.p][0][:, f, 0:cur.w], ALU.subtract).then_inc(s["hlo"], 1)
                        for tile in spread(early(prev, tiles), f, 8):
                            place(*tile)
                if nxt:
                    scaled(nxt)
                    if not prev:
                        low_rows(nxt)
                if prev:
                    if prev.c == 0:
                        dve.wait_ge(s[f"bld{prev.eh}"], (prev.el + 1) * 16)
                    for t in range(prev.t0, prev.t1) if prev.c < 2 else ():
                        m = SLOTS[t]
                        dve.wait_ge(s["om"], prev.q * 6 + t + 1)
                        if t < 2:
                            after(dve, "omul", prev.q * 9)
                        else:
                            dve.wait_ge(s["omul"], prev.q * 9 + t - 1)
                        v.tensor_tensor(ot[t % 2][0:m, :], bank[4 + t % 2][0:m, 0:D], b2b[prev.eh][0:m, :], ALU.add)\
                            .then_inc(s["oadd"], 1)
                        for tile in spread(tiles[-3:], t - prev.t0, 3):
                            place(*tile)
                        if nxt and t == prev.t0:
                            low_rows(nxt)
                    if prev.c == 2:
                        for d in range(2):
                            dve.wait_ge(s["omt"], prev.q * 2 + d + 1)
                            if d == 0:
                                after(dve, "obk", prev.q)
                            apart(dve)
                            v.tensor_scalar(oT[:, d, :], bank[4 + d][:, 0:TAIL_W], b2c[:, bass.ds(prev.e, 1), d], None,
                                            ALU.add).then_inc(s["oev"], 1)
                            if nxt and d == 1:
                                low_rows(nxt)
                            for tile in spread(tiles, d, 2):
                                place(*tile)
            dve.wait_ge(s["ld_par"], 96)
            dve.wait_ge(s["zero"], 2)
            one_hot(Job(0, 0))
            for t in range(9):
                place(Job(0, 0), t)
                if t == 5:
                    scaled(Job(0, 0))
                if t == 6:
                    low_rows(Job(0, 0))
            jobs(dve, emit)


def constants():
    import numpy as np
    c = np.zeros((P, NCONST), np.float32)

    def put(name, a):
        c[:a.shape[0], CONST[name][0]:CONST[name][1]] = a
    put("ident", np.eye(P))
    haar, scale = np.zeros((P, P)), np.zeros(P)
    level = np.zeros(P, int)
    at = 0
    for lv, low in ((3, True), (3, False), (2, False), (1, False)):
        n = 1 << lv
        for y in range(P >> lv):
            haar[at, y * n:(y + 1) * n] = 1
            if not low:
                haar[at, y * n + n // 2:(y + 1) * n] = -1
            scale[at] = 1.0 / n
            level[at] = 0 if low else {3: 1, 2: 2, 1: 3}[lv]
            at += 1
    put("fwd", haar.T)
    put("inv", haar * scale[:, None])
    q = np.arange(P)
    own, img = q // NB, q % NB
    same = own[:, None] == own[None, :]
    put("same", same)
    put("before", same & (img[:, None] < img[None, :]))
    put("causal", np.where(q[None, :] <= q[:, None], 0.0, MASKED))
    put("sign", np.stack([1.0 - 2.0 * ((q >> (lv - 1)) & 1) for lv in (1, 2, 3)], 1))
    put("slot", q[:, None] + P * np.arange(9)[None, :])
    put("batch", img[:, None])
    m = np.arange(CG * NJ)
    put("diag", (m // NJ)[:, None] == np.arange(CG)[None, :])
    lvl = np.array([3] + [3] * 3 + [2] * 3 + [1] * 3)
    put("pick", ((m % NJ)[:, None] == np.arange(NJ)[None, :]) * (0.5 ** lvl)[None, :])
    spread = np.zeros((NJ, LEAF, P))
    first = {1: 1, 2: 4, 3: 7}
    for g in range(LEAF):
        for p in range(P):
            r = level[p]
            if r == 0 and g == 0:
                j = 0
            elif r == g:
                j = first[r] + 2
            elif r > g:
                j = first[r]
            else:
                j = first[g] + 1
            spread[j, g, p] = (1 / 8, 1 / 8, 1 / 4, 1 / 2)[g]
    put("spread", spread.reshape(NJ, LEAF * P))
    put("owner", own[:, None] == np.arange(5)[None, :])
    put("rep1", q[:, None] % 64 == q[None, :] >> 1)
    put("rep2", q[:64, None] % 32 == q[None, :] >> 2)
    put("rep3", np.concatenate([q[:32, None] == 16 * h + (q[None, :] >> 3) for h in range(NH)], 1))
    return c


def kernel(x, cls_tok, L0_tok_Wa, L0_tok_ba, L0_tok_Wd1, L0_tok_bd1, L0_tok_Wd2, L0_tok_bd2, L0_tok_Wd3, L0_tok_bd3,
           L0_attn_R, L0_ffn_gate_w, L0_ffn_ln_gamma, L0_ffn_ln_beta, L0_ffn_fc1s, L0_ffn_b1s, L0_ffn_fc2s, L0_ffn_b2s):
    import numpy as np
    import concourse.bacc as bacc
    from concourse.bass_utils import run_bass_kernel_spmd

    def lay(a, *shape):
        return np.ascontiguousarray(a).reshape(shape)
    arrays = {
        "x": lay(np.asarray(x).reshape(NB, NH, P, D // CG, CG).transpose(2, 1, 3, 0, 4), P, NB * NH * D),
        "cls_tok": np.asarray(cls_tok),
        "Wa": np.asarray(L0_tok_Wa), "ba": np.asarray(L0_tok_ba),
        "Wd1": np.asarray(L0_tok_Wd1), "bd1": np.asarray(L0_tok_bd1),
        "Wd2": np.asarray(L0_tok_Wd2), "bd2": np.asarray(L0_tok_bd2),
        "Wd3": np.asarray(L0_tok_Wd3), "bd3": np.asarray(L0_tok_bd3),
        "R": np.asarray(L0_attn_R),
        "gate_w": np.asarray(L0_ffn_gate_w),
        "gate_wT": lay(np.asarray(L0_ffn_gate_w).T.reshape(2, P, NE).transpose(1, 0, 2), P, 2, NE),
        "gamma": lay(np.asarray(L0_ffn_ln_gamma).reshape(2, P).T, P, 2),
        "beta": lay(np.asarray(L0_ffn_ln_beta).reshape(2, P).T, P, 2),
        "fc1T": lay(np.asarray(L0_ffn_fc1s).transpose(0, 2, 1).reshape(NE, 2, P, NF).transpose(0, 2, 1, 3), NE, P, 2 * NF),
        "b1": lay(np.asarray(L0_ffn_b1s).reshape(NE, 8, P).transpose(2, 0, 1), P, NE, 8),
        "fc2T": lay(np.asarray(L0_ffn_fc2s).transpose(0, 2, 1).reshape(NE, 8, P, D).transpose(0, 2, 1, 3), NE, P, 8 * D),
        "b2": np.asarray(L0_ffn_b2s),
        "b2T": lay(np.asarray(L0_ffn_b2s).reshape(NE, 2, P).transpose(2, 0, 1), P, NE, 2),
        "const": constants(),
    }
    arrays = {k: np.ascontiguousarray(a) for k, a in arrays.items()}
    nc = bacc.Bacc("TRN2", target_bir_lowering=False, num_devices=1)
    args = [nc.dram_tensor(f"in_{k}", a.shape, mybir.dt.from_np(a.dtype), kind="ExternalInput").ap()
            for k, a in arrays.items()]
    out = nc.dram_tensor("out_0", (NB, NT, D), F32, kind="ExternalOutput").ap()
    build_program(nc, *args, out)
    r = run_bass_kernel_spmd(nc, [{f"in_{k}": a for k, a in arrays.items()}], core_ids=[0])
    return r.results[0]["out_0"]
```
